# Optimizing a Trainium2 kernel written in Bass

```python
import numpy as np
import jax
import jax.numpy as jnp

def _softmax(x, axis=-1):
    return jax.nn.softmax(x, axis=axis)

def _gelu(x):
    return jax.nn.gelu(x, approximate=True)

def _silu(x):
    return jax.nn.silu(x)

def _sigmoid(x):
    return jax.nn.sigmoid(x)

def _layernorm(x, axis=-1, eps=1e-05):
    m = jnp.mean(x, axis=axis, keepdims=True)
    v = jnp.var(x, axis=axis, keepdims=True)
    return (x - m) / jnp.sqrt(v + eps)

def _scatter_add(tgt, idx, src, axis=0):
    return tgt.at[idx].add(src)

def _segment_sum(src, seg, n):
    return jax.ops.segment_sum(src, seg, n)
kernel_name = 'mk_perceiver_d1_seqx_r8_a4fb94'

def setup_inputs(seed: int=0):
    np.random.seed(seed)
    _w = jnp.asarray

    def _rec_inputs():
        import jax
        import jax.numpy as jnp
        _rk = jax.random.key(seed)
        x = -0.0002928 + 1 * jax.random.normal(jax.random.fold_in(_rk, 1), (4, 128, 128), jnp.float32)
        _lenS = 128 - jax.random.randint(jax.random.fold_in(_rk, 7), (4,), 0, max(1, 128 // 4) + 1, jnp.int32)
        _lenS2 = 2048 - jax.random.randint(jax.random.fold_in(_rk, 8), (4,), 0, max(1, 2048 // 4) + 1, jnp.int32)
        _ctx_1024P = jax.random.normal(jax.random.fold_in(_rk, 11), (4, 16, 128), jnp.float32)
        _ctx_1024c = jax.random.dirichlet(jax.random.fold_in(_rk, 511), 0.3 * jnp.ones((16,), jnp.float32), (4, 2048))
        _ctx_1024t = jnp.einsum('bsk,bkd->bsd', _ctx_1024c, _ctx_1024P)
        _ctx_1024t = _ctx_1024t * jax.lax.rsqrt(jnp.mean(jnp.square(_ctx_1024t)) + 1e-12) * 0.953939
        ctx_1024 = -1.39393e-06 + 0.999914 * (_ctx_1024t + 0.3 * jax.random.normal(jax.random.fold_in(_rk, 611), (4, 2048, 128), jnp.float32))
        _validS = jnp.arange(128)[None, :] < _lenS[:, None]
        _validS2 = jnp.arange(2048)[None, :] < _lenS2[:, None]
        _causal = jnp.tril(jnp.ones((128, 128), dtype=bool))
        mask_1x1xSxS2_ff0 = jnp.where(jnp.ones((1, 1, 128, 2048), dtype=bool), 0.0, -1000000000.0).astype(jnp.float32)
        return (x, ctx_1024, mask_1x1xSxS2_ff0)
    x, ctx_1024, mask_1x1xSxS2_ff0 = _rec_inputs()

    def _L0_xattn_setup():
        import jax, jax.numpy as jnp
        import numpy as np
        D_MODEL = 128
        N_HEADS = 16
        HEAD_DIM = D_MODEL // N_HEADS
        key = jax.random.key(seed)
        ks = jax.random.split(key, 12)
        B, S = (2, 256)
        s = 1.0 / np.sqrt(D_MODEL)
        return {'Q': jax.random.normal(ks[0], (B, S, D_MODEL), jnp.float32), 'K': jax.random.normal(ks[1], (B, S, D_MODEL), jnp.float32), 'V': jax.random.normal(ks[2], (B, S, D_MODEL), jnp.float32), 'mask': jnp.zeros((1, 1, S, S), jnp.float32), 'Wq': jax.random.normal(ks[3], (D_MODEL, D_MODEL), jnp.float32) * s, 'bq': jnp.zeros((D_MODEL,), jnp.float32), 'Wk': jax.random.normal(ks[4], (D_MODEL, D_MODEL), jnp.float32) * s, 'bk': jnp.zeros((D_MODEL,), jnp.float32), 'Wv': jax.random.normal(ks[5], (D_MODEL, D_MODEL), jnp.float32) * s, 'bv': jnp.zeros((D_MODEL,), jnp.float32), 'Wo': jax.random.normal(ks[6], (D_MODEL, D_MODEL), jnp.float32) * s, 'bo': jnp.zeros((D_MODEL,), jnp.float32)}
    _L0_xattn_all = _L0_xattn_setup()
    _L0_xattn_in = {k: v for k, v in _L0_xattn_all.items() if k in ('Wq', 'bq', 'Wk', 'bk', 'Wv', 'bv', 'Wo', 'bo')}
    del _L0_xattn_all

    def _L0_attn_setup():
        import jax, jax.numpy as jnp
        import numpy as np
        import math
        EPS_A = 0.0001
        EPS = 1e-12

        def _l2_bounded(W, bound=1.0):
            sigma = jnp.linalg.svd(W, compute_uv=False)[0]
            return W / jnp.maximum(sigma / bound, 1.0)
        B, T, D = (4, 512, 128)
        N, D_out = (128, 128)
        key = jax.random.key(seed)
        ks = jax.random.split(key, 4)
        u = jax.random.normal(ks[0], (B, T, D), jnp.float32)
        W_in = 0.02 * jax.random.normal(ks[1], (N, D), jnp.float32)
        W_out = 0.02 * jax.random.normal(ks[2], (D_out, N), jnp.float32)
        Wp = 0.02 * jax.random.normal(ks[3], (3 * N, D), jnp.float32)
        bp = jnp.zeros((3 * N,), jnp.float32)
        rho, delta0 = (0.99, 1.0)
        alpha0 = -math.log(rho) / delta0
        alpha_log = jnp.full((N,), math.log(math.expm1(alpha0)), jnp.float32)
        delta_bias = jnp.full((N,), math.log(math.expm1(delta0)), jnp.float32)
        log_gamma = jnp.array(0.0, jnp.float32)
        return dict(u=u, W_in=W_in, W_out=W_out, Wp=Wp, bp=bp, alpha_log=alpha_log, delta_bias=delta_bias, log_gamma=log_gamma)
    _L0_attn_all = _L0_attn_setup()
    _L0_attn_in = {k: v for k, v in _L0_attn_all.items() if k in ('W_in', 'W_out', 'Wp', 'bp', 'alpha_log', 'delta_bias', 'log_gamma')}
    del _L0_attn_all

    def _L0_ffn_setup():
        import jax, jax.numpy as jnp
        import numpy as np

        def _binarize(w):
            alpha = jax.lax.stop_gradient(jnp.mean(jnp.abs(w), axis=1, keepdims=True))
            bw = alpha * jnp.sign(w)
            return w + jax.lax.stop_gradient(bw - w)
        key = jax.random.key(seed)
        k1, k2, k3, k4, k5 = jax.random.split(key, 5)
        D, H = (128, 512)
        x = jax.random.normal(k1, (64, 196, D), dtype=jnp.float32)
        w1 = jax.random.normal(k2, (H, D), dtype=jnp.float32) * 0.02
        b1 = jax.random.normal(k3, (H,), dtype=jnp.float32) * 0.02
        w2 = jax.random.normal(k4, (D, H), dtype=jnp.float32) * 0.02
        b2 = jax.random.normal(k5, (D,), dtype=jnp.float32) * 0.02
        return {'x': x, 'w1': w1, 'b1': b1, 'w2': w2, 'b2': b2}
    _L0_ffn_all = _L0_ffn_setup()
    _L0_ffn_in = {k: v for k, v in _L0_ffn_all.items() if k in ('w1', 'b1', 'w2', 'b2')}
    del _L0_ffn_all
    return {'x': x, 'ctx_1024': ctx_1024, 'mask_1x1xSxS2_ff0': mask_1x1xSxS2_ff0, 'L0_xattn_Wq': _L0_xattn_in['Wq'], 'L0_xattn_bq': _L0_xattn_in['bq'], 'L0_xattn_Wk': _L0_xattn_in['Wk'], 'L0_xattn_bk': _L0_xattn_in['bk'], 'L0_xattn_Wv': _L0_xattn_in['Wv'], 'L0_xattn_bv': _L0_xattn_in['bv'], 'L0_xattn_Wo': _L0_xattn_in['Wo'], 'L0_xattn_bo': _L0_xattn_in['bo'], 'L0_attn_W_in': _L0_attn_in['W_in'], 'L0_attn_W_out': _L0_attn_in['W_out'], 'L0_attn_Wp': _L0_attn_in['Wp'], 'L0_attn_bp': _L0_attn_in['bp'], 'L0_attn_alpha_log': _L0_attn_in['alpha_log'], 'L0_attn_delta_bias': _L0_attn_in['delta_bias'], 'L0_attn_log_gamma': _L0_attn_in['log_gamma'], 'L0_ffn_w1': _L0_ffn_in['w1'], 'L0_ffn_b1': _L0_ffn_in['b1'], 'L0_ffn_w2': _L0_ffn_in['w2'], 'L0_ffn_b2': _L0_ffn_in['b2']}

def reference(x, ctx_1024, mask_1x1xSxS2_ff0, L0_xattn_Wq, L0_xattn_bq, L0_xattn_Wk, L0_xattn_bk, L0_xattn_Wv, L0_xattn_bv, L0_xattn_Wo, L0_xattn_bo, L0_attn_W_in, L0_attn_W_out, L0_attn_Wp, L0_attn_bp, L0_attn_alpha_log, L0_attn_delta_bias, L0_attn_log_gamma, L0_ffn_w1, L0_ffn_b1, L0_ffn_w2, L0_ffn_b2):
    import jax
    import jax.numpy as jnp

    def _L0_xattn_ref(Q, K, V, mask, Wq, bq, Wk, bk, Wv, bv, Wo, bo):
        import jax, jax.numpy as jnp
        import numpy as np
        D_MODEL = 128
        N_HEADS = 16
        HEAD_DIM = D_MODEL // N_HEADS
        B, Sq, _ = Q.shape
        Sk = K.shape[1]
        q = (Q @ Wq.T + bq).reshape(B, Sq, N_HEADS, HEAD_DIM).transpose(0, 2, 1, 3)
        k = (K @ Wk.T + bk).reshape(B, Sk, N_HEADS, HEAD_DIM).transpose(0, 2, 1, 3)
        v = (V @ Wv.T + bv).reshape(B, Sk, N_HEADS, HEAD_DIM).transpose(0, 2, 1, 3)
        scores = jnp.einsum('bhqd,bhkd->bhqk', q, k) / jnp.sqrt(jnp.asarray(HEAD_DIM, q.dtype))
        scores = scores + mask
        attn = jax.nn.softmax(scores, axis=-1)
        out = jnp.einsum('bhqk,bhkd->bhqd', attn, v)
        out = out.transpose(0, 2, 1, 3).reshape(B, Sq, D_MODEL)
        return out @ Wo.T + bo

    def _L0_attn_ref(u, W_in, W_out, Wp, bp, alpha_log, delta_bias, log_gamma):
        import jax, jax.numpy as jnp
        import numpy as np
        import math
        EPS_A = 0.0001
        EPS = 1e-12

        def _l2_bounded(W, bound=1.0):
            sigma = jnp.linalg.svd(W, compute_uv=False)[0]
            return W / jnp.maximum(sigma / bound, 1.0)
        Win_n = _l2_bounded(W_in)
        Wout_n = _l2_bounded(W_out)
        u_scaled = jnp.exp(log_gamma) * jnp.einsum('btd,nd->btn', u, Win_n)
        raw = jnp.einsum('btd,kd->btk', u, Wp) + bp
        delta_raw, b_raw, c_raw = jnp.split(raw, 3, axis=-1)
        delta = jax.nn.softplus(delta_raw + delta_bias)
        alpha = jax.nn.softplus(alpha_log)
        a = jnp.minimum(jnp.exp(-delta * alpha), 1.0 - EPS_A)
        b = jnp.tanh(b_raw)
        c = jnp.tanh(c_raw)
        p = a * a + c * c
        r = b * b
        q = a * b
        disc = (p - r) * (p - r) + 4.0 * q * q
        lam_max = 0.5 * (p + r + jnp.sqrt(disc + EPS))
        sigma = jnp.sqrt(lam_max + EPS)
        scale = jnp.maximum(sigma, 1.0)
        a = a / scale
        b = b / scale
        c = c / scale
        bu = b * u_scaled

        def combine(left, right):
            a1, b1 = left
            a2, b2 = right
            return (a2 * a1, a2 * b1 + b2)
        a_p, b_p = jax.lax.associative_scan(combine, (a, bu), axis=1)
        z_bt = jnp.concatenate([jnp.zeros_like(b_p[:, :1]), b_p[:, :-1]], axis=1)
        y_hat = c * z_bt
        y = jnp.einsum('btn,on->bto', y_hat, Wout_n)
        return y

    def _L0_ffn_ref(x, w1, b1, w2, b2):
        import jax, jax.numpy as jnp
        import numpy as np

        def _binarize(w):
            alpha = jax.lax.stop_gradient(jnp.mean(jnp.abs(w), axis=1, keepdims=True))
            bw = alpha * jnp.sign(w)
            return w + jax.lax.stop_gradient(bw - w)
        bw1 = _binarize(w1)
        h = jnp.einsum('bsd,hd->bsh', x, bw1) + b1
        h = jax.nn.gelu(h, approximate=False)
        bw2 = _binarize(w2)
        out = jnp.einsum('bsh,dh->bsd', h, bw2) + b2
        return out
    x = x + _L0_xattn_ref(_layernorm(x, axis=-1), ctx_1024, ctx_1024, mask_1x1xSxS2_ff0, L0_xattn_Wq, L0_xattn_bq, L0_xattn_Wk, L0_xattn_bk, L0_xattn_Wv, L0_xattn_bv, L0_xattn_Wo, L0_xattn_bo)
    x = x + _L0_attn_ref(_layernorm(x, axis=-1), L0_attn_W_in, L0_attn_W_out, L0_attn_Wp, L0_attn_bp, L0_attn_alpha_log, L0_attn_delta_bias, L0_attn_log_gamma)
    x = x + _L0_ffn_ref(_layernorm(x, axis=-1), L0_ffn_w1, L0_ffn_b1, L0_ffn_w2, L0_ffn_b2)
    return x

_drawn_inputs = setup_inputs


def setup_inputs(seed=0):
    import zlib

    import numpy as np

    out = dict(_drawn_inputs(seed))
    spreads = {'L0_xattn_bq': (0.0, 0.376),
     'L0_xattn_bk': (0.0, 0.8),
     'L0_xattn_bv': (0.0, 0.1),
     'L0_xattn_bo': (0.0, 0.1),
     'L0_attn_bp': (0.0, 0.8),
     'L0_attn_alpha_log': (-4.595119953155518, 0.6),
     'L0_attn_delta_bias': (0.5413248538970947, 0.6)}
    factors = {'L0_attn_W_in': 5.559,
     'L0_attn_W_out': 5.318,
     'L0_attn_Wp': 5.494,
     'L0_ffn_b1': 8.0,
     'L0_ffn_b2': 3.169}
    for name, (base, spread) in spreads.items():
        noise = np.random.default_rng([zlib.crc32(name.encode()), seed]).standard_normal(out[name].shape)
        drawn = base * np.exp(spread * noise) if base else spread * noise
        out[name] = jnp.asarray(drawn.astype(out[name].dtype))
    for name, factor in factors.items():
        out[name] = (out[name] * factor).astype(out[name].dtype)
    return out
```

```python
import concourse.bass as bass
from concourse import mybir
from contextlib import ExitStack
import math

F32 = mybir.dt.float32
BF16 = mybir.dt.bfloat16
I32 = mybir.dt.int32
ALU = mybir.AluOpType
ACT = mybir.ActivationFunctionType
AX = mybir.AxisListType

P = 128
HEAD_COLS = 9
SQUARINGS = 24
SQ_PERIOD = 3
TINY = 1e-30
LN_EPS = 1e-5
EPS = 1e-12
EPS_A = 1e-4


def perceiver_block(nc, x, ctx_in, mask, Wq, bq, Wk, bk, Wv, bv, Wo, bo, W_in, W_out, Wp, bp,
                    alpha_log, delta_bias, log_gamma, w1, b1, w2, b2, ident_in, gather_in, head_rows_in, out):
    B, T, D = x.shape
    KEYS = ctx_in.shape[1]
    HEADS = 16
    HD = D // HEADS
    PAIRS = HEADS // 2
    CHUNKS = KEYS // 512
    KT = KEYS // P
    HID = w1.shape[0]
    HB = HID // P
    TOK = B * T
    UNITS = PAIRS * CHUNKS
    LEAD = 8
    assert (T, D, CHUNKS, B, HD) == (128, 128, 4, 4, 8)
    K_BLOCKS = (0, 1, 2, 0, 1, 0)
    Q_BLOCKS = (0, 0, 0, 1, 1, 2)
    MAX_ROW = 16 * len(Q_BLOCKS)

    ctx = ExitStack()
    with ctx:
        def sb(name, shape, dt=F32):
            return ctx.enter_context(nc.sbuf_tensor(name, shape, dt))

        sems = {}

        def sem(name):
            sems[name] = ctx.enter_context(nc.semaphore(name))
            return sems[name]

        ident = sb("ident", [P, P])
        ident_bf = sb("ident_bf", [P, P], BF16)
        head_rows = sb("head_rows", [P, 2])
        gather = sb("gather", [P, 2 * HEAD_COLS])
        ones = sb("ones", [P, P])
        x_sb = sb("x_sb", [P, B, D])
        w_nat = sb("w_nat", [P, 4, D])
        ssm_nat = sb("ssm_nat", [P, 5, D])
        w1_nat = sb("w1_nat", [P, HB, D])
        w2_nat = sb("w2_nat", [P, HID])
        wT = sb("wT", [P, 4, D])
        ssmT = sb("ssmT", [P, 5, D])
        w1T = sb("w1T", [P, HB, P])
        w2T = sb("w2T", [P, HB, D])
        vec = sb("vec", [P, 16])
        BQ, BK, ALPHA, DBIAS, LGAM, BP0, B1_0 = 0, 1, 2, 3, 4, 5, 8
        bv_rows = sb("bv_rows", [P, 4, D])
        bo_rows = sb("bo_rows", [P, D])
        b2_rows = sb("b2_rows", [P, D])
        x_bo = sb("x_bo", [P, B, D])
        bn = sb("bn", [P, B, 6])
        mv = sb("mv", [P, B, 2])
        var_eps = sb("var_eps", [P, B])
        rstd = sb("rstd", [P, B])
        neg_half = sb("neg_half", [P, B])
        xn = sb("xn", [P, B, D])
        xnT = sb("xnT", [P, TOK])
        q32 = sb("q32", [P, TOK])
        q_r1 = sb("q_r1", [P, TOK])
        q_parts = sb("q_parts", [P, 3, TOK], BF16)
        q_rows = sb("q_rows", [P, PAIRS, B, 2, T], BF16)
        ctx_buf = sb("ctx_buf", [P, CHUNKS, 4, D])
        ctxT = sb("ctxT", [P, 2, 512])
        k_parts = sb("k_parts", [P, 3, B * KEYS], BF16)
        k_r1 = sb("k_r1", [P, 2, 512])
        v_all = sb("v_all", [P, B * KT, HEADS * HEAD_COLS])
        k_rows = sb("k_rows", [P, 4, KEYS], BF16)
        q_max = sb("q_max", [P, 2, 2, T], BF16)
        v_now = sb("v_now", [P, 2, KT, 2 * HEAD_COLS])
        pmax = sb("pmax", [P, 2, 2, CHUNKS])
        negmax = sb("negmax", [P, 2, 2])
        nm_r1 = sb("nm_r1", [P, 2, 2])
        max_cols = sb("max_cols", [P, 2, 2, P], BF16)
        probs = sb("probs", [P, 4, 2, 512])
        oT_sb = sb("oT_sb", [P, 2, P])
        rden = sb("rden", [P, 2, 2])
        o_nat = w1_nat
        mask_parts = sb("mask_parts", [P, 3, KEYS], BF16)
        mask_abs = sb("mask_abs", [P, 1])
        mask_flag_f = sb("mask_flag_f", [1, 1])
        mask_flag = sb("mask_flag", [1, 1], I32)
        gram = sb("gram", [P, 2, P])
        power = sb("power", [P, 2, 2, P])
        sq_junk = sb("sq_junk", [P, 2, P])
        fro = sb("fro", [P, 2])
        fro_inv = sb("fro_inv", [P, 2])
        ray = sb("ray", [P, 4])
        norm_inv = sb("norm_inv", [P, 2])
        ray_all = sb("ray_all", [P, 4])
        sv = sb("sv", [P, 12])
        w_abs = sb("w_abs", [P, HB + 1])

        ps = ctx.enter_context(nc.psum_tensor("ps", [P, 8, 512], F32))

        mask_r = probs[:, 0:2, :, :].rearrange("p a b n -> p (a b n)")
        q_both = probs[:, 0:2, :, :].rearrange("p a b n -> p (a b n)").bitcast(BF16).rearrange(
            "p (i n) -> p i n", n=TOK)
        w_sgn = probs[:, 2, :, :].rearrange("p b (i n) -> p (b i) n", n=P)
        mask_sb = v_all[:, :, :].rearrange("p t n -> p (t n)")[:, B * KT * HEADS * HEAD_COLS - KEYS:]
        w_bin = probs[:, 3, :, :].rearrange("p b (i n) -> p (b i) n", n=P)
        gates = k_parts[:, :, :].rearrange("p a n -> p (a n)")[:, 0:15 * 2 * TOK].bitcast(F32).rearrange(
            "p (i n) -> p i n", n=TOK)
        (SP_ABS, SP_EXP, SP_LN, G_B, G_C, G_R, G_CC, G_A0, DELTA, U_S, G_A, G_Q, G_P, G_D, G_CS
         ) = (gates[:, i, :] for i in range(15))
        STATE = q32[:, :]

        ld = {n: sem("ld_" + n) for n in ("ident", "x", "wk", "w", "bias", "bias_qk", "ssm", "mlp", "mask", "rows")}
        ctx_loaded = [sem(f"ctx_loaded{c}") for c in range(CHUNKS)]
        ctx_turned = sem("ctx_turned")
        ctxT_ready = sem("ctxT_ready")
        kv_done = sem("kv_done")
        k1_ready = sem("k1_ready")
        r1_ready = sem("r1_ready")
        k2_ready = sem("k2_ready")
        k3_ready = sem("k3_ready")
        v_ready = sem("v_ready")
        sq_done = sem("sq_done")
        pow_ready = sem("pow_ready")
        fro_ready = sem("fro_ready")
        fro_summed = sem("fro_summed")
        fro_inv_ready = sem("fro_inv_ready")
        k_rows_loaded = [sem(f"k_rows_loaded{s}") for s in range(4)]
        v_now_ready = sem("v_now_ready")
        scores_ready = sem("scores_ready")
        pmax_ready = sem("pmax_ready")
        negmax_ready = sem("negmax_ready")
        split_step = sem("split_step")
        max_turned = sem("max_turned")
        q_max_ready = sem("q_max_ready")
        keyscores_ready = sem("keyscores_ready")
        probs_ready = sem("probs_ready")
        pv_done = sem("pv_done")
        oT_ready = sem("oT_ready")
        o_turned = sem("o_turned")
        rden_ready = sem("rden_ready")
        o_ready = sem("o_ready")
        stored = sem("stored")

        def once(name):
            return sems[name] if name in sems else sem(name)

        def wait(eng, s, value):
            if isinstance(value, int) and value <= 0:
                return
            eng.wait_ge(s, value)

        def hold(eng, s, value):
            wait(eng, s, value)
            if not isinstance(value, int):
                eng.sem_inc(once("passed_a_hold"))

        def loop_batches(eng, body):
            body(0)
            with eng.Fori(1, B - 1) as b:
                body(b)
            body(B - 1)

        block = ctx.enter_context(nc.Block())

        @block.sync
        def _(sp):
            def row(v, n):
                return v.rearrange("(a n) -> a n", a=1).broadcast_to((P, n))

            def load_ctx(b, c):
                if not isinstance(b, int) or b > 0:
                    wait(sp, ctx_turned, 4 * (b - 1) + c + 1)
                sp.dma_start(ctx_buf[:, c, :, :],
                             ctx_in[bass.ds(b, 1), 512 * c:512 * c + 512, :].rearrange(
                                 "b (p j) d -> p (b j) d", j=4)).then_inc(ctx_loaded[c], 16)

            sp.dma_start(w_nat[:, 1, :], Wk).then_inc(ld["wk"], 16)
            load_ctx(0, 0)
            sp.dma_start(w_nat[:, 2, :], Wv).then_inc(ld["wk"], 16)
            sp.dma_start(x_sb[:, :, :], x.rearrange("b t d -> t b d")).then_inc(ld["x"], 16)
            for c in range(1, CHUNKS):
                load_ctx(0, c)
            stack = [(p, block) for p in range(PAIRS) for block in range(len(Q_BLOCKS))]
            per_chunk = len(stack) // (CHUNKS * (B - 1))
            sp.wait_ge(once("q3_ready"), 1)
            sp.wait_ge(once("w_bin_ready"), 2)
            for b in range(1, B):
                for c in range(CHUNKS):
                    load_ctx(b, c)
                    for _ in range(per_chunk):
                        p, block = stack.pop(0)
                        sp.dma_start(q_both[16 * block:16 * block + 16, p, :],
                                     q_parts[16 * p:16 * p + 16, Q_BLOCKS[block], :]
                                     ).then_inc(once("q_loaded"), 16)

            def load_pair(b, p):
                slot = p % 4
                wait(sp, keyscores_ready, 2 * CHUNKS * (PAIRS * b + p - 3))
                for block, part in enumerate(K_BLOCKS):
                    sp.dma_start(k_rows[16 * block:16 * block + 16, slot, :],
                                 k_parts[16 * p:16 * p + 16, part, bass.ds(b * KEYS, KEYS)]
                                 ).then_inc(k_rows_loaded[slot], 16)

            sp.wait_ge(once("pads_ready"), 1)
            def pairs(b):
                sp.wait_ge(k3_ready, CHUNKS * b + CHUNKS)
                for p in range(PAIRS):
                    load_pair(b, p)
            pairs(0)
            with sp.Fori(1, B) as b:
                pairs(b)

            sp.wait_ge(once("out_ready"), 1)
            sp.dma_start(out.rearrange("b t d -> t b d"), xn[:, :, :]).then_inc(stored, 16)
            sp.wait_ge(stored, 16)

        @block.tensor
        def _(pe):
            pe.wait_ge(ld["ident"], 48)

            def turn(dst, src):
                return pe.transpose(dst, src, ident[:, :])

            pe.wait_ge(ld["wk"], 32)
            pe.wait_ge(ld["w"], 32)
            for i in range(4):
                t = turn(ps[:, 2, P * i:P * i + P], w_nat[:, i, :])
            t.then_inc(once("w_turned"), 1)
            pe.wait_ge(ld["ssm"], 48)
            for w in range(2):
                t = pe.matmul(ps[:, 6, P * w:P * w + P], ssm_nat[:, w, :], ssm_nat[:, w, :], start=True, stop=True)
            t.then_inc(sq_done, 1)
            for i in range(4):
                t = turn(ps[:, 3, P * i:P * i + P], ssm_nat[:, i, :])
            t.then_inc(once("ssm_turned"), 1)
            pe.wait_ge(once("xn_ready"), B)
            for i in range(B):
                t = turn(ps[:, 4, P * i:P * i + P], xn[:, i, :])
            t.then_inc(once("xn_turned"), 1)
            pe.wait_ge(once("ssmT_ready"), 1)
            pe.wait_ge(once("xnT_ready"), 1)
            pe.wait_ge(once("wT_ready"), 1)
            turn(ps[:, 3, 0:P], ssm_nat[:, 4, :])
            pe.matmul(ps[:, 5, :], wT[:, 0, :], xnT[:, :], start=True, stop=True).then_inc(once("q_done"), 1)
            pe.wait_ge(once("w_bin_ready"), 2)
            for i in range(HB):
                t = turn(ps[:, 0, P * i:P * i + P], w_bin[:, i, :])
            for i in range(HB):
                t = turn(ps[:, 1, P * i:P * i + P], w_bin[:, HB + i, :])
            t.then_inc(once("w_bin_turned"), 1)
            pe.wait_ge(once("mask_abs_ready"), 1)
            turn(ps[0:1, 2, 0:P], mask_abs[:, :]).then_inc(once("mask_turned"), 1)

            def turn_ctx(b, c):
                n = 4 * b + c
                wait(pe, ctxT_ready, n - 1)
                pe.wait_ge(ctx_loaded[c], 16 * b + 16)
                for j in range(4):
                    t = turn(ps[:, c % 2, P * j:P * j + P], ctx_buf[:, c, j, :])
                t.then_inc(ctx_turned, 1)

            def project(b, c):
                n = 4 * b + c
                k_bank, v_bank = ps[:, 2 + c % 2, :], 4 + c % 2
                pe.wait_ge(ctxT_ready, n + 1)
                wait(pe, k1_ready, n - 1)
                wait(pe, r1_ready, n - 1)
                wait(pe, v_ready, n - 1)
                pe.matmul(k_bank, wT[:, 1, :], ctxT[:, c % 2, :], start=True, stop=True)
                for j in range(4):
                    t = pe.matmul(ps[:, v_bank, P * j:P * j + P], ctxT[:, c % 2, P * j:P * j + P], wT[:, 2, :],
                                  start=True, stop=True)
                t.then_inc(kv_done, 1)

            def square(k, at, norms):
                if at % SQ_PERIOD == 0:
                    pe.wait_ge(fro_ready, 2 * norms + 2)
                    pe.matmul(ps[:, 7, 0:2], ones[:, :], fro[:, :], start=True, stop=True).then_inc(fro_summed, 1)
                pe.wait_ge(pow_ready, k + 1)
                for w in range(2):
                    t = pe.matmul(ps[:, 6, P * w:P * w + P], power[:, at % 2, w, :], power[:, at % 2, w, :],
                                  start=True, stop=True)
                t.then_inc(sq_done, 1)

            pe.wait_ge(once("pe_setup_copied"), 6)
            def prep(b):
                at = 0
                for c in range(CHUNKS):
                    turn_ctx(b, c)
                    square(6 * b + at, at, 2 * b + at // SQ_PERIOD)
                    at += 1
                    if c > 0:
                        project(b, c - 1)
                    elif not isinstance(b, int) or b > 0:
                        project(b - 1, CHUNKS - 1)
                    if c % 2 == 1:
                        square(6 * b + at, at, 2 * b + at // SQ_PERIOD)
                        at += 1
            loop_batches(pe, prep)
            project(B - 1, CHUNKS - 1)
            pe.wait_ge(pow_ready, SQUARINGS + 1)
            for w in range(2):
                t = pe.matmul(ps[:, 6, P * w:P * w + P], gram[:, w, :], power[:, 0, w, :], start=True, stop=True)
            t.then_inc(once("ray_done"), 1)
            pe.wait_ge(once("ray_ready"), 4)
            pe.matmul(ps[:, 7, 0:4], ones[:, :], ray[:, :], start=True, stop=True).then_inc(once("ray_summed"), 1)

            def mask_query(bank, c, m):
                for s in range(3):
                    pe.matmul(ps[:, bank, :], ident_bf[:, :],
                              mask_parts[:, s, 512 * c:512 * c + 512].rearrange("q (p j) -> q j p", j=4),
                              start=(s == 0), stop=False)

            def mask_key(dst, c, j, first):
                keys = mask_parts[:, :, 512 * c:512 * c + 512].rearrange("q s (p j) -> q s j p", j=4)
                for s in range(3):
                    pe.matmul(dst, keys[:, s, j, :], ident_bf[:, :], start=first and s == 0, stop=False,
                              skip_group_check=True)

            def scores(b, u, masked):
                p, c = divmod(u, CHUNKS)
                slot = p % 4
                if c == 0:
                    pe.wait_ge(k_rows_loaded[slot], 16 * len(K_BLOCKS) * (2 * b + p // 4 + 1))
                wait(pe, pmax_ready, UNITS * b + u - 1)
                bank = 2 * (u % 2)
                if masked:
                    for h in range(2):
                        mask_query(bank + h, c, h)
                for h in range(2):
                    t = pe.matmul(ps[:, bank + h, :], q_rows[:, p, bass.ds(b, 1), h, :].rearrange("r b q -> r (b q)"),
                                  k_rows[:, slot, 512 * c:512 * c + 512], start=not masked, stop=True)
                t.then_inc(scores_ready, 1)

            def turn_max(b, p):
                pe.wait_ge(split_step, 4 * (PAIRS * b + p) + 4)
                wait(pe, o_ready, PAIRS * b + p - 1)
                for h in range(2):
                    t = pe.matmul(ps[:, 6 + p % 2, 128 + P * h:128 + P * h + P], max_cols[:, p % 2, h, :],
                                  ident_bf[:, :], start=True, stop=True)
                t.then_inc(max_turned, 1)

            def keyscores(b, u, masked):
                p, c = divmod(u, CHUNKS)
                if c == 0:
                    pe.wait_ge(q_max_ready, PAIRS * b + p + 1)
                for half in range(2):
                    wait(pe, probs_ready, 2 * (UNITS * b + u) - 1 + half)
                    for j in (2 * half, 2 * half + 1):
                        dst = ps[:, 4 + half, 2 * P * (j % 2):2 * P * (j % 2) + 2 * P]
                        if masked:
                            for h in range(2):
                                mask_key(dst[:, P * h:P * h + P], c, j, j % 2 == 0 and h == 0)
                        at = 512 * c + P * j
                        t = pe.matmul(dst, k_rows[:, p % 4, at:at + P],
                                      q_max[:, p % 2, :, :].rearrange("r h q -> r (h q)"),
                                      start=not masked, stop=True, skip_group_check=masked)
                    t.then_inc(keyscores_ready, 1)

            def pv(b, u):
                p, c = divmod(u, CHUNKS)
                if c == 0:
                    pe.wait_ge(v_now_ready, PAIRS * b + p + 1)
                    wait(pe, o_ready, PAIRS * b + p - 1)
                    pe.wait_ge(q_max_ready, PAIRS * b + p + 1)
                pe.wait_ge(probs_ready, 2 * (UNITS * b + u) + 2)
                for j in range(4):
                    for h in range(2):
                        at = 32 * (2 * (j % 2) + h)
                        t = pe.matmul(ps[at:at + HEAD_COLS, 6 + p % 2, 0:P],
                                      v_now[:, p % 2, 4 * c + j, HEAD_COLS * h:HEAD_COLS * h + HEAD_COLS],
                                      probs[:, c, j // 2, P * (2 * (j % 2) + h):P * (2 * (j % 2) + h) + P],
                                      start=(c == 0 and j < 2), stop=(c == CHUNKS - 1 and j >= 2))
                t.then_inc(pv_done, 1)

            def turn_out(b, p):
                pe.wait_ge(oT_ready, PAIRS * b + p + 1)
                pe.matmul(ps[:, 6 + p % 2, 384:384 + 2 * HEAD_COLS], oT_sb[:, p % 2, :], gather[:, :],
                          start=True, stop=True).then_inc(o_turned, 1)

            def attend(masked):
                for u in range(6):
                    scores(0, u, masked)
                turn_max(0, 0)
                for u in range(6, LEAD):
                    scores(0, u, masked)
                keyscores(0, 0, masked)

                def batch(b):
                    last = isinstance(b, int) and b == B - 1
                    first = isinstance(b, int) and b == 0
                    for u in range(UNITS):
                        p, c = divmod(u, CHUNKS)
                        if u + 1 < UNITS:
                            keyscores(b, u + 1, masked)
                        elif not last:
                            keyscores(b + 1, 0, masked)
                        if u + LEAD < UNITS:
                            scores(b, u + LEAD, masked)
                        elif not last:
                            scores(b + 1, u + LEAD - UNITS, masked)
                        if c == 0 and p > 0:
                            turn_out(b, p - 1)
                        elif c == 0 and not first:
                            turn_out(b - 1, PAIRS - 1)
                        pv(b, u)
                        if c == 1 and p + 1 < PAIRS:
                            turn_max(b, p + 1)
                        elif c == 1 and not last:
                            turn_max(b + 1, 0)
                loop_batches(pe, batch)
                turn_out(B - 1, PAIRS - 1)

            pe.wait_ge(once("q_rows_ready"), 2)
            pe.wait_ge(v_ready, B * CHUNKS)
            pe.wait_ge(k2_ready, B * CHUNKS)
            pe.wait_ge(r1_ready, B * CHUNKS)
            pe.wait_ge(once("ray_all_ready"), 1)
            pe.wait_ge(once("out_banks_zeroed"), 2)
            pe.wait_ge(once("mask_flag_ready"), 1)
            any_mask = pe.value_load(mask_flag[0:1, 0:1], min_val=0, max_val=1)
            with pe.If(any_mask > 0):
                attend(True)
            with pe.Else():
                attend(False)
            pe.wait_ge(o_ready, B * PAIRS)

            for b in range(B):
                t = turn(ps[:, 0, P * b:P * b + P], o_nat[:, b, :])
            t.then_inc(once("oN_turned"), 1)
            pe.wait_ge(once("oNT_ready"), 1)
            for b in range(B):
                t = pe.matmul(ps[:, 1, P * b:P * b + P], xnT[:, P * b:P * b + P], wT[:, 3, :], start=True, stop=True)
            t.then_inc(once("attn_done"), 1)

            pe.wait_ge(once("ln2_ready"), B)
            for b in range(B):
                t = turn(ps[:, 2, P * b:P * b + P], xn[:, b, :])
            t.then_inc(once("ln2_turned"), 1)
            pe.wait_ge(once("ln2T_ready"), 1)
            for i, bank in ((2, 3), (3, 4), (4, 5), (0, 6)):
                pe.matmul(ps[:, bank, :], ssmT[:, i, :], xnT[:, :], start=True, stop=True
                          ).then_inc(once("ssm_done"), 1)
            pe.wait_ge(once("yhat_ready"), 1)
            for b in range(B):
                t = pe.matmul(ps[:, 7, P * b:P * b + P], q_r1[:, P * b:P * b + P], ssmT[:, 1, :],
                              start=True, stop=True)
            t.then_inc(once("y_done"), 1)

            pe.wait_ge(once("ln3_ready"), B)
            for b in range(B):
                t = turn(ps[:, 0, P * b:P * b + P], xn[:, b, :])
            t.then_inc(once("ln3_turned"), 1)
            pe.wait_ge(once("ln3T_ready"), 1)
            for i in range(HB):
                pe.matmul(ps[:, 1 + i, :], w1T[:, i, :], xnT[:, :], start=True, stop=True
                          ).then_inc(once("h_done"), 1)
            for i in range(HB):
                pe.wait_ge(once("gelu_ready"), i + 1)
                for b in range(B):
                    t = pe.matmul(ps[:, 5, P * b:P * b + P], probs[:, i, 0, P * b:P * b + P], w2T[:, i, :],
                                  start=(i == 0 and b == 0), stop=(i == HB - 1), skip_group_check=True)
            t.then_inc(once("mlp_done"), 1)

        @block.scalar
        def _(act):
            act.dma_start(ident[:, :], ident_in).then_inc(ld["ident"], 16)
            act.dma_start(gather[:, :], gather_in).then_inc(ld["ident"], 16)
            act.dma_start(head_rows[:, :], head_rows_in).then_inc(ld["ident"], 16)
            act.dma_start(w_nat[:, 0, :], Wq).then_inc(ld["w"], 16)
            act.dma_start(w_nat[:, 3, :], Wo).then_inc(ld["w"], 16)
            col = lambda v: v.rearrange("(p a) -> p a", a=1)
            act.dma_start(vec[:, BK:BK + 1], col(bk)).then_inc(ld["bias_qk"], 16)
            act.dma_start(vec[:, BQ:BQ + 1], col(bq)).then_inc(ld["bias_qk"], 16)
            act.dma_start(ssm_nat[:, 0, :], W_in).then_inc(ld["ssm"], 16)
            act.dma_start(ssm_nat[:, 1, :], W_out).then_inc(ld["ssm"], 16)
            act.dma_start(ssm_nat[:, 2:5, :], Wp.rearrange("(a p) d -> p a d", p=P)).then_inc(ld["ssm"], 16)

            def copy(dst, src, s, n=1):
                act.activation(dst, src, ACT.Copy).then_inc(s, n)

            act.wait_ge(once("w_turned"), 1)
            copy(wT[:, :, :].rearrange("p a d -> p (a d)"), ps[:, 2, :], once("wT_ready"))
            act.wait_ge(once("ssm_turned"), 1)
            copy(ssmT[:, 0:4, :].rearrange("p a d -> p (a d)"), ps[:, 3, :], once("ssmT_ready"))
            act.wait_ge(once("xn_turned"), 1)
            copy(xnT[:, :], ps[:, 4, :], once("xnT_ready"))
            act.wait_ge(once("q_done"), 1)
            copy(ssmT[:, 4, :], ps[:, 3, 0:P], once("pe_setup_copied"))
            act.wait_ge(ld["bias"], 16 * 10)
            act.wait_ge(ld["bias_qk"], 32)
            act.activation(sv[:, 0:1], vec[:, ALPHA:ALPHA + 1], ACT.Abs).then_inc(once("alpha_step"), 1)
            act.wait_ge(once("alpha_step"), 1)
            act.activation(sv[:, 1:2], sv[:, 0:1], ACT.Exp, scale=-1.0).then_inc(once("alpha_step"), 1)
            act.wait_ge(once("alpha_step"), 2)
            act.activation(sv[:, 2:3], sv[:, 1:2], ACT.Ln, bias=1.0).then_inc(once("alpha_step"), 1)
            act.activation(sv[:, 3:4], vec[:, LGAM:LGAM + 1], ACT.Exp).then_inc(once("alpha_step"), 1)
            act.wait_ge(once("w_bin_turned"), 1)
            copy(w1T[:, :, :].rearrange("p a d -> p (a d)"), ps[:, 0, :], once("pe_setup_copied"))
            copy(w2T[:, :, :].rearrange("p a d -> p (a d)"), ps[:, 1, :], once("pe_setup_copied"))

            def copy_ctx(b, c):
                n = 4 * b + c
                hold(act, ctx_turned, n + 1)
                hold(act, kv_done, n - 1)
                copy(ctxT[:, c % 2, :], ps[:, c % 2, :], ctxT_ready)

            def split_k(b, c):
                n = 4 * b + c
                keys = bass.ds(b * KEYS + 512 * c, 512)
                hold(act, kv_done, n + 1)
                act.activation(k_parts[:, 0, keys], ps[:, 2 + c % 2, :], ACT.Identity,
                               bias=vec[:, BK:BK + 1]).then_inc(k1_ready, 1)
                hold(act, r1_ready, n + 1)
                copy(k_parts[:, 1, keys], k_r1[:, c % 2, :], k2_ready)

            def prep(b):
                for c in range(CHUNKS):
                    copy_ctx(b, c)
                    if c > 0:
                        split_k(b, c - 1)
                    elif not isinstance(b, int) or b > 0:
                        split_k(b - 1, CHUNKS - 1)
            loop_batches(act, prep)
            split_k(B - 1, CHUNKS - 1)

            def exp_unit(b, u):
                c = u % CHUNKS
                for h in range(2):
                    hold(act, keyscores_ready, 2 * (UNITS * b + u) + h + 1)
                    if h == 0:
                        hold(act, pv_done, UNITS * b + u - 3)
                    act.activation(probs[:, c, h, :], ps[:, 4 + h, :], ACT.Exp).then_inc(probs_ready, 1)

            def copy_out(b, p):
                hold(act, pv_done, CHUNKS * (PAIRS * b + p) + CHUNKS)
                hold(act, o_turned, PAIRS * b + p - 1)
                copy(oT_sb[:, p % 2, :], ps[:, 6 + p % 2, 0:P], oT_ready)

            def batch(b):
                first = isinstance(b, int) and b == 0
                for u in range(UNITS):
                    exp_unit(b, u)
                    if u % CHUNKS == 0:
                        if u > 0:
                            copy_out(b, u // CHUNKS - 1)
                        elif not first:
                            copy_out(b - 1, PAIRS - 1)
            loop_batches(act, batch)
            copy_out(B - 1, PAIRS - 1)

            act.wait_ge(once("oN_turned"), 1)
            copy(xnT[:, :], ps[:, 0, :], once("oNT_ready"))
            act.wait_ge(once("ln2_turned"), 1)
            copy(xnT[:, :], ps[:, 2, :], once("ln2T_ready"))

            act.wait_ge(once("small_ready"), 2)
            act.wait_ge(once("ssm_done"), 1)
            act.activation(SP_ABS, ps[:, 3, :], ACT.Abs, bias=sv[:, 5:6]).then_inc(once("sp_step"), 1)
            act.wait_ge(once("sp_step"), 1)
            act.activation(SP_EXP, SP_ABS, ACT.Exp, scale=-1.0).then_inc(once("sp_step"), 1)
            act.wait_ge(once("sp_step"), 2)
            act.activation(SP_LN, SP_EXP, ACT.Ln, bias=1.0).then_inc(once("sp_step"), 1)
            act.wait_ge(once("ssm_done"), 3)
            act.activation(G_B, ps[:, 4, :], ACT.Tanh, bias=vec[:, BP0 + 1:BP0 + 2]).then_inc(once("tanh_ready"), 1)
            act.activation(G_C, ps[:, 5, :], ACT.Tanh, bias=vec[:, BP0 + 2:BP0 + 3]).then_inc(once("tanh_ready"), 1)
            act.wait_ge(once("tanh_ready"), 2)
            act.activation(G_R, G_B, ACT.Square).then_inc(once("r_ready"), 1)
            act.activation(G_CC, G_C, ACT.Square).then_inc(once("cc_ready"), 1)
            act.wait_ge(once("delta_ready"), 1)
            act.activation(G_A0, DELTA, ACT.Exp, scale=sv[:, 4:5]).then_inc(once("a0_ready"), 1)
            act.wait_ge(once("disc_ready"), 1)
            act.activation(G_D, G_D, ACT.Sqrt).then_inc(once("disc_root"), 1)
            act.wait_ge(once("lam_ready"), 1)
            act.activation(G_CC, G_P, ACT.Sqrt).then_inc(once("lam_root"), 1)
            act.wait_ge(once("ln3_turned"), 1)
            copy(xnT[:, :], ps[:, 0, :], once("ln3T_ready"))
            for i in range(HB):
                act.wait_ge(once("h_done"), i + 1)
                act.activation(probs[:, i, 0, :], ps[:, 1 + i, :], ACT.Gelu, bias=vec[:, B1_0 + i:B1_0 + i + 1]
                               ).then_inc(once("gelu_ready"), 1)

        @block.gpsimd
        def _(gp):
            gp.memset(ones[:, :], 1.0).then_inc(once("ones_ready"), 1)
            gp.memset(neg_half[:, :], -0.5).then_inc(once("half_ready"), 1)

            def root_inv(name):
                gp.wait_ge(once(name + "_var"), 1)
                gp.tensor_tensor(rstd[:, :], var_eps[:, :], neg_half[:, :], ALU.pow).then_inc(once(name + "_rstd"), 1)

            def spread(v, n):
                return v.rearrange("(a n) -> a n", a=1).broadcast_to((P, n))
            for j in range(4):
                gp.dma_start(bv_rows[:, j, :], spread(bv, D)).then_inc(ld["rows"], 16)
            gp.dma_start(bo_rows[:, :], spread(bo, D)).then_inc(ld["rows"], 16)
            gp.dma_start(b2_rows[:, :], spread(b2, D)).then_inc(ld["rows"], 16)
            col = lambda v: v.rearrange("(p a) -> p a", a=1)
            gp.dma_start(vec[:, ALPHA:ALPHA + 1], col(alpha_log)).then_inc(ld["bias"], 16)
            gp.dma_start(vec[:, DBIAS:DBIAS + 1], col(delta_bias)).then_inc(ld["bias"], 16)
            gp.dma_start(vec[:, LGAM:LGAM + 1], log_gamma.broadcast_to((P, 1))).then_inc(ld["bias"], 16)
            for i in range(3):
                gp.dma_start(vec[:, BP0 + i:BP0 + i + 1], col(bp[P * i:P * i + P])).then_inc(ld["bias"], 16)
            for i in range(HB):
                gp.dma_start(vec[:, B1_0 + i:B1_0 + i + 1], col(b1[P * i:P * i + P])).then_inc(ld["bias"], 16)
            gp.dma_start(w1_nat[:, :, :], w1.rearrange("(a p) d -> p a d", p=P)).then_inc(ld["mlp"], 16)
            gp.dma_start(w2_nat[:, :], w2).then_inc(ld["mlp"], 16)
            gp.dma_start(mask_sb, mask.rearrange("a b q k -> (a b q) k")).then_inc(ld["mask"], 16)
            gp.wait_ge(once("half_ready"), 1)
            root_inv("xn")
            gp.memset(k_rows[:, :, :], 1.0).then_inc(once("pad_step"), 1)
            gp.memset(q_rows[:, :, :], 0.0).then_inc(once("pad_step"), 1)
            gp.memset(max_cols[:, :, :, :], 0.0).then_inc(once("pad_step"), 1)
            gp.wait_ge(ld["ident"], 48)
            gp.wait_ge(once("pad_step"), 3)
            gp.tensor_copy(ident_bf[:, :], ident[:, :]).then_inc(once("pads_ready"), 1)
            gp.wait_ge(ld["x"], 16)
            gp.wait_ge(ld["rows"], 16 * 6)
            for b in range(B):
                gp.tensor_tensor(x_bo[:, b, :], x_sb[:, b, :], bo_rows[:, :], ALU.add).then_inc(once("x_bo_ready"), 1)

            def third(b, c):
                n = 4 * b + c
                keys = bass.ds(b * KEYS + 512 * c, 512)
                hold(gp, k2_ready, n + 1)
                gp.tensor_tensor(k_parts[:, 2, keys], k_r1[:, c % 2, :], k_parts[:, 1, keys], ALU.subtract
                                 ).then_inc(k3_ready, 1)

            def prep(b):
                for c in range(CHUNKS):
                    third(b, c)
            with gp.Fori(0, B) as b:
                prep(b)

            def take_v(b, p):
                hold(gp, pv_done, CHUNKS * (PAIRS * b + p - 1))
                gp.tensor_copy(v_now[:, p % 2, :, :],
                               v_all[:, bass.ds(b * KT, KT), 2 * HEAD_COLS * p:2 * HEAD_COLS * (p + 1)]
                               ).then_inc(v_now_ready, 1)

            def split_max(b, p):
                i = PAIRS * b + p
                nm, r1, cols_ = negmax[:, p % 2, :], nm_r1[:, p % 2, :], max_cols[:, p % 2, :, :]
                hold(gp, negmax_ready, i + 1)
                hold(gp, max_turned, i - 1)
                gp.tensor_copy(cols_[:, :, MAX_ROW], nm).then_inc(split_step, 1)
                hold(gp, split_step, 4 * i + 1)
                gp.tensor_tensor(r1, nm, cols_[:, :, MAX_ROW], ALU.subtract).then_inc(split_step, 1)
                hold(gp, split_step, 4 * i + 2)
                gp.tensor_copy(cols_[:, :, MAX_ROW + 1], r1).then_inc(split_step, 1)
                hold(gp, split_step, 4 * i + 3)
                gp.tensor_tensor(cols_[:, :, MAX_ROW + 2], r1, cols_[:, :, MAX_ROW + 1], ALU.subtract
                                 ).then_inc(split_step, 1)

            gp.wait_ge(v_ready, B * CHUNKS)
            gp.wait_ge(once("v_ones_ready"), 1)
            def batch(b):
                for p in range(PAIRS):
                    split_max(b, p)
                    take_v(b, p)
            gp.wait_ge(once("norm_step"), 2)
            gp.tensor_tensor(norm_inv[:, :], norm_inv[:, :], neg_half[:, 0:2], ALU.pow).then_inc(once("norm_ready"), 1)
            loop_batches(gp, batch)
            root_inv("ln2")
            root_inv("ln3")

        @block.vector
        def _(dve):
            def layernorm(src, name):
                s = once(name + "_step")
                for b in range(B):
                    dve.bn_stats(bn[:, b, :], src[:, b, :]).then_inc(s, 1)
                dve.wait_ge(s, B)
                for b in range(B):
                    dve.bn_aggr(mv[:, b, :], bn[:, b, :]).then_inc(s, 1)
                dve.wait_ge(s, 2 * B)
                dve.tensor_scalar(var_eps[:, :], mv[:, :, 1], LN_EPS, None, ALU.add).then_inc(once(name + "_var"), 1)
                dve.wait_ge(once(name + "_rstd"), 1)
                for b in range(B):
                    dve.tensor_scalar(xn[:, b, :], src[:, b, :], mv[:, b, 0:1], rstd[:, b:b + 1],
                                      ALU.subtract, ALU.mult).then_inc(once(name + "_ready"), 1)

            dve.wait_ge(ld["x"], 16)
            layernorm(x_sb, "xn")
            dve.wait_ge(sq_done, 1)
            dve.tensor_copy(gram[:, :, :], ps[:, 6, 0:2 * P].rearrange("p (w d) -> p w d", w=2)
                            ).then_inc(once("gram_ready"), 1)
            dve.wait_ge(once("gram_ready"), 1)
            dve.tensor_copy(power[:, 0, :, :], gram[:, :, :]).then_inc(pow_ready, 1)
            dve.wait_ge(once("q_done"), 1)
            dve.wait_ge(ld["bias"], 16 * 10)
            dve.wait_ge(ld["bias_qk"], 32)
            dve.tensor_scalar(q32[:, :], ps[:, 5, :], vec[:, BQ:BQ + 1], 1.0 / math.sqrt(HD), ALU.add, ALU.mult
                              ).then_inc(once("q_step"), 1)
            dve.wait_ge(once("q_step"), 1)
            dve.tensor_copy(q_parts[:, 0, :], q32[:, :]).then_inc(once("q_step"), 1)
            dve.wait_ge(once("q_step"), 2)
            dve.tensor_tensor(q_r1[:, :], q32[:, :], q_parts[:, 0, :], ALU.subtract).then_inc(once("q_step"), 1)
            dve.wait_ge(once("q_step"), 3)
            dve.tensor_copy(q_parts[:, 1, :], q_r1[:, :]).then_inc(once("q_step"), 1)
            dve.wait_ge(once("q_step"), 4)
            dve.wait_ge(once("pads_ready"), 1)
            dve.tensor_tensor(q_parts[:, 2, :], q_r1[:, :], q_parts[:, 1, :], ALU.subtract
                              ).then_inc(once("q3_ready"), 1)
            dve.wait_ge(ld["mlp"], 32)
            for i in range(HB):
                dve.tensor_reduce(w_abs[:, i:i + 1], w1_nat[:, i, :], AX.X, ALU.add, apply_absolute_value=True
                                  ).then_inc(once("wabs_ready"), 1)
            dve.tensor_reduce(w_abs[:, HB:HB + 1], w2_nat[:, :], AX.X, ALU.add, apply_absolute_value=True
                              ).then_inc(once("wabs_ready"), 1)
            dve.wait_ge(once("wabs_ready"), HB + 1)
            w2_dst = slice(HB, 2 * HB)
            flat = lambda t, sl: t[:, sl, :].rearrange("p a d -> p (a d)")
            for sl, nat in ((slice(0, HB), w1_nat[:, :, :].rearrange("p a d -> p (a d)")), (w2_dst, w2_nat[:, :])):
                dve.tensor_scalar(flat(w_bin, sl), nat, 0.0, None, ALU.is_lt).then_inc(once("wsgn_step"), 1)
            dve.wait_ge(once("wsgn_step"), 2)
            for sl, nat in ((slice(0, HB), w1_nat[:, :, :].rearrange("p a d -> p (a d)")), (w2_dst, w2_nat[:, :])):
                dve.scalar_tensor_tensor(flat(w_sgn, sl), nat, 0.0, flat(w_bin, sl), ALU.is_gt, ALU.subtract
                                         ).then_inc(once("wsgn_step"), 1)
            dve.tensor_scalar(w_abs[:, 0:HB], w_abs[:, 0:HB], 1.0 / D, None, ALU.mult).then_inc(once("wsgn_step"), 1)
            dve.tensor_scalar(w_abs[:, HB:HB + 1], w_abs[:, HB:HB + 1], 1.0 / HID, None, ALU.mult
                              ).then_inc(once("wsgn_step"), 1)
            dve.wait_ge(once("wsgn_step"), 6)
            for i in range(2 * HB):
                nat = w1_nat[:, i, :] if i < HB else w2_nat[:, P * (i - HB):P * (i - HB) + P]
                a = w_abs[:, i:i + 1] if i < HB else w_abs[:, HB:HB + 1]
                dve.scalar_tensor_tensor(w_bin[:, i, :], w_sgn[:, i, :], a, nat, ALU.mult, ALU.subtract
                                         ).then_inc(once("wsgn_step"), 1)
            dve.wait_ge(once("wsgn_step"), 6 + 2 * HB)
            for sl, nat in ((slice(0, HB), w1_nat[:, :, :].rearrange("p a d -> p (a d)")), (w2_dst, w2_nat[:, :])):
                dve.tensor_tensor(flat(w_bin, sl), flat(w_bin, sl), nat, ALU.add).then_inc(once("w_bin_ready"), 1)
            dve.wait_ge(ld["mask"], 16)
            dve.tensor_reduce(mask_abs[:, :], mask_sb, AX.X, ALU.max, apply_absolute_value=True
                              ).then_inc(once("mask_abs_ready"), 1)
            dve.tensor_copy(mask_parts[:, 0, :], mask_sb).then_inc(once("mask_step"), 1)
            dve.wait_ge(once("mask_step"), 1)
            dve.tensor_tensor(mask_r, mask_sb, mask_parts[:, 0, :], ALU.subtract
                              ).then_inc(once("mask_step"), 1)
            dve.wait_ge(once("mask_step"), 2)
            dve.tensor_copy(mask_parts[:, 1, :], mask_r).then_inc(once("mask_step"), 1)
            dve.wait_ge(once("mask_step"), 3)
            dve.tensor_tensor(mask_parts[:, 2, :], mask_r, mask_parts[:, 1, :], ALU.subtract
                              ).then_inc(once("mask_step"), 1)
            dve.wait_ge(once("mask_turned"), 1)
            dve.tensor_reduce(mask_flag_f[:, :], ps[0:1, 2, 0:P], AX.X, ALU.max).then_inc(once("flag_step"), 1)
            dve.wait_ge(once("flag_step"), 1)
            dve.wait_ge(once("mask_step"), 4)
            dve.tensor_scalar(mask_flag[:, :], mask_flag_f[:, :], 0.0, None, ALU.is_gt
                              ).then_inc(once("mask_flag_ready"), 1)
            dve.memset(v_all[:, :, :].rearrange("p t (h m) -> p (t h) m", m=HEAD_COLS)[:, :, HD:HD + 1], 1.0
                       ).then_inc(once("v_ones_ready"), 1)
            dve.wait_ge(once("alpha_step"), 4)
            dve.tensor_scalar(sv[:, 6:7], vec[:, ALPHA:ALPHA + 1], 0.0, sv[:, 2:3], ALU.max, ALU.add
                              ).then_inc(once("small_step"), 1)
            dve.wait_ge(once("small_step"), 1)
            dve.tensor_scalar(sv[:, 4:5], sv[:, 6:7], -1.0, None, ALU.mult).then_inc(once("small_ready"), 1)
            dve.tensor_tensor(sv[:, 5:6], vec[:, BP0:BP0 + 1], vec[:, DBIAS:DBIAS + 1], ALU.add
                              ).then_inc(once("small_ready"), 1)
            dve.wait_ge(ld["rows"], 16 * 6)
            dve.wait_ge(once("ones_ready"), 1)
            dve.wait_ge(once("wT_ready"), 1)
            dve.memset(sv[:, 11:12], 0.0).then_inc(once("pe_setup_copied"), 3)

            def rest_k(b, c):
                n = 4 * b + c
                keys = bass.ds(b * KEYS + 512 * c, 512)
                dve.wait_ge(k1_ready, n + 1)
                wait(dve, k3_ready, n - 1)
                wait(dve, k2_ready, n - 1)
                dve.scalar_tensor_tensor(k_r1[:, c % 2, :], ps[:, 2 + c % 2, :], vec[:, BK:BK + 1],
                                         k_parts[:, 0, keys], ALU.add, ALU.subtract).then_inc(r1_ready, 1)

            def take_vall(b, c):
                dve.wait_ge(kv_done, 4 * b + c + 1)
                dst = v_all[:, bass.ds(b * KT + 4 * c, 4), :].rearrange("p t (h m) -> p t h m", m=HEAD_COLS)
                dve.tensor_tensor(dst[:, :, :, 0:HD],
                                  ps[:, 4 + c % 2, :].rearrange("p (t h m) -> p t h m", t=4, m=HD),
                                  bv_rows[:, :, :].rearrange("p t (h m) -> p t h m", m=HD), ALU.add
                                  ).then_inc(v_ready, 1)

            def next_power(k, at, norms):
                if at % SQ_PERIOD == 0:
                    for w in range(2):
                        dve.tensor_tensor_reduce(sq_junk[:, w, :], power[:, at % 2, w, :], power[:, at % 2, w, :],
                                                 1.0, 0.0, ALU.mult, ALU.add, fro[:, w:w + 1]).then_inc(fro_ready, 1)
                    dve.wait_ge(fro_summed, norms + 1)
                    dve.tensor_scalar(fro_inv[:, :], ps[:, 7, 0:2], TINY, None, ALU.max).then_inc(fro_inv_ready, 1)
                    dve.wait_ge(fro_inv_ready, 2 * norms + 1)
                    dve.reciprocal(fro_inv[:, :], fro_inv[:, :]).then_inc(fro_inv_ready, 1)
                    dve.wait_ge(fro_inv_ready, 2 * norms + 2)
                    dve.wait_ge(sq_done, k + 2)
                    for w in range(2):
                        t = dve.tensor_scalar(power[:, (at + 1) % 2, w, :], ps[:, 6, P * w:P * w + P],
                                              fro_inv[:, w:w + 1], None, ALU.mult)
                        if w == 0:
                            t.then_inc(once("pow_half"), 1)
                    t.then_inc(pow_ready, 1)
                else:
                    dve.wait_ge(sq_done, k + 2)
                    dve.tensor_copy(power[:, (at + 1) % 2, :, :],
                                    ps[:, 6, 0:2 * P].rearrange("p (w d) -> p w d", w=2)).then_inc(pow_ready, 1)

            def prep(b):
                at = 0
                for c in range(CHUNKS):
                    dve.wait_ge(pow_ready, 6 * b + at + 1)
                    next_power(6 * b + at, at, 2 * b + at // SQ_PERIOD)
                    at += 1
                    if c > 0 or not isinstance(b, int) or b > 0:
                        pb, pc = (b, c - 1) if c > 0 else (b - 1, CHUNKS - 1)
                        rest_k(pb, pc)
                        take_vall(pb, pc)
                    if c % 2 == 1:
                        dve.wait_ge(pow_ready, 6 * b + at + 1)
                        next_power(6 * b + at, at, 2 * b + at // SQ_PERIOD)
                        at += 1
            loop_batches(dve, prep)
            rest_k(B - 1, CHUNKS - 1)
            take_vall(B - 1, CHUNKS - 1)
            dve.wait_ge(once("q_loaded"), 16 * PAIRS * len(Q_BLOCKS))
            for h in range(2):
                dve.tensor_scalar(q_rows[0:MAX_ROW, :, :, h, :].rearrange("r p b q -> r (p b) q"),
                                  q_both[0:MAX_ROW, :, :].rearrange("r p (b q) -> r (p b) q", b=B),
                                  head_rows[0:MAX_ROW, h:h + 1], None, ALU.mult).then_inc(once("q_rows_ready"), 1)
            dve.wait_ge(once("ray_done"), 1)
            for w in range(2):
                dve.tensor_tensor_reduce(sq_junk[:, w, :], ps[:, 6, P * w:P * w + P], power[:, 0, w, :],
                                         1.0, 0.0, ALU.mult, ALU.add, ray[:, w:w + 1]).then_inc(once("ray_ready"), 1)
            dve.wait_ge(once("ray_ready"), 2)
            for w in range(2):
                dve.tensor_tensor_reduce(sq_junk[:, w, :], power[:, 0, w, :], power[:, 0, w, :],
                                         1.0, 0.0, ALU.mult, ALU.add, ray[:, 2 + w:3 + w]
                                         ).then_inc(once("ray_ready"), 1)
            dve.wait_ge(once("ray_summed"), 1)
            dve.tensor_scalar(ray_all[:, :], ps[:, 7, 0:4], TINY, None, ALU.max).then_inc(once("ray_all_ready"), 1)
            dve.wait_ge(once("ray_all_ready"), 1)
            dve.reciprocal(fro_inv[:, :], ray_all[:, 2:4]).then_inc(once("ray_inv"), 1)
            dve.wait_ge(once("ray_inv"), 1)
            dve.tensor_tensor(norm_inv[:, :], ray_all[:, 0:2], fro_inv[:, :], ALU.mult).then_inc(once("norm_step"), 1)
            dve.wait_ge(once("norm_step"), 1)
            dve.tensor_scalar(norm_inv[:, :], norm_inv[:, :], 1.0, None, ALU.max).then_inc(once("norm_step"), 1)
            for i in range(2):
                dve.memset(ps[:, 6 + i, 0:P], 0.0).then_inc(once("out_banks_zeroed"), 1)

            def max_unit(b, u):
                p, c = divmod(u, CHUNKS)
                dve.wait_ge(scores_ready, UNITS * b + u + 1)
                if c == 0:
                    wait(dve, negmax_ready, PAIRS * b + p - 1)
                bank = 2 * (u % 2)
                dve.tensor_reduce(pmax[:, p % 2, :, c], ps[:, bank:bank + 2, :], AX.X, ALU.max
                                  ).then_inc(pmax_ready, 1)

            def neg_max(b, p):
                i = PAIRS * b + p
                dve.wait_ge(pmax_ready, CHUNKS * i + CHUNKS)
                wait(dve, split_step, 4 * (i - 1))
                dve.tensor_reduce(negmax[:, p % 2, :], pmax[:, p % 2, :, :], AX.X, ALU.max, negate=True
                                  ).then_inc(negmax_ready, 1)

            def add_max(b, p):
                dve.wait_ge(max_turned, PAIRS * b + p + 1)
                wait(dve, keyscores_ready, 2 * CHUNKS * (PAIRS * b + p - 1))
                dve.tensor_tensor(q_max[:, p % 2, :, :],
                                  ps[:, 6 + p % 2, 128:384].rearrange("r (h q) -> r h q", h=2),
                                  q_rows[:, p, bass.ds(b, 1), :, :].rearrange("r b h q -> r (b h) q"), ALU.add).then_inc(q_max_ready, 1)

            def normalise(b, p):
                i = PAIRS * b + p
                o = ps[:, 6 + p % 2, 384:384 + 2 * HEAD_COLS].rearrange("q (h m) -> q h m", h=2)
                dve.wait_ge(o_turned, i + 1)
                wait(dve, o_ready, i - 1)
                dve.reciprocal(rden[:, p % 2, :], o[:, :, HD]).then_inc(rden_ready, 1)
                dve.wait_ge(rden_ready, i + 1)
                dve.tensor_tensor(o_nat[:, bass.ds(b, 1), 16 * p:16 * p + 16].rearrange("q b (h m) -> q (b h) m", h=2),
                                  o[:, :, 0:HD], rden[:, p % 2, :].unsqueeze(2).broadcast_to((P, 2, HD)), ALU.mult
                                  ).then_inc(o_ready, 1)

            def before(b, p, lag):
                if p >= lag:
                    return b, p - lag
                if isinstance(b, int) and b == 0:
                    return None
                return b - 1, p - lag + PAIRS

            def batch(b):
                for u in range(UNITS):
                    p, c = divmod(u, CHUNKS)
                    max_unit(b, u)
                    if c == CHUNKS - 1:
                        neg_max(b, p)
                    if c == 0 and before(b, p, 3):
                        normalise(*before(b, p, 3))
                    if c == 1 and before(b, p, 1):
                        add_max(*before(b, p, 1))
            dve.wait_ge(once("q_rows_ready"), 2)
            loop_batches(dve, batch)
            normalise(B - 1, PAIRS - 3)
            add_max(B - 1, PAIRS - 1)
            normalise(B - 1, PAIRS - 2)
            normalise(B - 1, PAIRS - 1)

            tail = once("tail_step")
            steps = [0]

            def step(t, wait_for=True):
                t.then_inc(tail, 1)
                steps[0] += 1
                if wait_for:
                    dve.wait_ge(tail, steps[0])

            dve.wait_ge(once("norm_ready"), 1)
            step(dve.tensor_tensor(sv[:, 7:8], sv[:, 3:4], norm_inv[:, 0:1], ALU.mult))
            flat_bd = lambda t: t[:, :, :].rearrange("p b d -> p (b d)")
            dve.wait_ge(once("attn_done"), 1)
            dve.wait_ge(once("x_bo_ready"), B)
            step(dve.tensor_tensor(flat_bd(x_sb), ps[:, 1, :], flat_bd(x_bo), ALU.add))
            layernorm(x_sb, "ln2")
            dve.wait_ge(once("ssm_done"), 4)
            dve.wait_ge(once("sp_step"), 3)
            step(dve.tensor_scalar(DELTA, ps[:, 3, :], sv[:, 5:6], 0.0, ALU.add, ALU.max))
            dve.tensor_tensor(DELTA, DELTA, SP_LN, ALU.add).then_inc(once("delta_ready"), 1)
            step(dve.tensor_scalar(U_S, ps[:, 6, :], sv[:, 7:8], None, ALU.mult))
            dve.wait_ge(once("tanh_ready"), 2)
            step(dve.tensor_tensor(U_S, U_S, G_B, ALU.mult))
            dve.wait_ge(once("a0_ready"), 1)
            step(dve.tensor_scalar(G_A, G_A0, 1.0 - EPS_A, None, ALU.min))
            step(dve.tensor_tensor(G_Q, G_A, G_B, ALU.mult), False)
            step(dve.tensor_tensor(G_P, G_A, G_A, ALU.mult))
            dve.wait_ge(once("cc_ready"), 1)
            step(dve.tensor_tensor(G_P, G_P, G_CC, ALU.add))
            dve.wait_ge(once("r_ready"), 1)
            step(dve.tensor_tensor(G_D, G_P, G_R, ALU.subtract), False)
            step(dve.tensor_tensor(G_P, G_P, G_R, ALU.add))
            step(dve.tensor_tensor(G_D, G_D, G_D, ALU.mult), False)
            step(dve.scalar_tensor_tensor(G_Q, G_Q, 4.0, G_Q, ALU.mult, ALU.mult))
            dve.scalar_tensor_tensor(G_D, G_D, EPS, G_Q, ALU.add, ALU.add).then_inc(once("disc_ready"), 1)
            dve.wait_ge(once("disc_root"), 1)
            step(dve.tensor_tensor(G_P, G_P, G_D, ALU.add))
            step(dve.tensor_scalar(G_P, G_P, 0.5, EPS, ALU.mult, ALU.add))
            dve.tensor_scalar(G_P, G_P, 1.0, None, ALU.max).then_inc(once("lam_ready"), 1)
            dve.wait_ge(once("lam_root"), 1)
            step(dve.reciprocal(G_P, G_CC))
            step(dve.tensor_tensor(G_A, G_A, G_P, ALU.mult), False)
            step(dve.tensor_tensor(U_S, U_S, G_P, ALU.mult), False)
            step(dve.tensor_tensor(G_CS, G_C, G_P, ALU.mult))
            for b in range(B):
                t = slice(T * b, T * b + T)
                step(dve.tensor_tensor_scan(STATE[:, t], G_A[:, t], U_S[:, t], 0.0, ALU.mult, ALU.add), False)
            step(dve.memset(q_r1[:, :].rearrange("p (b t) -> p b t", b=B)[:, :, 0:1], 0.0))
            by_t = lambda a: a.rearrange("p (b t) -> p b t", b=B)
            dve.tensor_tensor(by_t(q_r1[:, :])[:, :, 1:T], by_t(G_CS)[:, :, 1:T], by_t(STATE)[:, :, 0:T - 1],
                              ALU.mult).then_inc(once("yhat_ready"), 1)
            dve.wait_ge(once("y_done"), 1)
            step(dve.scalar_tensor_tensor(flat_bd(x_sb), ps[:, 7, :], norm_inv[:, 1:2], flat_bd(x_sb),
                                          ALU.mult, ALU.add))
            layernorm(x_sb, "ln3")
            for b in range(B):
                step(dve.tensor_tensor(x_bo[:, b, :], x_sb[:, b, :], b2_rows[:, :], ALU.add), b == B - 1)
            dve.wait_ge(once("mlp_done"), 1)
            dve.wait_ge(once("ln3_turned"), 1)
            dve.tensor_tensor(flat_bd(xn), ps[:, 5, :], flat_bd(x_bo), ALU.add).then_inc(once("out_ready"), 1)


_INS = ['x', 'ctx_1024', 'mask_1x1xSxS2_ff0', 'L0_xattn_Wq', 'L0_xattn_bq', 'L0_xattn_Wk', 'L0_xattn_bk',
        'L0_xattn_Wv', 'L0_xattn_bv', 'L0_xattn_Wo', 'L0_xattn_bo', 'L0_attn_W_in', 'L0_attn_W_out', 'L0_attn_Wp',
        'L0_attn_bp', 'L0_attn_alpha_log', 'L0_attn_delta_bias', 'L0_attn_log_gamma', 'L0_ffn_w1', 'L0_ffn_b1',
        'L0_ffn_w2', 'L0_ffn_b2']


def kernel(**inputs):
    import numpy as _np
    import concourse.bacc as _bacc
    from concourse import mybir as _mybir
    from concourse.bass_utils import run_bass_kernel_spmd as _run

    gather = _np.zeros((P, 2 * HEAD_COLS), _np.float32)
    for tile in range(4):
        for m in range(HEAD_COLS):
            gather[32 * tile + m, HEAD_COLS * (tile % 2) + m] = 1.0
    head_rows = (_np.arange(P)[:, None] // 8 % 2 == _np.arange(2)[None, :]).astype(_np.float32)
    consts = {"ident": _np.eye(P, dtype=_np.float32), "gather": gather, "head_rows": head_rows}

    nc = _bacc.Bacc("TRN2", target_bir_lowering=False, num_devices=1)
    arrays, args = {}, []
    for name in _INS + list(consts):
        a = _np.ascontiguousarray(consts[name] if name in consts else inputs[name])
        if a.ndim == 0:
            a = a.reshape(1)
        arrays[f"in_{name}_dram"] = a
        args.append(nc.dram_tensor(f"in_{name}_dram", a.shape, _mybir.dt.from_np(a.dtype),
                                   kind="ExternalInput").ap())
    args.append(nc.dram_tensor("out_0_dram", (4, 128, 128), _mybir.dt.float32, kind="ExternalOutput").ap())
    perceiver_block(nc, *args)
    r = _run(nc, [arrays], core_ids=[0])
    return r.results[0]["out_0_dram"]
```

```python
import concourse.bass as bass
from concourse import mybir
from contextlib import ExitStack
import math

F32 = mybir.dt.float32
BF16 = mybir.dt.bfloat16
I32 = mybir.dt.int32
ALU = mybir.AluOpType
ACT = mybir.ActivationFunctionType
AX = mybir.AxisListType

P = 128
HEAD_COLS = 9
SQUARINGS = 24
SQ_PERIOD = 3
TINY = 1e-30
LN_EPS = 1e-5
EPS = 1e-12
EPS_A = 1e-4


def perceiver_block(nc, x, ctx_in, mask, Wq, bq, Wk, bk, Wv, bv, Wo, bo, W_in, W_out, Wp, bp,
                    alpha_log, delta_bias, log_gamma, w1, b1, w2, b2, ident_in, gather_in, head_rows_in, out):
    B, T, D = x.shape
    KEYS = ctx_in.shape[1]
    HEADS = 16
    HD = D // HEADS
    PAIRS = HEADS // 2
    CHUNKS = KEYS // 512
    KT = KEYS // P
    HID = w1.shape[0]
    HB = HID // P
    TOK = B * T
    UNITS = PAIRS * CHUNKS
    LEAD = 8
    assert (T, D, CHUNKS, B, HD) == (128, 128, 4, 4, 8)
    K_BLOCKS = (0, 1, 2, 0, 1, 0)
    Q_BLOCKS = (0, 0, 0, 1, 1, 2)
    MAX_ROW = 16 * len(Q_BLOCKS)
    BK, BQ, BV, ALPHA, DBIAS, BP0, B1_0, VECS = 0, 1, 2, 3, 4, 5, 8, 12

    ctx = ExitStack()
    with ctx:
        def sb(name, shape, dt=F32):
            return ctx.enter_context(nc.sbuf_tensor(name, shape, dt))

        sems = {}

        def sem(name):
            sems[name] = ctx.enter_context(nc.semaphore(name))
            return sems[name]

        ident = sb("ident", [P, P])
        ident_bf = sb("ident_bf", [P, P], BF16)
        head_rows = sb("head_rows", [P, 2])
        gather = sb("gather", [P, 2 * HEAD_COLS])
        ones = sb("ones", [P, P])
        x_sb = sb("x_sb", [P, B, D])
        w_kv = sb("w_kv", [P, 2, D])
        w_nat = sb("w_nat", [P, 7, D])
        w1_nat = sb("w1_nat", [P, HB, D])
        w2_nat = sb("w2_nat", [P, HID])
        kvT = sb("kvT", [P, 2, D])
        wT = sb("wT", [P, 7, D])
        W_IN, W_OUT, W_P, W_Q, W_O = 0, 1, 2, 5, 6
        w1T = sb("w1T", [P, HB, P])
        w2T = sb("w2T", [P, HB, D])
        vec_nat = sb("vec_nat", [VECS, P])
        vec = sb("vec", [P, VECS])
        log_gain = sb("log_gain", [P, 1])
        bo_rows = sb("bo_rows", [P, D])
        b2_rows = sb("b2_rows", [P, D])
        x_bo = sb("x_bo", [P, B, D])
        bn = sb("bn", [P, B, 6])
        mv = sb("mv", [P, B, 2])
        var_eps = sb("var_eps", [P, B])
        rstd = sb("rstd", [P, B])
        neg_half = sb("neg_half", [P, B])
        xn = sb("xn", [P, B, D])
        xnT = sb("xnT", [P, TOK])
        q32 = sb("q32", [P, TOK])
        q_r1 = sb("q_r1", [P, TOK])
        q_parts = sb("q_parts", [P, 3, TOK], BF16)
        q_rows = sb("q_rows", [P, PAIRS, B, 2, T], BF16)
        ctx_buf = sb("ctx_buf", [P, CHUNKS, 4, D])
        ctxT = sb("ctxT", [P, 2, 512])
        k_parts = sb("k_parts", [P, 3, B * KEYS], BF16)
        k_r1 = sb("k_r1", [P, 2, 512])
        v_all = sb("v_all", [P, B * KT, HEADS * HEAD_COLS])
        k_rows = sb("k_rows", [P, 4, KEYS], BF16)
        q_max = sb("q_max", [P, 2, 2, T], BF16)
        v_now = sb("v_now", [P, 2, KT, 2 * HEAD_COLS])
        pmax = sb("pmax", [P, 2, 2, CHUNKS])
        negmax = sb("negmax", [P, 2, 2])
        nm_r1 = sb("nm_r1", [P, 2, 2])
        max_cols = sb("max_cols", [P, 2, 2, P], BF16)
        probs = sb("probs", [P, 4, 2, 512])
        oT_sb = sb("oT_sb", [P, 2, P])
        rden = sb("rden", [P, 2, 2])
        o_nat = w1_nat
        mask_sb = sb("mask_sb", [P, KEYS])
        select = sb("select", [P, 3, PAIRS, MAX_ROW], BF16)
        mask_abs = sb("mask_abs", [P, 1])
        mask_flag_f = sb("mask_flag_f", [1, 1])
        mask_flag = sb("mask_flag", [1, 1], I32)
        gram = sb("gram", [P, 2, P])
        power = sb("power", [P, 2, 2, P])
        sq_junk = sb("sq_junk", [P, 2, P])
        fro = sb("fro", [P, 2])
        fro_inv = sb("fro_inv", [P, 2])
        ray = sb("ray", [P, 4])
        norm_inv = sb("norm_inv", [P, 2])
        ray_all = sb("ray_all", [P, 4])
        sv = sb("sv", [P, 12])
        w_abs = sb("w_abs", [P, HB + 1])

        ps = ctx.enter_context(nc.psum_tensor("ps", [P, 8, 512], F32))

        w_sgn = probs[:, 2, :, :].rearrange("p b (i n) -> p (b i) n", n=P)
        w_bin = probs[:, 3, :, :].rearrange("p b (i n) -> p (b i) n", n=P)
        gates = k_parts[:, :, :].rearrange("p a n -> p (a n)")[:, 0:15 * 2 * TOK].bitcast(F32).rearrange(
            "p (i n) -> p i n", n=TOK)
        (SP_ABS, SP_EXP, SP_LN, G_B, G_C, G_R, G_CC, G_A0, DELTA, U_S, G_A, G_Q, G_P, G_D, G_CS
         ) = (gates[:, i, :] for i in range(15))
        STATE = q32[:, :]

        ld = {n: sem("ld_" + n) for n in ("ident", "x", "kv", "vec", "ssm", "w", "head_rows", "mlp", "mask", "rows", "gather", "log_gain", "wp")}
        ctx_loaded = [sem(f"ctx_loaded{c}") for c in range(CHUNKS)]
        ctx_turned = sem("ctx_turned")
        ctxT_ready = sem("ctxT_ready")
        k_done = sem("k_done")
        v_done = sem("v_done")
        k1_ready = sem("k1_ready")
        r1_ready = sem("r1_ready")
        k2_ready = sem("k2_ready")
        k3_ready = sem("k3_ready")
        v_ready = sem("v_ready")
        sq_done = sem("sq_done")
        pow_ready = sem("pow_ready")
        fro_ready = sem("fro_ready")
        fro_summed = sem("fro_summed")
        fro_inv_ready = sem("fro_inv_ready")
        k_rows_loaded = [sem(f"k_rows_loaded{s}") for s in range(4)]
        v_now_ready = sem("v_now_ready")
        scores_ready = sem("scores_ready")
        pmax_ready = sem("pmax_ready")
        negmax_ready = sem("negmax_ready")
        split_step = sem("split_step")
        max_turned = sem("max_turned")
        q_max_ready = sem("q_max_ready")
        keyscores_ready = sem("keyscores_ready")
        probs_ready = sem("probs_ready")
        pv_done = sem("pv_done")
        oT_ready = sem("oT_ready")
        o_turned = sem("o_turned")
        rden_ready = sem("rden_ready")
        o_ready = sem("o_ready")
        stored = sem("stored")

        def once(name):
            return sems[name] if name in sems else sem(name)

        def wait(eng, s, value):
            if isinstance(value, int) and value <= 0:
                return
            eng.wait_ge(s, value)

        def hold(eng, s, value):
            wait(eng, s, value)
            if not isinstance(value, int):
                eng.sem_inc(once("passed_a_hold"))

        def chunk_before(b, c, lag):
            if c >= lag:
                return b, c - lag
            return None if isinstance(b, int) and b == 0 else (b - 1, c - lag + CHUNKS)

        def loop_batches(eng, body):
            body(0)
            with eng.Fori(1, B - 1) as b:
                body(b)
            body(B - 1)

        block = ctx.enter_context(nc.Block())

        @block.sync
        def _(sp):
            def load_ctx(b, c):
                if not isinstance(b, int) or b > 0:
                    wait(sp, ctx_turned, 4 * (b - 1) + c + 1)
                sp.dma_start(ctx_buf[:, c, :, :],
                             ctx_in[bass.ds(b, 1), 512 * c:512 * c + 512, :].rearrange(
                                 "b (p j) d -> p (b j) d", j=4)).then_inc(ctx_loaded[c], 16)

            sp.dma_start(w_kv[:, 0, :], Wk).then_inc(ld["kv"], 16)
            load_ctx(0, 0)
            sp.dma_start(w_kv[:, 1, :], Wv).then_inc(ld["kv"], 16)
            sp.dma_start(w_nat[:, W_IN, :], W_in).then_inc(ld["ssm"], 16)
            sp.dma_start(w_nat[:, W_OUT, :], W_out).then_inc(ld["ssm"], 16)
            load_ctx(0, 1)
            sp.dma_start(x_sb[:, :, :], x.rearrange("b t d -> t b d")).then_inc(ld["x"], 16)
            load_ctx(0, 2)
            load_ctx(0, 3)
            sp.dma_start(w_nat[:, W_P:W_P + 3, :], Wp.rearrange("(a p) d -> p a d", p=P)).then_inc(ld["wp"], 16)
            sp.dma_start(w_nat[:, W_Q, :], Wq).then_inc(ld["w"], 16)
            sp.dma_start(w_nat[:, W_O, :], Wo).then_inc(ld["w"], 16)
            load_ctx(1, 0)
            sp.dma_start(w1_nat[:, :, :], w1.rearrange("(a p) d -> p a d", p=P)).then_inc(ld["mlp"], 16)
            sp.dma_start(w2_nat[:, :], w2).then_inc(ld["mlp"], 16)

            def load_pair(b, p, blocks=range(len(K_BLOCKS))):
                slot = p % 4
                wait(sp, keyscores_ready, 2 * CHUNKS * (PAIRS * b + p - 3))
                for block in blocks:
                    part = K_BLOCKS[block]
                    sp.dma_start(k_rows[16 * block:16 * block + 16, slot, :],
                                 k_parts[16 * p:16 * p + 16, part, bass.ds(b * KEYS, KEYS)]
                                 ).then_inc(k_rows_loaded[slot], 16)

            for c in range(1, CHUNKS):
                load_ctx(1, c)
            sp.dma_start(mask_sb[:, :], mask.rearrange("a b q k -> (a b q) k")).then_inc(ld["mask"], 16)
            half = len(K_BLOCKS) // 2
            sp.wait_ge(once("k_pads_ready"), 1)
            for n in range(2 * CHUNKS, B * CHUNKS):
                load_ctx(n // CHUNKS, n % CHUNKS)
                i = n - 2 * CHUNKS
                if i == 0:
                    sp.wait_ge(k3_ready, CHUNKS)
                load_pair(0, i // 2, range(half * (i % 2), half * (i % 2) + half))

            def pairs(b, first=0):
                sp.wait_ge(k3_ready, CHUNKS * b + CHUNKS)
                for p in range(first, PAIRS):
                    load_pair(b, p)
            pairs(0, 4)
            with sp.Fori(1, B) as b:
                pairs(b)

            sp.wait_ge(once("out_ready"), 1)
            sp.dma_start(out.rearrange("b t d -> t b d"), xn[:, :, :]).then_inc(stored, 16)
            sp.wait_ge(stored, 16)

        @block.tensor
        def _(pe):
            pe.wait_ge(ld["ident"], 16)

            def turn(dst, src):
                return pe.transpose(dst, src, ident[:, :])

            pe.wait_ge(ld["kv"], 32)
            for i in range(2):
                turn(ps[:, 1, P * i:P * i + P], w_kv[:, i, :])
            pe.wait_ge(ld["vec"], 16 * 7)
            pe.transpose(ps[:, 1, 2 * P:2 * P + VECS], vec_nat[:, :], ident[0:VECS, 0:VECS]
                         ).then_inc(once("kv_turned"), 1)

            def turn_ctx(b, c):
                n = 4 * b + c
                wait(pe, ctxT_ready, n)
                pe.wait_ge(ctx_loaded[c], 16 * b + 16)
                for j in range(4):
                    t = turn(ps[:, 0, P * j:P * j + P], ctx_buf[:, c, j, :])
                t.then_inc(ctx_turned, 1)

            def project_k(b, c):
                n = 4 * b + c
                pe.wait_ge(ctxT_ready, n + 1)
                wait(pe, k1_ready, n - 1)
                wait(pe, r1_ready, n - 1)
                pe.matmul(ps[:, 2 + c % 2, :], kvT[:, 0, :], ctxT[:, c % 2, :], start=True, stop=True
                          ).then_inc(k_done, 1)

            def project_v(b, c):
                wait(pe, v_ready, 4 * b + c - 1)
                for j in range(4):
                    t = pe.matmul(ps[:, 4 + c % 2, P * j:P * j + P], ctxT[:, c % 2, P * j:P * j + P], kvT[:, 1, :],
                                  start=True, stop=True)
                t.then_inc(v_done, 1)

            def square(b, at):
                k, norms = 6 * b + at, 2 * b + at // SQ_PERIOD
                if at % SQ_PERIOD == 0:
                    pe.wait_ge(fro_ready, 2 * norms + 2)
                    pe.matmul(ps[:, 7, 0:2], ones[:, :], fro[:, :], start=True, stop=True
                              ).then_inc(fro_summed, 1)
                pe.wait_ge(pow_ready, k + 1)
                for w in range(2):
                    t = pe.matmul(ps[:, 6, P * w:P * w + P], power[:, at % 2, w, :], power[:, at % 2, w, :],
                                  start=True, stop=True)
                t.then_inc(sq_done, 1)

            def place_q(b, c):
                pair = CHUNKS * (b - 1) + c
                pe.wait_ge(once("q_bank_free"), 2 * pair + 1)
                for part in range(3):
                    t = pe.matmul(ps[0:MAX_ROW, 1, :],
                                  select[:, part, bass.ds(pair, 1), :].rearrange("k p m -> k (p m)"),
                                  q_parts[:, part, :], start=part == 0, stop=part == 2)
                t.then_inc(once("q_placed"), 1)

            def turn_weights(first, n, s):
                for i in range(n):
                    t = turn(ps[:, 1, P * i:P * i + P], w_nat[:, first + i, :])
                t.then_inc(s, 1)

            def prep(b, extra):
                at = 0
                for c in range(CHUNKS):
                    last = chunk_before(b, c, 1)
                    turn_ctx(b, c)
                    square(b, at)
                    at += 1
                    if last:
                        project_k(*last)
                    if c % 2 == 1:
                        square(b, at)
                        at += 1
                    if last:
                        project_v(*last)
                    extra(b, c)

            def extra_first(b, c):
                if c == 0:
                    pe.wait_ge(once("kvT_ready"), 1)
                    pe.wait_ge(ld["wp"], 16)
                    turn_weights(0, 4, once("w_turned"))
                elif c == 1:
                    pe.wait_ge(once("wT_ready"), 1)
                    pe.wait_ge(ld["w"], 32)
                    turn_weights(4, 3, once("w_turned"))
                elif c == 2:
                    pe.wait_ge(once("wT_ready"), 2)
                    pe.wait_ge(once("xn_ready"), B)
                    for i in range(B):
                        t = turn(ps[:, 1, P * i:P * i + P], xn[:, i, :])
                    t.then_inc(once("xn_turned"), 1)
                else:
                    pe.wait_ge(once("xnT_ready"), 1)
                    pe.matmul(ps[:, 1, :], wT[:, W_Q, :], xnT[:, :], start=True, stop=True).then_inc(once("q_done"), 1)

            def extra_last(b, c):
                if c < 2:
                    pe.wait_ge(once("w_bin_ready"), 2)
                    if c == 0:
                        pe.wait_ge(once("q_bank_free"), 2 * PAIRS + 1)
                    else:
                        pe.wait_ge(once("w1T_ready"), 1)
                    for i in range(HB):
                        t = turn(ps[:, 1, P * i:P * i + P], w_bin[:, HB * c + i, :])
                    t.then_inc(once("w_bin_turned"), 1)
                elif c == 2:
                    pe.wait_ge(once("w2T_ready"), 1)
                    pe.wait_ge(once("mask_abs_ready"), 1)
                    turn(ps[0:1, 1, 0:P], mask_abs[:, :]).then_inc(once("mask_turned"), 1)

            pe.wait_ge(ld["ssm"], 32)
            for w in range(2):
                t = pe.matmul(ps[:, 6, P * w:P * w + P], w_nat[:, w, :], w_nat[:, w, :], start=True, stop=True)
            t.then_inc(sq_done, 1)
            pe.wait_ge(once("kvT_ready"), 1)
            pe.wait_ge(once("ones_ready"), 1)
            prep(0, extra_first)
            with pe.Fori(1, B - 1) as b:
                prep(b, place_q)
            prep(B - 1, extra_last)
            project_k(B - 1, CHUNKS - 1)
            pe.wait_ge(pow_ready, SQUARINGS + 1)
            for w in range(2):
                t = pe.matmul(ps[:, 6, P * w:P * w + P], gram[:, w, :], power[:, 0, w, :], start=True, stop=True)
            t.then_inc(once("ray_done"), 1)
            project_v(B - 1, CHUNKS - 1)

            def mask_query(bank, c):
                pe.matmul(ps[:, bank, :], ident[:, :], mask_sb[:, 512 * c:512 * c + 512].rearrange(
                    "q (p j) -> q j p", j=4), start=True, stop=False)

            def mask_key(dst, c, j, first):
                keys = mask_sb[:, 512 * c:512 * c + 512].rearrange("q (p j) -> q j p", j=4)
                pe.matmul(dst, keys[:, j, :], ident[:, :], start=first, stop=False, skip_group_check=True)

            def scores(b, u, masked):
                p, c = divmod(u, CHUNKS)
                slot = p % 4
                if c == 0:
                    pe.wait_ge(k_rows_loaded[slot], 16 * len(K_BLOCKS) * (2 * b + p // 4 + 1))
                wait(pe, pmax_ready, UNITS * b + u - 1)
                bank = 2 * (u % 2)
                if masked:
                    for h in range(2):
                        mask_query(bank + h, c)
                for h in range(2):
                    t = pe.matmul(ps[:, bank + h, :], q_rows[:, p, bass.ds(b, 1), h, :].rearrange("r b q -> r (b q)"),
                                  k_rows[:, slot, 512 * c:512 * c + 512], start=not masked, stop=True)
                t.then_inc(scores_ready, 1)

            def turn_max(b, p):
                pe.wait_ge(split_step, 4 * (PAIRS * b + p) + 4)
                wait(pe, o_ready, PAIRS * b + p - 1)
                for h in range(2):
                    t = pe.matmul(ps[:, 6 + p % 2, 128 + P * h:128 + P * h + P], max_cols[:, p % 2, h, :],
                                  ident_bf[:, :], start=True, stop=True)
                t.then_inc(max_turned, 1)

            def keyscores(b, u, masked):
                p, c = divmod(u, CHUNKS)
                if c == 0:
                    pe.wait_ge(q_max_ready, PAIRS * b + p + 1)
                for half in range(2):
                    wait(pe, probs_ready, 2 * (UNITS * b + u) - 1 + half)
                    for j in (2 * half, 2 * half + 1):
                        dst = ps[:, 4 + half, 2 * P * (j % 2):2 * P * (j % 2) + 2 * P]
                        if masked:
                            for h in range(2):
                                mask_key(dst[:, P * h:P * h + P], c, j, j % 2 == 0 and h == 0)
                        at = 512 * c + P * j
                        t = pe.matmul(dst, k_rows[:, p % 4, at:at + P],
                                      q_max[:, p % 2, :, :].rearrange("r h q -> r (h q)"),
                                      start=not masked, stop=True, skip_group_check=masked)
                    t.then_inc(keyscores_ready, 1)

            def pv(b, u):
                p, c = divmod(u, CHUNKS)
                if c == 0:
                    pe.wait_ge(v_now_ready, PAIRS * b + p + 1)
                    wait(pe, o_ready, PAIRS * b + p - 1)
                    pe.wait_ge(q_max_ready, PAIRS * b + p + 1)
                pe.wait_ge(probs_ready, 2 * (UNITS * b + u) + 2)
                for j in range(4):
                    for h in range(2):
                        at = 32 * (2 * (j % 2) + h)
                        t = pe.matmul(ps[at:at + HEAD_COLS, 6 + p % 2, 0:P],
                                      v_now[:, p % 2, 4 * c + j, HEAD_COLS * h:HEAD_COLS * h + HEAD_COLS],
                                      probs[:, c, j // 2, P * (2 * (j % 2) + h):P * (2 * (j % 2) + h) + P],
                                      start=(c == 0 and j < 2), stop=(c == CHUNKS - 1 and j >= 2))
                t.then_inc(pv_done, 1)

            def turn_out(b, p):
                pe.wait_ge(oT_ready, PAIRS * b + p + 1)
                pe.matmul(ps[:, 6 + p % 2, 384:384 + 2 * HEAD_COLS], oT_sb[:, p % 2, :], gather[:, :],
                          start=True, stop=True).then_inc(o_turned, 1)

            def attend(masked):
                for u in range(2):
                    scores(0, u, masked)
                pe.wait_ge(once("ray_ready"), 4)
                pe.matmul(ps[:, 7, 0:4], ones[:, :], ray[:, :], start=True, stop=True
                          ).then_inc(once("ray_summed"), 1)
                for u in range(2, 6):
                    scores(0, u, masked)
                pe.wait_ge(once("ray_all_ready"), 1)
                pe.wait_ge(once("out_banks_zeroed"), 2)
                pe.wait_ge(v_ready, B * CHUNKS)
                turn_max(0, 0)
                for u in range(6, LEAD):
                    scores(0, u, masked)
                keyscores(0, 0, masked)

                def batch(b):
                    last = isinstance(b, int) and b == B - 1
                    first = isinstance(b, int) and b == 0
                    for u in range(UNITS):
                        p, c = divmod(u, CHUNKS)
                        if u + 1 < UNITS:
                            keyscores(b, u + 1, masked)
                        elif not last:
                            keyscores(b + 1, 0, masked)
                        if u + LEAD < UNITS:
                            scores(b, u + LEAD, masked)
                        elif not last:
                            scores(b + 1, u + LEAD - UNITS, masked)
                        if c == 0 and p > 0:
                            turn_out(b, p - 1)
                        elif c == 0 and not first:
                            turn_out(b - 1, PAIRS - 1)
                        pv(b, u)
                        if c == 1 and p + 1 < PAIRS:
                            turn_max(b, p + 1)
                        elif c == 1 and not last:
                            turn_max(b + 1, 0)
                loop_batches(pe, batch)
                turn_out(B - 1, PAIRS - 1)

            pe.wait_ge(k1_ready, B * CHUNKS)
            pe.wait_ge(r1_ready, B * CHUNKS)
            pe.wait_ge(once("mask_flag_ready"), 1)
            pe.wait_ge(once("ident_bf_ready"), 1)
            pe.wait_ge(ld["gather"], 16)
            pe.wait_ge(once("q_pads_ready"), 2)
            any_mask = pe.value_load(mask_flag[0:1, 0:1], min_val=0, max_val=1)
            with pe.If(any_mask > 0):
                attend(True)
            with pe.Else():
                attend(False)
            pe.wait_ge(o_ready, B * PAIRS)

            for b in range(B):
                t = turn(ps[:, 0, P * b:P * b + P], o_nat[:, b, :])
            t.then_inc(once("oN_turned"), 1)
            pe.wait_ge(once("oNT_ready"), 1)
            for b in range(B):
                t = pe.matmul(ps[:, 1, P * b:P * b + P], xnT[:, P * b:P * b + P], wT[:, W_O, :], start=True, stop=True)
            t.then_inc(once("attn_done"), 1)

            pe.wait_ge(once("ln2_ready"), B)
            for b in range(B):
                t = turn(ps[:, 2, P * b:P * b + P], xn[:, b, :])
            t.then_inc(once("ln2_turned"), 1)
            pe.wait_ge(once("ln2T_ready"), 1)
            for i, bank in ((W_P, 3), (W_P + 1, 4), (W_P + 2, 5), (W_IN, 6)):
                pe.matmul(ps[:, bank, :], wT[:, i, :], xnT[:, :], start=True, stop=True
                          ).then_inc(once("ssm_done"), 1)
            pe.wait_ge(once("yhat_ready"), 1)
            for b in range(B):
                t = pe.matmul(ps[:, 7, P * b:P * b + P], q_r1[:, P * b:P * b + P], wT[:, W_OUT, :],
                              start=True, stop=True)
            t.then_inc(once("y_done"), 1)

            pe.wait_ge(once("ln3_ready"), B)
            for b in range(B):
                t = turn(ps[:, 0, P * b:P * b + P], xn[:, b, :])
            t.then_inc(once("ln3_turned"), 1)
            pe.wait_ge(once("ln3T_ready"), 1)
            for i in range(HB):
                pe.matmul(ps[:, 1 + i, :], w1T[:, i, :], xnT[:, :], start=True, stop=True
                          ).then_inc(once("h_done"), 1)
            for i in range(HB):
                pe.wait_ge(once("gelu_ready"), i + 1)
                for b in range(B):
                    t = pe.matmul(ps[:, 5, P * b:P * b + P], probs[:, i, 0, P * b:P * b + P], w2T[:, i, :],
                                  start=(i == 0 and b == 0), stop=(i == HB - 1), skip_group_check=True)
            t.then_inc(once("mlp_done"), 1)

        @block.scalar
        def _(act):
            act.dma_start(ident[:, :], ident_in).then_inc(ld["ident"], 16)
            rows = lambda v: v.rearrange("(a p) -> a p", p=P)
            for v, at in ((bk, BK), (bq, BQ), (bv, BV), (alpha_log, ALPHA), (delta_bias, DBIAS), (bp, BP0), (b1, B1_0)):
                n = v.shape[0] // P
                act.dma_start(vec_nat[at:at + n, :], rows(v)).then_inc(ld["vec"], 16)

            def copy(dst, src, s, n=1):
                act.activation(dst, src, ACT.Copy).then_inc(s, n)

            act.wait_ge(once("kv_turned"), 1)
            copy(kvT[:, :, :].rearrange("p a d -> p (a d)"), ps[:, 1, 0:2 * P], once("vec_ready"))
            copy(vec[:, :], ps[:, 1, 2 * P:2 * P + VECS], once("kvT_ready"))

            def copy_ctx(b, c):
                n = 4 * b + c
                hold(act, ctx_turned, n + 1)
                hold(act, v_done, n - 1)
                copy(ctxT[:, c % 2, :], ps[:, 0, :], ctxT_ready)

            def first_k(b, c):
                hold(act, k_done, 4 * b + c + 1)
                act.activation(k_parts[:, 0, bass.ds(b * KEYS + 512 * c, 512)], ps[:, 2 + c % 2, :], ACT.Identity,
                               bias=vec[:, BK:BK + 1]).then_inc(k1_ready, 1)

            def second_k(b, c):
                hold(act, r1_ready, 4 * b + c + 1)
                copy(k_parts[:, 1, bass.ds(b * KEYS + 512 * c, 512)], k_r1[:, c % 2, :], k2_ready)

            def take_vall(b, c):
                hold(act, v_done, 4 * b + c + 1)
                dst = v_all[:, bass.ds(b * KT + 4 * c, 4), :].rearrange("p t (h m) -> p (t h) m", m=HEAD_COLS)
                copy(dst[:, :, 0:HD], ps[:, 4 + c % 2, :].rearrange("p (t m) -> p t m", m=HD), v_ready)

            def prep(b, extra):
                for c in range(CHUNKS):
                    copy_ctx(b, c)
                    extra(c)
                    if chunk_before(b, c, 2):
                        take_vall(*chunk_before(b, c, 2))
                    if chunk_before(b, c, 1):
                        first_k(*chunk_before(b, c, 1))
                    if chunk_before(b, c, 2):
                        second_k(*chunk_before(b, c, 2))

            def extra_first(c):
                if c == 1:
                    act.wait_ge(once("w_turned"), 1)
                    copy(wT[:, 0:4, :].rearrange("p a d -> p (a d)"), ps[:, 1, :], once("wT_ready"))
                elif c == 2:
                    act.wait_ge(once("w_turned"), 2)
                    copy(wT[:, 4:7, :].rearrange("p a d -> p (a d)"), ps[:, 1, 0:3 * P], once("wT_ready"))
                elif c == 3:
                    act.wait_ge(once("xn_turned"), 1)
                    copy(xnT[:, :], ps[:, 1, :], once("xnT_ready"))

            def extra_last(c):
                if c == 1:
                    act.wait_ge(once("w_bin_turned"), 1)
                    copy(w1T[:, :, :].rearrange("p a d -> p (a d)"), ps[:, 1, :], once("w1T_ready"))
                elif c == 2:
                    act.wait_ge(once("w_bin_turned"), 2)
                    copy(w2T[:, :, :].rearrange("p a d -> p (a d)"), ps[:, 1, :], once("w2T_ready"))

            prep(0, extra_first)
            with act.Fori(1, B - 1) as b:
                prep(b, lambda c: None)
            prep(B - 1, extra_last)
            first_k(B - 1, CHUNKS - 1)
            take_vall(B - 1, CHUNKS - 2)
            second_k(B - 1, CHUNKS - 2)
            take_vall(B - 1, CHUNKS - 1)
            second_k(B - 1, CHUNKS - 1)
            act.wait_ge(ld["log_gain"], 16)
            act.activation(sv[:, 0:1], vec[:, ALPHA:ALPHA + 1], ACT.Abs).then_inc(once("alpha_step"), 1)
            act.wait_ge(once("alpha_step"), 1)
            act.activation(sv[:, 1:2], sv[:, 0:1], ACT.Exp, scale=-1.0).then_inc(once("alpha_step"), 1)
            act.wait_ge(once("alpha_step"), 2)
            act.activation(sv[:, 2:3], sv[:, 1:2], ACT.Ln, bias=1.0).then_inc(once("alpha_step"), 1)
            act.activation(sv[:, 3:4], log_gain[:, :], ACT.Exp).then_inc(once("alpha_step"), 1)

            def exp_unit(b, u):
                c = u % CHUNKS
                for h in range(2):
                    hold(act, keyscores_ready, 2 * (UNITS * b + u) + h + 1)
                    if h == 0:
                        hold(act, pv_done, UNITS * b + u - 3)
                    act.activation(probs[:, c, h, :], ps[:, 4 + h, :], ACT.Exp).then_inc(probs_ready, 1)

            def copy_out(b, p):
                hold(act, pv_done, CHUNKS * (PAIRS * b + p) + CHUNKS)
                hold(act, o_turned, PAIRS * b + p - 1)
                copy(oT_sb[:, p % 2, :], ps[:, 6 + p % 2, 0:P], oT_ready)

            def batch(b):
                first = isinstance(b, int) and b == 0
                for u in range(UNITS):
                    exp_unit(b, u)
                    if u % CHUNKS == 0:
                        if u > 0:
                            copy_out(b, u // CHUNKS - 1)
                        elif not first:
                            copy_out(b - 1, PAIRS - 1)
            loop_batches(act, batch)
            copy_out(B - 1, PAIRS - 1)

            act.wait_ge(once("oN_turned"), 1)
            act.activation(xnT[:, :], ps[:, 0, :], ACT.Identity, bias=vec[:, BV:BV + 1]).then_inc(once("oNT_ready"), 1)
            act.wait_ge(once("ln2_turned"), 1)
            copy(xnT[:, :], ps[:, 2, :], once("ln2T_ready"))

            act.wait_ge(once("small_ready"), 2)
            act.wait_ge(once("ssm_done"), 1)
            act.activation(SP_ABS, ps[:, 3, :], ACT.Abs, bias=sv[:, 5:6]).then_inc(once("sp_step"), 1)
            act.wait_ge(once("sp_step"), 1)
            act.activation(SP_EXP, SP_ABS, ACT.Exp, scale=-1.0).then_inc(once("sp_step"), 1)
            act.wait_ge(once("sp_step"), 2)
            act.activation(SP_LN, SP_EXP, ACT.Ln, bias=1.0).then_inc(once("sp_step"), 1)
            act.wait_ge(once("ssm_done"), 3)
            act.activation(G_B, ps[:, 4, :], ACT.Tanh, bias=vec[:, BP0 + 1:BP0 + 2]).then_inc(once("tanh_ready"), 1)
            act.activation(G_C, ps[:, 5, :], ACT.Tanh, bias=vec[:, BP0 + 2:BP0 + 3]).then_inc(once("tanh_ready"), 1)
            act.wait_ge(once("tanh_ready"), 2)
            act.activation(G_R, G_B, ACT.Square).then_inc(once("r_ready"), 1)
            act.activation(G_CC, G_C, ACT.Square).then_inc(once("cc_ready"), 1)
            act.wait_ge(once("delta_ready"), 1)
            act.activation(G_A0, DELTA, ACT.Exp, scale=sv[:, 4:5]).then_inc(once("a0_ready"), 1)
            act.wait_ge(once("disc_ready"), 1)
            act.activation(G_D, G_D, ACT.Sqrt).then_inc(once("disc_root"), 1)
            act.wait_ge(once("lam_ready"), 1)
            act.activation(G_CC, G_P, ACT.Sqrt).then_inc(once("lam_root"), 1)
            act.wait_ge(once("ln3_turned"), 1)
            copy(xnT[:, :], ps[:, 0, :], once("ln3T_ready"))
            for i in range(HB):
                act.wait_ge(once("h_done"), i + 1)
                act.activation(probs[:, i, 0, :], ps[:, 1 + i, :], ACT.Gelu, bias=vec[:, B1_0 + i:B1_0 + i + 1]
                               ).then_inc(once("gelu_ready"), 1)

        @block.gpsimd
        def _(gp):
            gp.memset(ones[:, :], 1.0).then_inc(once("ones_ready"), 1)
            gp.memset(neg_half[:, :], -0.5).then_inc(once("half_ready"), 1)

            def root_inv(name):
                gp.wait_ge(once(name + "_var"), 1)
                gp.tensor_tensor(rstd[:, :], var_eps[:, :], neg_half[:, :], ALU.pow).then_inc(once(name + "_rstd"), 1)

            gp.dma_start(head_rows[:, :], head_rows_in).then_inc(ld["head_rows"], 16)
            spread = lambda v: v.rearrange("(a n) -> a n", a=1).broadcast_to((P, D))
            gp.dma_start(bo_rows[:, :], spread(bo)).then_inc(ld["rows"], 16)
            gp.dma_start(b2_rows[:, :], spread(b2)).then_inc(ld["rows"], 16)
            gp.dma_start(log_gain[:, :], log_gamma.broadcast_to((P, 1))).then_inc(ld["log_gain"], 16)
            gp.dma_start(gather[:, :], gather_in).then_inc(ld["gather"], 16)
            gp.memset(q_rows[:, :, :, :, :].rearrange("r p b h q -> r (p b h q)").bitcast(F32), 0.0
                      ).then_inc(once("q_pads_ready"), 1)
            gp.memset(select[:, :, :, :].rearrange("k s p m -> k (s p m)").bitcast(F32), 0.0).then_inc(once("select_step"), 1)
            gp.wait_ge(once("half_ready"), 1)
            root_inv("xn")
            gp.wait_ge(ld["ident"], 16)
            gp.wait_ge(once("select_step"), 1)
            for block, part in enumerate(Q_BLOCKS):
                gp.tensor_copy(select[:, part, :, 16 * block:16 * block + 16],
                               ident[:, :].rearrange("k (p r) -> k p r", r=16)).then_inc(once("select_ready"), 1)
            gp.memset(v_all[:, :, :].rearrange("p t (h m) -> p (t h) m", m=HEAD_COLS)[:, :, HD:HD + 1], 1.0
                      ).then_inc(once("v_ones_ready"), 1)
            gp.memset(max_cols[:, :, :, :], 0.0).then_inc(once("q_pads_ready"), 1)

            def third(b, c):
                n = 4 * b + c
                keys = bass.ds(b * KEYS + 512 * c, 512)
                hold(gp, k2_ready, n + 1)
                gp.tensor_tensor(k_parts[:, 2, keys], k_r1[:, c % 2, :], k_parts[:, 1, keys], ALU.subtract
                                 ).then_inc(k3_ready, 1)

            w_halves = ((slice(0, HB), w1_nat[:, :, :].rearrange("p a d -> p (a d)")), (slice(HB, 2 * HB), w2_nat[:, :]))
            flat = lambda t, sl: t[:, sl, :].rearrange("p a d -> p (a d)")

            def binarise(c, half):
                sl, nat = w_halves[half]
                step = once("w_bin_step")
                if c == 0:
                    gp.wait_ge(once("w_neg_ready"), 2)
                    gp.tensor_tensor(flat(w_sgn, sl), flat(w_sgn, sl), flat(w_bin, sl), ALU.subtract).then_inc(step, 1)
                elif c == 1:
                    gp.wait_ge(step, half + 1)
                    gp.wait_ge(once("w_abs_ready"), 2)
                    if half == 0:
                        a = w_abs[:, 0:HB].unsqueeze(2).broadcast_to((P, HB, D))
                    else:
                        a = w_abs[:, HB:HB + 1].unsqueeze(2).broadcast_to((P, HB, D))
                    gp.tensor_tensor(w_bin[:, sl, :], w_sgn[:, sl, :], a, ALU.mult).then_inc(step, 1)
                elif c == 2:
                    gp.wait_ge(step, 2 + half + 1)
                    gp.tensor_tensor(flat(w_bin, sl), flat(w_bin, sl), nat, ALU.subtract).then_inc(step, 1)
                else:
                    gp.wait_ge(step, 4 + half + 1)
                    gp.tensor_tensor(flat(w_bin, sl), flat(w_bin, sl), nat, ALU.add).then_inc(once("w_bin_ready"), 1)

            for c in range(CHUNKS):
                third(0, c)
                if c < 2:
                    for b in range(2 * c, 2 * c + 2):
                        gp.wait_ge(ld["rows"], 32)
                        gp.tensor_tensor(x_bo[:, b, :], x_sb[:, b, :], bo_rows[:, :], ALU.add
                                         ).then_inc(once("x_bo_ready"), 1)
            for c in range(CHUNKS):
                binarise(c, 0)
                third(1, c)
                binarise(c, 1)
            with gp.Fori(2, B) as b:
                for c in range(CHUNKS):
                    third(b, c)

            def take_v(b, p):
                hold(gp, pv_done, CHUNKS * (PAIRS * b + p - 1))
                gp.tensor_copy(v_now[:, p % 2, :, :],
                               v_all[:, bass.ds(b * KT, KT), 2 * HEAD_COLS * p:2 * HEAD_COLS * (p + 1)]
                               ).then_inc(v_now_ready, 1)

            def split_max(b, p):
                i = PAIRS * b + p
                nm, r1, cols_ = negmax[:, p % 2, :], nm_r1[:, p % 2, :], max_cols[:, p % 2, :, :]
                hold(gp, negmax_ready, i + 1)
                hold(gp, max_turned, i - 1)
                gp.tensor_copy(cols_[:, :, MAX_ROW], nm).then_inc(split_step, 1)
                hold(gp, split_step, 4 * i + 1)
                gp.tensor_tensor(r1, nm, cols_[:, :, MAX_ROW], ALU.subtract).then_inc(split_step, 1)
                hold(gp, split_step, 4 * i + 2)
                gp.tensor_copy(cols_[:, :, MAX_ROW + 1], r1).then_inc(split_step, 1)
                hold(gp, split_step, 4 * i + 3)
                gp.tensor_tensor(cols_[:, :, MAX_ROW + 2], r1, cols_[:, :, MAX_ROW + 1], ALU.subtract
                                 ).then_inc(split_step, 1)

            gp.wait_ge(v_ready, B * CHUNKS)
            gp.wait_ge(once("v_ones_ready"), 1)
            def batch(b):
                for p in range(PAIRS):
                    split_max(b, p)
                    take_v(b, p)
            gp.wait_ge(once("norm_step"), 2)
            gp.tensor_tensor(norm_inv[:, :], norm_inv[:, :], neg_half[:, 0:2], ALU.pow).then_inc(once("norm_ready"), 1)
            loop_batches(gp, batch)
            root_inv("ln2")
            root_inv("ln3")

        @block.vector
        def _(dve):
            def layernorm(src, name):
                s = once(name + "_step")
                for b in range(B):
                    dve.bn_stats(bn[:, b, :], src[:, b, :]).then_inc(s, 1)
                dve.wait_ge(s, B)
                for b in range(B):
                    dve.bn_aggr(mv[:, b, :], bn[:, b, :]).then_inc(s, 1)
                dve.wait_ge(s, 2 * B)
                dve.tensor_scalar(var_eps[:, :], mv[:, :, 1], LN_EPS, None, ALU.add).then_inc(once(name + "_var"), 1)
                dve.wait_ge(once(name + "_rstd"), 1)
                for b in range(B):
                    dve.tensor_scalar(xn[:, b, :], src[:, b, :], mv[:, b, 0:1], rstd[:, b:b + 1],
                                      ALU.subtract, ALU.mult).then_inc(once(name + "_ready"), 1)

            dve.memset(k_rows[:, :, :], 1.0).then_inc(once("k_pads_ready"), 1)
            dve.wait_ge(sq_done, 1)
            dve.tensor_copy(gram[:, :, :], ps[:, 6, 0:2 * P].rearrange("p (w d) -> p w d", w=2)
                            ).then_inc(once("gram_ready"), 1)
            dve.wait_ge(once("gram_ready"), 1)
            dve.tensor_copy(power[:, 0, :, :], gram[:, :, :]).then_inc(pow_ready, 1)

            def split_q():
                dve.wait_ge(once("q_done"), 1)
                dve.tensor_scalar(q32[:, :], ps[:, 1, :], vec[:, BQ:BQ + 1], 1.0 / math.sqrt(HD), ALU.add, ALU.mult
                                  ).then_inc(once("q_step"), 1)
                dve.wait_ge(once("q_step"), 1)
                dve.tensor_copy(q_parts[:, 0, :], q32[:, :]).then_inc(once("q_step"), 1)
                dve.wait_ge(once("q_step"), 2)
                dve.tensor_tensor(q_r1[:, :], q32[:, :], q_parts[:, 0, :], ALU.subtract).then_inc(once("q_step"), 1)
                dve.wait_ge(once("q_step"), 3)
                dve.tensor_copy(q_parts[:, 1, :], q_r1[:, :]).then_inc(once("q_step"), 1)
                dve.wait_ge(once("q_step"), 4)
                dve.wait_ge(once("select_ready"), len(Q_BLOCKS))
                dve.tensor_tensor(q_parts[:, 2, :], q_r1[:, :], q_parts[:, 1, :], ALU.subtract
                                  ).then_inc(once("q_bank_free"), 1)

            def weight_means():
                dve.wait_ge(ld["mlp"], 32)
                dve.tensor_reduce(w_abs[:, 0:HB], w1_nat[:, :, :], AX.X, ALU.add, apply_absolute_value=True
                                  ).then_inc(once("w_abs_step"), 1)
                dve.tensor_reduce(w_abs[:, HB:HB + 1], w2_nat[:, :], AX.X, ALU.add, apply_absolute_value=True
                                  ).then_inc(once("w_abs_step"), 1)
                flat = lambda t, half: t[:, HB * half:HB * half + HB, :].rearrange("p a d -> p (a d)")
                for half, nat in enumerate((w1_nat[:, :, :].rearrange("p a d -> p (a d)"), w2_nat[:, :])):
                    dve.tensor_scalar(flat(w_sgn, half), nat, 0.0, None, ALU.is_gt)
                    dve.tensor_scalar(flat(w_bin, half), nat, 0.0, None, ALU.is_lt).then_inc(once("w_neg_ready"), 1)
                dve.wait_ge(once("w_abs_step"), 2)
                dve.tensor_scalar(w_abs[:, 0:HB], w_abs[:, 0:HB], 1.0 / D, None, ALU.mult
                                  ).then_inc(once("w_abs_ready"), 1)
                dve.tensor_scalar(w_abs[:, HB:HB + 1], w_abs[:, HB:HB + 1], 1.0 / HID, None, ALU.mult
                                  ).then_inc(once("w_abs_ready"), 1)

            def mask_magnitude():
                dve.wait_ge(ld["mask"], 16)
                dve.tensor_reduce(mask_abs[:, :], mask_sb[:, :], AX.X, ALU.max, apply_absolute_value=True
                                  ).then_inc(once("mask_abs_ready"), 1)

            def flag_mask():
                dve.wait_ge(once("mask_turned"), 1)
                dve.tensor_reduce(mask_flag_f[:, :], ps[0:1, 1, 0:P], AX.X, ALU.max).then_inc(once("flag_step"), 1)
                dve.wait_ge(once("flag_step"), 1)
                dve.tensor_scalar(mask_flag[:, :], mask_flag_f[:, :], 0.0, None, ALU.is_gt
                                  ).then_inc(once("mask_flag_ready"), 1)

            def rest_k(b, c):
                n = 4 * b + c
                keys = bass.ds(b * KEYS + 512 * c, 512)
                dve.wait_ge(k1_ready, n + 1)
                wait(dve, k3_ready, n - 1)
                wait(dve, k2_ready, n - 1)
                dve.scalar_tensor_tensor(k_r1[:, c % 2, :], ps[:, 2 + c % 2, :], vec[:, BK:BK + 1],
                                         k_parts[:, 0, keys], ALU.add, ALU.subtract).then_inc(r1_ready, 1)

            def sum_squares(slot):
                for w in range(2):
                    dve.tensor_tensor_reduce(sq_junk[:, w, :], power[:, slot, w, :], power[:, slot, w, :],
                                             1.0, 0.0, ALU.mult, ALU.add, fro[:, w:w + 1]).then_inc(fro_ready, 1)

            def next_power(b, at):
                k, norms = 6 * b + at, 2 * b + at // SQ_PERIOD
                dve.wait_ge(pow_ready, k + 1)
                if at % SQ_PERIOD == 0:
                    dve.wait_ge(fro_summed, norms + 1)
                    dve.tensor_scalar(fro_inv[:, :], ps[:, 7, 0:2], TINY, None, ALU.max).then_inc(fro_inv_ready, 1)
                    dve.wait_ge(fro_inv_ready, 2 * norms + 1)
                    dve.reciprocal(fro_inv[:, :], fro_inv[:, :]).then_inc(fro_inv_ready, 1)
                    dve.wait_ge(fro_inv_ready, 2 * norms + 2)
                    dve.wait_ge(sq_done, k + 2)
                    for w in range(2):
                        t = dve.tensor_scalar(power[:, (at + 1) % 2, w, :], ps[:, 6, P * w:P * w + P],
                                              fro_inv[:, w:w + 1], None, ALU.mult)
                        if w == 0:
                            t.then_inc(once("pow_half"), 1)
                    t.then_inc(pow_ready, 1)
                else:
                    dve.wait_ge(sq_done, k + 2)
                    dve.tensor_copy(power[:, (at + 1) % 2, :, :],
                                    ps[:, 6, 0:2 * P].rearrange("p (w d) -> p w d", w=2)).then_inc(pow_ready, 1)
                if (at + 1) % SQ_PERIOD == 0:
                    dve.wait_ge(pow_ready, k + 2)
                    sum_squares((at + 1) % 2)

            def spread_q(b, c):
                pair = CHUNKS * (b - 1) + c
                dve.wait_ge(once("q_placed"), pair + 1)
                for h in range(2):
                    dve.tensor_scalar(q_rows[0:MAX_ROW, bass.ds(pair, 1), :, h, :].rearrange("r p b q -> r (p b) q"),
                                      ps[0:MAX_ROW, 1, :].rearrange("r (b q) -> r b q", b=B),
                                      head_rows[0:MAX_ROW, h:h + 1], None, ALU.mult).then_inc(once("q_bank_free"), 1)

            def prep(b, extra):
                at = 0
                for c in range(CHUNKS):
                    next_power(b, at)
                    at += 1
                    if c % 2 == 1:
                        next_power(b, at)
                        at += 1
                    if chunk_before(b, c, 1):
                        rest_k(*chunk_before(b, c, 1))
                    extra(b, c)

            def extra_first(b, c):
                if c == 0:
                    dve.wait_ge(ld["x"], 16)
                    layernorm(x_sb, "xn")
                elif c == 1:
                    dve.wait_ge(ld["ident"], 16)
                    dve.tensor_copy(ident_bf[:, :], ident[:, :]).then_inc(once("ident_bf_ready"), 1)
                elif c == 2:
                    weight_means()
                else:
                    split_q()

            def extra_last(b, c):
                if c == 1:
                    mask_magnitude()
                elif c == 3:
                    flag_mask()

            dve.wait_ge(pow_ready, 1)
            sum_squares(0)
            dve.wait_ge(ld["head_rows"], 16)
            dve.wait_ge(once("q_pads_ready"), 1)
            prep(0, extra_first)
            with dve.Fori(1, B - 1) as b:
                prep(b, spread_q)
            prep(B - 1, extra_last)
            rest_k(B - 1, CHUNKS - 1)
            dve.wait_ge(once("ray_done"), 1)
            for w in range(2):
                dve.tensor_tensor_reduce(sq_junk[:, w, :], ps[:, 6, P * w:P * w + P], power[:, 0, w, :],
                                         1.0, 0.0, ALU.mult, ALU.add, ray[:, w:w + 1]).then_inc(once("ray_ready"), 1)
            dve.wait_ge(once("ray_ready"), 2)
            for w in range(2):
                dve.tensor_tensor_reduce(sq_junk[:, w, :], power[:, 0, w, :], power[:, 0, w, :],
                                         1.0, 0.0, ALU.mult, ALU.add, ray[:, 2 + w:3 + w]
                                         ).then_inc(once("ray_ready"), 1)
            dve.wait_ge(once("ray_summed"), 1)
            dve.tensor_scalar(ray_all[:, :], ps[:, 7, 0:4], TINY, None, ALU.max).then_inc(once("ray_all_ready"), 1)
            dve.wait_ge(once("ray_all_ready"), 1)
            dve.reciprocal(fro_inv[:, :], ray_all[:, 2:4]).then_inc(once("ray_inv"), 1)
            dve.wait_ge(once("ray_inv"), 1)
            dve.tensor_tensor(norm_inv[:, :], ray_all[:, 0:2], fro_inv[:, :], ALU.mult).then_inc(once("norm_step"), 1)
            dve.wait_ge(once("norm_step"), 1)
            dve.tensor_scalar(norm_inv[:, :], norm_inv[:, :], 1.0, None, ALU.max).then_inc(once("norm_step"), 1)
            for i in range(2):
                dve.memset(ps[:, 6 + i, 0:P], 0.0).then_inc(once("out_banks_zeroed"), 1)

            def max_unit(b, u):
                p, c = divmod(u, CHUNKS)
                dve.wait_ge(scores_ready, UNITS * b + u + 1)
                if c == 0:
                    wait(dve, negmax_ready, PAIRS * b + p - 1)
                bank = 2 * (u % 2)
                dve.tensor_reduce(pmax[:, p % 2, :, c], ps[:, bank:bank + 2, :], AX.X, ALU.max
                                  ).then_inc(pmax_ready, 1)

            def neg_max(b, p):
                i = PAIRS * b + p
                dve.wait_ge(pmax_ready, CHUNKS * i + CHUNKS)
                wait(dve, split_step, 4 * (i - 1))
                dve.tensor_reduce(negmax[:, p % 2, :], pmax[:, p % 2, :, :], AX.X, ALU.max, negate=True
                                  ).then_inc(negmax_ready, 1)

            def add_max(b, p):
                dve.wait_ge(max_turned, PAIRS * b + p + 1)
                wait(dve, keyscores_ready, 2 * CHUNKS * (PAIRS * b + p - 1))
                dve.tensor_tensor(q_max[:, p % 2, :, :],
                                  ps[:, 6 + p % 2, 128:384].rearrange("r (h q) -> r h q", h=2),
                                  q_rows[:, p, bass.ds(b, 1), :, :].rearrange("r b h q -> r (b h) q"), ALU.add).then_inc(q_max_ready, 1)

            def out_of(p):
                return ps[:, 6 + p % 2, 384:384 + 2 * HEAD_COLS].rearrange("q (h m) -> q h m", h=2)

            def invert(b, p):
                dve.wait_ge(o_turned, PAIRS * b + p + 1)
                wait(dve, o_ready, PAIRS * b + p - 1)
                dve.reciprocal(rden[:, p % 2, :], out_of(p)[:, :, HD]).then_inc(rden_ready, 1)

            def normalise(b, p):
                i, o = PAIRS * b + p, out_of(p)
                dve.wait_ge(rden_ready, i + 1)
                dve.tensor_tensor(o_nat[:, bass.ds(b, 1), 16 * p:16 * p + 16].rearrange("q b (h m) -> q (b h) m", h=2),
                                  o[:, :, 0:HD], rden[:, p % 2, :].unsqueeze(2).broadcast_to((P, 2, HD)), ALU.mult
                                  ).then_inc(o_ready, 1)

            def before(b, p, lag):
                if p >= lag:
                    return b, p - lag
                if isinstance(b, int) and b == 0:
                    return None
                return b - 1, p - lag + PAIRS

            def batch(b):
                for u in range(UNITS):
                    p, c = divmod(u, CHUNKS)
                    max_unit(b, u)
                    if c == CHUNKS - 1:
                        neg_max(b, p)
                    if c == 0 and before(b, p, 3):
                        invert(*before(b, p, 3))
                    if c == 0 and before(b, p, 3):
                        normalise(*before(b, p, 3))
                    if c == 1 and before(b, p, 1):
                        add_max(*before(b, p, 1))
            loop_batches(dve, batch)
            for p in range(PAIRS - 3, PAIRS):
                invert(B - 1, p)
                normalise(B - 1, p)
                if p == PAIRS - 3:
                    add_max(B - 1, PAIRS - 1)

            tail = once("tail_step")
            steps = [0]

            def step(t, wait_for=True):
                t.then_inc(tail, 1)
                steps[0] += 1
                if wait_for:
                    dve.wait_ge(tail, steps[0])

            dve.tensor_scalar(sv[:, 6:7], vec[:, ALPHA:ALPHA + 1], 0.0, sv[:, 2:3], ALU.max, ALU.add
                              ).then_inc(once("small_step"), 1)
            dve.wait_ge(once("small_step"), 1)
            dve.tensor_scalar(sv[:, 4:5], sv[:, 6:7], -1.0, None, ALU.mult).then_inc(once("small_ready"), 1)
            dve.tensor_tensor(sv[:, 5:6], vec[:, BP0:BP0 + 1], vec[:, DBIAS:DBIAS + 1], ALU.add
                              ).then_inc(once("small_ready"), 1)
            dve.wait_ge(once("norm_ready"), 1)
            step(dve.tensor_tensor(sv[:, 7:8], sv[:, 3:4], norm_inv[:, 0:1], ALU.mult))
            flat_bd = lambda t: t[:, :, :].rearrange("p b d -> p (b d)")
            dve.wait_ge(once("attn_done"), 1)
            dve.wait_ge(once("x_bo_ready"), B)
            step(dve.tensor_tensor(flat_bd(x_sb), ps[:, 1, :], flat_bd(x_bo), ALU.add))
            layernorm(x_sb, "ln2")
            dve.wait_ge(once("ssm_done"), 4)
            dve.wait_ge(once("sp_step"), 3)
            step(dve.tensor_scalar(DELTA, ps[:, 3, :], sv[:, 5:6], 0.0, ALU.add, ALU.max))
            dve.tensor_tensor(DELTA, DELTA, SP_LN, ALU.add).then_inc(once("delta_ready"), 1)
            step(dve.tensor_scalar(U_S, ps[:, 6, :], sv[:, 7:8], None, ALU.mult))
            dve.wait_ge(once("tanh_ready"), 2)
            step(dve.tensor_tensor(U_S, U_S, G_B, ALU.mult))
            dve.wait_ge(once("a0_ready"), 1)
            step(dve.tensor_scalar(G_A, G_A0, 1.0 - EPS_A, None, ALU.min))
            step(dve.tensor_tensor(G_Q, G_A, G_B, ALU.mult), False)
            step(dve.tensor_tensor(G_P, G_A, G_A, ALU.mult))
            dve.wait_ge(once("cc_ready"), 1)
            step(dve.tensor_tensor(G_P, G_P, G_CC, ALU.add))
            dve.wait_ge(once("r_ready"), 1)
            step(dve.tensor_tensor(G_D, G_P, G_R, ALU.subtract), False)
            step(dve.tensor_tensor(G_P, G_P, G_R, ALU.add))
            step(dve.tensor_tensor(G_D, G_D, G_D, ALU.mult), False)
            step(dve.scalar_tensor_tensor(G_Q, G_Q, 4.0, G_Q, ALU.mult, ALU.mult))
            dve.scalar_tensor_tensor(G_D, G_D, EPS, G_Q, ALU.add, ALU.add).then_inc(once("disc_ready"), 1)
            dve.wait_ge(once("disc_root"), 1)
            step(dve.tensor_tensor(G_P, G_P, G_D, ALU.add))
            step(dve.tensor_scalar(G_P, G_P, 0.5, EPS, ALU.mult, ALU.add))
            dve.tensor_scalar(G_P, G_P, 1.0, None, ALU.max).then_inc(once("lam_ready"), 1)
            dve.wait_ge(once("lam_root"), 1)
            step(dve.reciprocal(G_P, G_CC))
            step(dve.tensor_tensor(G_A, G_A, G_P, ALU.mult), False)
            step(dve.tensor_tensor(U_S, U_S, G_P, ALU.mult), False)
            step(dve.tensor_tensor(G_CS, G_C, G_P, ALU.mult))
            for b in range(B):
                t = slice(T * b, T * b + T)
                step(dve.tensor_tensor_scan(STATE[:, t], G_A[:, t], U_S[:, t], 0.0, ALU.mult, ALU.add), False)
            step(dve.memset(q_r1[:, :].rearrange("p (b t) -> p b t", b=B)[:, :, 0:1], 0.0))
            by_t = lambda a: a.rearrange("p (b t) -> p b t", b=B)
            dve.tensor_tensor(by_t(q_r1[:, :])[:, :, 1:T], by_t(G_CS)[:, :, 1:T], by_t(STATE)[:, :, 0:T - 1],
                              ALU.mult).then_inc(once("yhat_ready"), 1)
            dve.wait_ge(once("y_done"), 1)
            step(dve.scalar_tensor_tensor(flat_bd(x_sb), ps[:, 7, :], norm_inv[:, 1:2], flat_bd(x_sb),
                                          ALU.mult, ALU.add))
            layernorm(x_sb, "ln3")
            for b in range(B):
                step(dve.tensor_tensor(x_bo[:, b, :], x_sb[:, b, :], b2_rows[:, :], ALU.add), b == B - 1)
            dve.wait_ge(once("mlp_done"), 1)
            dve.wait_ge(once("ln3_turned"), 1)
            dve.tensor_tensor(flat_bd(xn), ps[:, 5, :], flat_bd(x_bo), ALU.add).then_inc(once("out_ready"), 1)


_INS = ['x', 'ctx_1024', 'mask_1x1xSxS2_ff0', 'L0_xattn_Wq', 'L0_xattn_bq', 'L0_xattn_Wk', 'L0_xattn_bk',
        'L0_xattn_Wv', 'L0_xattn_bv', 'L0_xattn_Wo', 'L0_xattn_bo', 'L0_attn_W_in', 'L0_attn_W_out', 'L0_attn_Wp',
        'L0_attn_bp', 'L0_attn_alpha_log', 'L0_attn_delta_bias', 'L0_attn_log_gamma', 'L0_ffn_w1', 'L0_ffn_b1',
        'L0_ffn_w2', 'L0_ffn_b2']


def kernel(**inputs):
    import numpy as _np
    import concourse.bacc as _bacc
    from concourse import mybir as _mybir
    from concourse.bass_utils import run_bass_kernel_spmd as _run

    gather = _np.zeros((P, 2 * HEAD_COLS), _np.float32)
    for tile in range(4):
        for m in range(HEAD_COLS):
            gather[32 * tile + m, HEAD_COLS * (tile % 2) + m] = 1.0
    head_rows = (_np.arange(P)[:, None] // 8 % 2 == _np.arange(2)[None, :]).astype(_np.float32)
    consts = {"ident": _np.eye(P, dtype=_np.float32), "gather": gather, "head_rows": head_rows}

    nc = _bacc.Bacc("TRN2", target_bir_lowering=False, num_devices=1)
    arrays, args = {}, []
    for name in _INS + list(consts):
        a = _np.ascontiguousarray(consts[name] if name in consts else inputs[name])
        if a.ndim == 0:
            a = a.reshape(1)
        arrays[f"in_{name}_dram"] = a
        args.append(nc.dram_tensor(f"in_{name}_dram", a.shape, _mybir.dt.from_np(a.dtype),
                                   kind="ExternalInput").ap())
    args.append(nc.dram_tensor("out_0_dram", (4, 128, 128), _mybir.dt.float32, kind="ExternalOutput").ap())
    perceiver_block(nc, *args)
    r = _run(nc, [arrays], core_ids=[0])
    return r.results[0]["out_0_dram"]
```

```python
import concourse.bass as bass
from concourse import mybir
from contextlib import ExitStack
import math

F32 = mybir.dt.float32
BF16 = mybir.dt.bfloat16
I32 = mybir.dt.int32
ALU = mybir.AluOpType
ACT = mybir.ActivationFunctionType
AX = mybir.AxisListType

P = 128
HEAD_COLS = 9
SQUARINGS = 24
SQ_PERIOD = 3
TINY = 1e-30
LN_EPS = 1e-5
EPS = 1e-12
EPS_A = 1e-4


def perceiver_block(nc, x, ctx_in, mask, Wq, bq, Wk, bk, Wv, bv, Wo, bo, W_in, W_out, Wp, bp,
                    alpha_log, delta_bias, log_gamma, w1, b1, w2, b2, ident_in, gather_in, head_rows_in, out):
    B, T, D = x.shape
    KEYS = ctx_in.shape[1]
    HEADS = 16
    HD = D // HEADS
    PAIRS = HEADS // 2
    CHUNKS = KEYS // 512
    KT = KEYS // P
    HID = w1.shape[0]
    HB = HID // P
    TOK = B * T
    UNITS = PAIRS * CHUNKS
    LEAD = 8
    assert (T, D, CHUNKS, B, HD) == (128, 128, 4, 4, 8)
    K_BLOCKS = (0, 1, 2, 0, 1, 0)
    Q_BLOCKS = (0, 0, 0, 1, 1, 2)
    MAX_ROW = 16 * len(Q_BLOCKS)
    BK, BQ, BV, ALPHA, DBIAS, BP0, B1_0, VECS = 0, 1, 2, 3, 4, 5, 8, 12

    ctx = ExitStack()
    with ctx:
        def sb(name, shape, dt=F32):
            return ctx.enter_context(nc.sbuf_tensor(name, shape, dt))

        sems = {}

        def sem(name):
            sems[name] = ctx.enter_context(nc.semaphore(name))
            return sems[name]

        ident = sb("ident", [P, P])
        ident_bf = sb("ident_bf", [P, P], BF16)
        head_rows = sb("head_rows", [P, 2])
        gather = sb("gather", [P, 2 * HEAD_COLS])
        ones = sb("ones", [P, P])
        x_sb = sb("x_sb", [P, B, D])
        w_kv = sb("w_kv", [P, 2, D])
        w_nat = sb("w_nat", [P, 7, D])
        w1_nat = sb("w1_nat", [P, HB, D])
        w2_nat = sb("w2_nat", [P, HID])
        kvT = sb("kvT", [P, 2, D])
        wT = sb("wT", [P, 7, D])
        W_IN, W_OUT, W_Q, W_O, W_P = 0, 1, 2, 3, 4
        w1T = sb("w1T", [P, HB, P])
        w2T = sb("w2T", [P, HB, D])
        vec_nat = sb("vec_nat", [VECS, P])
        vec = sb("vec", [P, VECS])
        log_gain = sb("log_gain", [P, 1])
        bo_rows = sb("bo_rows", [P, D])
        b2_rows = sb("b2_rows", [P, D])
        x_bo = sb("x_bo", [P, B, D])
        bn = sb("bn", [P, B, 6])
        mv = sb("mv", [P, B, 2])
        var_eps = sb("var_eps", [P, B])
        rstd = sb("rstd", [P, B])
        neg_half = sb("neg_half", [P, B])
        xn = sb("xn", [P, B, D])
        xnT = sb("xnT", [P, TOK])
        q32 = sb("q32", [P, TOK])
        q_r1 = sb("q_r1", [P, TOK])
        q_parts = sb("q_parts", [P, 3, TOK], BF16)
        q_rows = sb("q_rows", [P, PAIRS, B, 2, T], BF16)
        ctx_buf = sb("ctx_buf", [P, CHUNKS, 4, D])
        ctxT = sb("ctxT", [P, 2, 512])
        k_parts = sb("k_parts", [P, 3, B * KEYS], BF16)
        k_r1 = sb("k_r1", [P, 2, 512])
        v_all = sb("v_all", [P, B * KT, HEADS * HEAD_COLS])
        k_rows = sb("k_rows", [P, 4, KEYS], BF16)
        q_max = sb("q_max", [P, 2, 2, T], BF16)
        v_now = sb("v_now", [P, 2, KT, 2 * HEAD_COLS])
        pmax = sb("pmax", [P, 2, 2, CHUNKS])
        negmax = sb("negmax", [P, 2, 2])
        nm_r1 = sb("nm_r1", [P, 2, 2])
        max_cols = sb("max_cols", [P, 2, 2, P], BF16)
        probs = sb("probs", [P, 4, 2, 512])
        oT_sb = sb("oT_sb", [P, 2, P])
        rden = sb("rden", [P, 2, 2])
        o_nat = w1_nat
        mask_sb = sb("mask_sb", [P, KEYS])
        mask_abs = sb("mask_abs", [P, 3])
        mask_flag_f = sb("mask_flag_f", [1, 1])
        mask_flag = sb("mask_flag", [1, 1], I32)
        gram = sb("gram", [P, 2, P])
        power = sb("power", [P, 2, 2, P])
        sq_junk = sb("sq_junk", [P, 2, P])
        fro = sb("fro", [P, 2])
        fro_inv = sb("fro_inv", [P, 2])
        ray = sb("ray", [P, 4])
        norm_inv = sb("norm_inv", [P, 2])
        ray_all = sb("ray_all", [P, 4])
        sv = sb("sv", [P, 12])
        w_abs = sb("w_abs", [P, HB + 1])

        ps = ctx.enter_context(nc.psum_tensor("ps", [P, 8, 512], F32))

        q_both = probs[:, 0:2, :, :].rearrange("p a b n -> p (a b n)").bitcast(BF16).rearrange(
            "p (i n) -> p i n", n=TOK)
        w_sgn = probs[:, 2, :, :].rearrange("p b (i n) -> p (b i) n", n=P)
        w_bin = probs[:, 3, :, :].rearrange("p b (i n) -> p (b i) n", n=P)
        gates = k_parts[:, :, :].rearrange("p a n -> p (a n)")[:, 0:18 * 2 * TOK].bitcast(F32).rearrange(
            "p (i n) -> p i n", n=TOK)
        (SP_ABS, SP_EXP, SP_LN, G_B, G_C, G_R, G_CC, G_A0, DELTA, U_S, G_A, G_Q, G_P, G_D, G_CS, G_S, G_L, G_INV
         ) = (gates[:, i, :] for i in range(18))
        STATE = q32[:, :]

        q_dram = nc.dram_tensor("q_parts_dram", (P, 3, TOK), BF16, kind="Internal").ap()

        ld = {n: sem("ld_" + n) for n in ("ident", "x", "kv", "vec_qk", "vec", "ssm", "w", "wp", "head_rows", "mlp",
                                          "mask", "rows", "gather", "log_gain")}
        ctx_loaded = [sem(f"ctx_loaded{c}") for c in range(CHUNKS)]
        ctx_turned = sem("ctx_turned")
        ctxT_ready = sem("ctxT_ready")
        k_done = sem("k_done")
        v_done = sem("v_done")
        k1_ready = sem("k1_ready")
        r1_ready = sem("r1_ready")
        k2_ready = sem("k2_ready")
        k3_ready = sem("k3_ready")
        v_ready = sem("v_ready")
        sq_done = sem("sq_done")
        pow_ready = sem("pow_ready")
        fro_ready = sem("fro_ready")
        fro_summed = sem("fro_summed")
        fro_inv_ready = sem("fro_inv_ready")
        k_rows_loaded = [sem(f"k_rows_loaded{s}") for s in range(4)]
        v_now_ready = sem("v_now_ready")
        scores_ready = sem("scores_ready")
        pmax_ready = sem("pmax_ready")
        negmax_ready = sem("negmax_ready")
        split_step = sem("split_step")
        max_turned = sem("max_turned")
        q_max_ready = sem("q_max_ready")
        keyscores_ready = sem("keyscores_ready")
        probs_ready = sem("probs_ready")
        pv_done = sem("pv_done")
        oT_ready = sem("oT_ready")
        o_turned = sem("o_turned")
        rden_ready = sem("rden_ready")
        o_ready = sem("o_ready")
        stored = sem("stored")

        def once(name):
            return sems[name] if name in sems else sem(name)

        def wait(eng, s, value):
            if isinstance(value, int) and value <= 0:
                return
            eng.wait_ge(s, value)

        def hold(eng, s, value):
            wait(eng, s, value)
            if not isinstance(value, int):
                eng.sem_inc(once("passed_a_hold"))

        def chunk_before(b, c, lag):
            if c >= lag:
                return b, c - lag
            return None if isinstance(b, int) and b == 0 else (b - 1, c - lag + CHUNKS)

        def loop_batches(eng, body):
            body(0)
            with eng.Fori(1, B - 1) as b:
                body(b)
            body(B - 1)

        HALF = TOK // 2
        halves = (range(0, B // 2), range(B // 2, B))
        TURN, PROJ = 2, 1
        RAW_DELTA, RAW_BC, RAW_U = 3, 0, 1
        Y, HIDDEN, OUT = 3, 0, 3

        def bank(h, i):
            return ps[:, 4 * h + i, :]

        def cols(h):
            return slice(HALF * h, HALF * h + HALF)

        block = ctx.enter_context(nc.Block())

        @block.sync
        def _(sp):
            def load_ctx(b, c):
                if not isinstance(b, int) or b > 0:
                    wait(sp, ctx_turned, 4 * (b - 1) + c + 1)
                sp.dma_start(ctx_buf[:, c, :, :],
                             ctx_in[bass.ds(b, 1), 512 * c:512 * c + 512, :].rearrange(
                                 "b (p j) d -> p (b j) d", j=4)).then_inc(ctx_loaded[c], 16)

            sp.dma_start(w_kv[:, 0, :], Wk).then_inc(ld["kv"], 16)
            load_ctx(0, 0)
            sp.dma_start(w_kv[:, 1, :], Wv).then_inc(ld["kv"], 16)
            sp.dma_start(w_nat[:, W_IN, :], W_in).then_inc(ld["ssm"], 16)
            sp.dma_start(w_nat[:, W_OUT, :], W_out).then_inc(ld["ssm"], 16)
            load_ctx(0, 1)
            sp.dma_start(x_sb[:, :, :], x.rearrange("b t d -> t b d")).then_inc(ld["x"], 16)
            sp.dma_start(w_nat[:, W_Q, :], Wq).then_inc(ld["w"], 16)
            sp.dma_start(w_nat[:, W_O, :], Wo).then_inc(ld["w"], 16)
            load_ctx(0, 2)
            load_ctx(0, 3)
            for v, at in ((bv, BV), (alpha_log, ALPHA), (delta_bias, DBIAS), (bp, BP0), (b1, B1_0)):
                n = v.shape[0] // P
                sp.dma_start(vec_nat[at:at + n, :], v.rearrange("(a p) -> a p", p=P)).then_inc(ld["vec"], 16)
            sp.dma_start(w_nat[:, W_P:W_P + 3, :], Wp.rearrange("(a p) d -> p a d", p=P)).then_inc(ld["wp"], 16)
            load_ctx(1, 0)
            sp.dma_start(w1_nat[:, :, :], w1.rearrange("(a p) d -> p a d", p=P)).then_inc(ld["mlp"], 16)
            sp.dma_start(w2_nat[:, :], w2).then_inc(ld["mlp"], 16)

            def load_pair(b, p, blocks=range(len(K_BLOCKS))):
                slot = p % 4
                wait(sp, keyscores_ready, 2 * CHUNKS * (PAIRS * b + p - 3))
                for block in blocks:
                    part = K_BLOCKS[block]
                    sp.dma_start(k_rows[16 * block:16 * block + 16, slot, :],
                                 k_parts[16 * p:16 * p + 16, part, bass.ds(b * KEYS, KEYS)]
                                 ).then_inc(k_rows_loaded[slot], 16)

            for c in range(1, CHUNKS):
                load_ctx(1, c)
            sp.dma_start(mask_sb[:, :], mask.rearrange("a b q k -> (a b q) k")).then_inc(ld["mask"], 16)
            load_ctx(2, 0)
            sp.wait_ge(once("q_parts_ready"), 1)
            sp.dma_start(q_dram, q_parts[:, :, :]).then_inc(once("q_stored"), 16)
            load_ctx(2, 1)
            sp.wait_ge(once("q_stored"), 16)
            for block, part in enumerate(Q_BLOCKS):
                sp.dma_start(q_both[16 * block:16 * block + 16, :, :],
                             q_dram[:, part, :].rearrange("(p r) n -> r p n", r=16)).then_inc(once("q_loaded"), 16)
            sp.wait_ge(once("k_pads_ready"), 1)
            sp.dma_start(k_rows[MAX_ROW:P, 2:4, :], k_rows[MAX_ROW:P, 0:2, :]).then_inc(once("k_pads_copied"), 16)
            half = len(K_BLOCKS) // 2
            sp.wait_ge(k3_ready, CHUNKS)
            for i in range(2 * CHUNKS):
                if i > 1:
                    load_ctx(2 + i // CHUNKS, i % CHUNKS)
                load_pair(0, i // 2, range(half * (i % 2), half * (i % 2) + half))

            def pairs(b, first=0):
                sp.wait_ge(k3_ready, CHUNKS * b + CHUNKS)
                for p in range(first, PAIRS):
                    load_pair(b, p)
            pairs(0, 4)
            with sp.Fori(1, B) as b:
                pairs(b)

            for h in range(2):
                sp.wait_ge(once("out_ready"), h + 1)
                sp.dma_start(out[2 * h:2 * h + 2, :, :].rearrange("b t d -> t b d"), xn[:, 2 * h:2 * h + 2, :]
                             ).then_inc(stored, 16)
            sp.wait_ge(stored, 32)

        @block.tensor
        def _(pe):
            pe.wait_ge(ld["ident"], 16)

            def turn(dst, src):
                return pe.transpose(dst, src, ident[:, :])

            pe.wait_ge(ld["kv"], 32)
            for i in range(2):
                turn(ps[:, 1, P * i:P * i + P], w_kv[:, i, :])
            pe.wait_ge(ld["vec_qk"], 32)
            pe.transpose(ps[:, 1, 2 * P:2 * P + 2], vec_nat[0:2, :], ident[0:2, 0:2]).then_inc(once("kv_turned"), 1)

            def turn_ctx(b, c):
                n = 4 * b + c
                wait(pe, ctxT_ready, n)
                pe.wait_ge(ctx_loaded[c], 16 * b + 16)
                for j in range(4):
                    t = turn(ps[:, 0, P * j:P * j + P], ctx_buf[:, c, j, :])
                t.then_inc(ctx_turned, 1)

            def project_k(b, c):
                n = 4 * b + c
                pe.wait_ge(ctxT_ready, n + 1)
                wait(pe, k1_ready, n - 1)
                wait(pe, r1_ready, n - 1)
                pe.matmul(ps[:, 2 + c % 2, :], kvT[:, 0, :], ctxT[:, c % 2, :], start=True, stop=True
                          ).then_inc(k_done, 1)

            def project_v(b, c):
                wait(pe, v_ready, 4 * b + c - 1)
                for j in range(4):
                    t = pe.matmul(ps[:, 4 + c % 2, P * j:P * j + P], ctxT[:, c % 2, P * j:P * j + P], kvT[:, 1, :],
                                  start=True, stop=True)
                t.then_inc(v_done, 1)

            def square(b, at):
                k, norms = 6 * b + at, 2 * b + at // SQ_PERIOD
                if at % SQ_PERIOD == 0:
                    pe.wait_ge(fro_ready, 2 * norms + 2)
                    pe.matmul(ps[:, 7, 0:2], ones[:, :], fro[:, :], start=True, stop=True
                              ).then_inc(fro_summed, 1)
                pe.wait_ge(pow_ready, k + 1)
                for w in range(2):
                    t = pe.matmul(ps[:, 6, P * w:P * w + P], power[:, at % 2, w, :], power[:, at % 2, w, :],
                                  start=True, stop=True)
                t.then_inc(sq_done, 1)

            def turn_weights(first, n, s):
                for i in range(n):
                    t = turn(ps[:, 1, P * i:P * i + P], w_nat[:, first + i, :])
                t.then_inc(s, 1)

            def prep(b, extra):
                at = 0
                for c in range(CHUNKS):
                    last = chunk_before(b, c, 1)
                    turn_ctx(b, c)
                    square(b, at)
                    at += 1
                    if last:
                        project_k(*last)
                    if c % 2 == 1:
                        square(b, at)
                        at += 1
                    if last:
                        project_v(*last)
                    extra(b, c)

            def extra_first(b, c):
                if c == 0:
                    pe.wait_ge(ld["w"], 32)
                    turn_weights(0, 4, once("w_turned"))
                elif c == 1:
                    pe.wait_ge(once("wT_ready"), 1)
                    pe.wait_ge(once("xn_ready"), B)
                    for i in range(B):
                        t = turn(ps[:, 1, P * i:P * i + P], xn[:, i, :])
                    t.then_inc(once("xn_turned"), 1)
                elif c == 2:
                    pe.wait_ge(once("xnT_ready"), 1)
                    pe.matmul(ps[:, 1, :], wT[:, W_Q, :], xnT[:, :], start=True, stop=True).then_inc(once("q_done"), 1)
                else:
                    pe.wait_ge(once("q_step"), 1)
                    pe.wait_ge(ld["wp"], 16)
                    pe.wait_ge(ld["vec"], 16 * 5)
                    pe.transpose(ps[:, 1, 3 * P:3 * P + VECS], vec_nat[:, :], ident[0:VECS, 0:VECS])
                    turn_weights(4, 3, once("w_turned"))

            def extra_last(b, c):
                if c < 2:
                    pe.wait_ge(once("w_bin_ready"), 2)
                    if c == 0:
                        pe.wait_ge(once("wT_ready"), 2)
                    else:
                        pe.wait_ge(once("w1T_ready"), 1)
                    for i in range(HB):
                        t = turn(ps[:, 1, P * i:P * i + P], w_bin[:, HB * c + i, :])
                    t.then_inc(once("w_bin_turned"), 1)
                elif c == 2:
                    pe.wait_ge(once("w2T_ready"), 1)
                    pe.wait_ge(once("mask_abs_ready"), 1)
                    turn(ps[0:1, 1, 0:P], mask_abs[:, 0:1]).then_inc(once("mask_turned"), 1)

            pe.wait_ge(ld["ssm"], 32)
            for w in range(2):
                t = pe.matmul(ps[:, 6, P * w:P * w + P], w_nat[:, w, :], w_nat[:, w, :], start=True, stop=True)
            t.then_inc(sq_done, 1)
            pe.wait_ge(once("kvT_ready"), 1)
            pe.wait_ge(once("ones_ready"), 1)
            prep(0, extra_first)
            with pe.Fori(1, B - 1) as b:
                prep(b, lambda b, c: None)
            prep(B - 1, extra_last)
            pe.wait_ge(once("mask_flag_ready"), 1)
            any_mask = pe.value_load(mask_flag[0:1, 0:1], min_val=0, max_val=1)
            project_k(B - 1, CHUNKS - 1)
            pe.wait_ge(pow_ready, SQUARINGS + 1)
            for w in range(2):
                t = pe.matmul(ps[:, 6, P * w:P * w + P], gram[:, w, :], power[:, 0, w, :], start=True, stop=True)
            t.then_inc(once("ray_done"), 1)
            project_v(B - 1, CHUNKS - 1)

            def mask_query(bank, c):
                pe.matmul(ps[:, bank, :], ident[:, :], mask_sb[:, 512 * c:512 * c + 512].rearrange(
                    "q (p j) -> q j p", j=4), start=True, stop=False)

            def mask_key(dst, c, j, first):
                keys = mask_sb[:, 512 * c:512 * c + 512].rearrange("q (p j) -> q j p", j=4)
                pe.matmul(dst, keys[:, j, :], ident[:, :], start=first, stop=False, skip_group_check=True)

            def scores(b, u, masked):
                p, c = divmod(u, CHUNKS)
                slot = p % 4
                if c == 0:
                    pe.wait_ge(k_rows_loaded[slot], 16 * len(K_BLOCKS) * (2 * b + p // 4 + 1))
                wait(pe, pmax_ready, UNITS * b + u - 1)
                bank = 2 * (u % 2)
                if masked:
                    for h in range(2):
                        mask_query(bank + h, c)
                for h in range(2):
                    t = pe.matmul(ps[:, bank + h, :], q_rows[:, p, bass.ds(b, 1), h, :].rearrange("r b q -> r (b q)"),
                                  k_rows[:, slot, 512 * c:512 * c + 512], start=not masked, stop=True)
                t.then_inc(scores_ready, 1)

            def turn_max(b, p):
                pe.wait_ge(split_step, 4 * (PAIRS * b + p) + 4)
                wait(pe, o_ready, PAIRS * b + p - 1)
                for h in range(2):
                    t = pe.matmul(ps[:, 6 + p % 2, 128 + P * h:128 + P * h + P], max_cols[:, p % 2, h, :],
                                  ident_bf[:, :], start=True, stop=True)
                t.then_inc(max_turned, 1)

            def keyscores(b, u, masked):
                p, c = divmod(u, CHUNKS)
                if c == 0:
                    pe.wait_ge(q_max_ready, PAIRS * b + p + 1)
                for half in range(2):
                    wait(pe, probs_ready, 2 * (UNITS * b + u) - 1 + half)
                    for j in (2 * half, 2 * half + 1):
                        dst = ps[:, 4 + half, 2 * P * (j % 2):2 * P * (j % 2) + 2 * P]
                        if masked:
                            for h in range(2):
                                mask_key(dst[:, P * h:P * h + P], c, j, j % 2 == 0 and h == 0)
                        at = 512 * c + P * j
                        t = pe.matmul(dst, k_rows[:, p % 4, at:at + P],
                                      q_max[:, p % 2, :, :].rearrange("r h q -> r (h q)"),
                                      start=not masked, stop=True, skip_group_check=masked)
                    t.then_inc(keyscores_ready, 1)

            def pv(b, u):
                p, c = divmod(u, CHUNKS)
                if c == 0:
                    pe.wait_ge(v_now_ready, PAIRS * b + p + 1)
                    wait(pe, o_ready, PAIRS * b + p - 1)
                    pe.wait_ge(q_max_ready, PAIRS * b + p + 1)
                pe.wait_ge(probs_ready, 2 * (UNITS * b + u) + 2)
                for j in range(4):
                    for h in range(2):
                        at = 32 * (2 * (j % 2) + h)
                        t = pe.matmul(ps[at:at + HEAD_COLS, 6 + p % 2, 0:P],
                                      v_now[:, p % 2, 4 * c + j, HEAD_COLS * h:HEAD_COLS * h + HEAD_COLS],
                                      probs[:, c, j // 2, P * (2 * (j % 2) + h):P * (2 * (j % 2) + h) + P],
                                      start=(c == 0 and j < 2), stop=(c == CHUNKS - 1 and j >= 2))
                t.then_inc(pv_done, 1)

            def turn_out(b, p):
                pe.wait_ge(oT_ready, PAIRS * b + p + 1)
                pe.matmul(ps[:, 6 + p % 2, 384:384 + 2 * HEAD_COLS], oT_sb[:, p % 2, :], gather[:, :],
                          start=True, stop=True).then_inc(o_turned, 1)

            def attend(masked):
                for u in range(2):
                    scores(0, u, masked)
                pe.wait_ge(once("ray_ready"), 4)
                pe.matmul(ps[:, 7, 0:4], ones[:, :], ray[:, :], start=True, stop=True
                          ).then_inc(once("ray_summed"), 1)
                for u in range(2, 6):
                    scores(0, u, masked)
                pe.wait_ge(once("out_banks_zeroed"), 1)
                turn_max(0, 0)
                for u in range(6, LEAD):
                    scores(0, u, masked)
                pe.wait_ge(v_ready, B * CHUNKS)
                keyscores(0, 0, masked)
                pe.wait_ge(once("out_banks_zeroed"), 2)

                def batch(b):
                    last = isinstance(b, int) and b == B - 1
                    first = isinstance(b, int) and b == 0
                    for u in range(UNITS):
                        p, c = divmod(u, CHUNKS)
                        if u + 1 < UNITS:
                            keyscores(b, u + 1, masked)
                        elif not last:
                            keyscores(b + 1, 0, masked)
                        if u + LEAD < UNITS:
                            scores(b, u + LEAD, masked)
                        elif not last:
                            scores(b + 1, u + LEAD - UNITS, masked)
                        if c == 0 and p > 0:
                            turn_out(b, p - 1)
                        elif c == 0 and not first:
                            turn_out(b - 1, PAIRS - 1)
                        pv(b, u)
                        if c == 1 and p + 1 < PAIRS:
                            turn_max(b, p + 1)
                        elif c == 1 and not last:
                            turn_max(b + 1, 0)
                loop_batches(pe, batch)
                turn_out(B - 1, PAIRS - 1)

            pe.wait_ge(k1_ready, B * CHUNKS)
            pe.wait_ge(r1_ready, B * CHUNKS)
            pe.wait_ge(once("w2T_ready"), 1)
            pe.wait_ge(once("q_rows_ready"), 2 * CHUNKS)
            pe.wait_ge(once("k_pads_copied"), 16)
            pe.wait_ge(once("ident_bf_ready"), 1)
            pe.wait_ge(ld["gather"], 16)
            pe.wait_ge(once("q_pads_ready"), 2)
            with pe.If(any_mask > 0):
                attend(True)
            with pe.Else():
                attend(False)
            pe.wait_ge(o_ready, B * PAIRS)

            def turn_half(h, src, s):
                for b in halves[h]:
                    t = turn(bank(h, TURN)[:, P * (b % 2):P * (b % 2) + P], src[:, b, :])
                t.then_inc(s, 1)

            def by_token(h, at, lhsT, rhs, s):
                for b in halves[h]:
                    t = pe.matmul(bank(h, at)[:, P * (b % 2):P * (b % 2) + P], lhsT[:, P * b:P * b + P], rhs,
                                  start=True, stop=True)
                t.then_inc(s, 1)

            for h in range(2):
                turn_half(h, o_nat, once("oN_turned"))
            for h in range(2):
                pe.wait_ge(once("oNT_ready"), h + 1)
                by_token(h, PROJ, xnT, wT[:, W_O, :], once("attn_done"))
            for h in range(2):
                pe.wait_ge(once("ln2_ready"), 2 * h + 2)
                turn_half(h, xn, once("ln2_turned"))
            for h in range(2):
                pe.wait_ge(once("ln2T_ready"), h + 1)
                pe.matmul(bank(h, RAW_DELTA)[:, 0:HALF], wT[:, W_P, :], xnT[:, cols(h)], start=True, stop=True
                          ).then_inc(once("ssm_done"), 1)
            for h in range(2):
                for i in range(2):
                    t = pe.matmul(bank(h, RAW_BC)[:, HALF * i:HALF * i + HALF], wT[:, W_P + 1 + i, :],
                                  xnT[:, cols(h)], start=True, stop=True)
                t.then_inc(once("ssm_done"), 1)
            for h in range(2):
                pe.matmul(bank(h, RAW_U)[:, 0:HALF], wT[:, W_IN, :], xnT[:, cols(h)], start=True, stop=True
                          ).then_inc(once("ssm_done"), 1)
            for h in range(2):
                pe.wait_ge(once("yhat_ready"), h + 1)
                by_token(h, Y, q_r1, wT[:, W_OUT, :], once("y_done"))
            for h in range(2):
                pe.wait_ge(once("ln3_ready"), 2 * h + 2)
                turn_half(h, xn, once("ln3_turned"))
            for h in range(2):
                pe.wait_ge(once("ln3T_ready"), h + 1)
                for i in range(HB):
                    t = pe.matmul(bank(h, HIDDEN + i // 2)[:, HALF * (i % 2):HALF * (i % 2) + HALF], w1T[:, i, :],
                                  xnT[:, cols(h)], start=True, stop=True)
                    if i % 2 == 1:
                        t.then_inc(once("h_done"), 1)
            for h in range(2):
                for i in range(HB):
                    pe.wait_ge(once("gelu_ready"), HB * h + i + 1)
                    for b in halves[h]:
                        t = pe.matmul(bank(h, OUT)[:, P * (b % 2):P * (b % 2) + P],
                                      probs[:, i, 0, P * b:P * b + P], w2T[:, i, :],
                                      start=(i == 0 and b % 2 == 0), stop=(i == HB - 1), skip_group_check=True)
                t.then_inc(once("mlp_done"), 1)

        @block.scalar
        def _(act):
            act.dma_start(ident[:, :], ident_in).then_inc(ld["ident"], 16)
            rows = lambda v: v.rearrange("(a p) -> a p", p=P)
            for v, at in ((bk, BK), (bq, BQ)):
                act.dma_start(vec_nat[at:at + 1, :], rows(v)).then_inc(ld["vec_qk"], 16)

            def copy(dst, src, s, n=1):
                act.activation(dst, src, ACT.Copy).then_inc(s, n)

            act.wait_ge(once("kv_turned"), 1)
            copy(kvT[:, :, :].rearrange("p a d -> p (a d)"), ps[:, 1, 0:2 * P], once("vec_ready"))
            copy(vec[:, 0:2], ps[:, 1, 2 * P:2 * P + 2], once("kvT_ready"))

            def copy_ctx(b, c):
                n = 4 * b + c
                hold(act, ctx_turned, n + 1)
                hold(act, v_done, n - 1)
                copy(ctxT[:, c % 2, :], ps[:, 0, :], ctxT_ready)

            def first_k(b, c):
                hold(act, k_done, 4 * b + c + 1)
                act.activation(k_parts[:, 0, bass.ds(b * KEYS + 512 * c, 512)], ps[:, 2 + c % 2, :], ACT.Identity,
                               bias=vec[:, BK:BK + 1]).then_inc(k1_ready, 1)

            def second_k(b, c):
                hold(act, r1_ready, 4 * b + c + 1)
                copy(k_parts[:, 1, bass.ds(b * KEYS + 512 * c, 512)], k_r1[:, c % 2, :], k2_ready)

            def take_vall(b, c):
                hold(act, v_done, 4 * b + c + 1)
                dst = v_all[:, bass.ds(b * KT + 4 * c, 4), :].rearrange("p t (h m) -> p (t h) m", m=HEAD_COLS)
                copy(dst[:, :, 0:HD], ps[:, 4 + c % 2, :].rearrange("p (t m) -> p t m", m=HD), v_ready)

            def prep(b, extra):
                for c in range(CHUNKS):
                    copy_ctx(b, c)
                    extra(c)
                    if chunk_before(b, c, 2):
                        take_vall(*chunk_before(b, c, 2))
                    if chunk_before(b, c, 1):
                        first_k(*chunk_before(b, c, 1))
                    if chunk_before(b, c, 2):
                        second_k(*chunk_before(b, c, 2))

            def extra_first(c):
                if c == 1:
                    act.wait_ge(once("w_turned"), 1)
                    copy(wT[:, 0:4, :].rearrange("p a d -> p (a d)"), ps[:, 1, :], once("wT_ready"))
                elif c == 2:
                    act.wait_ge(once("xn_turned"), 1)
                    copy(xnT[:, :], ps[:, 1, :], once("xnT_ready"))

            def extra_last(c):
                if c == 1:
                    act.wait_ge(once("w_bin_turned"), 1)
                    copy(w1T[:, :, :].rearrange("p a d -> p (a d)"), ps[:, 1, :], once("w1T_ready"))
                elif c == 2:
                    act.wait_ge(once("w_bin_turned"), 2)
                    copy(w2T[:, :, :].rearrange("p a d -> p (a d)"), ps[:, 1, :], once("w2T_ready"))

            prep(0, extra_first)
            act.wait_ge(once("w_turned"), 2)
            copy(wT[:, 4:7, :].rearrange("p a d -> p (a d)"), ps[:, 1, 0:3 * P], once("vec_ready"))
            copy(vec[:, 2:VECS], ps[:, 1, 3 * P + 2:3 * P + VECS], once("wT_ready"))
            with act.Fori(1, B - 1) as b:
                prep(b, lambda c: None)
            prep(B - 1, extra_last)
            first_k(B - 1, CHUNKS - 1)
            take_vall(B - 1, CHUNKS - 2)
            second_k(B - 1, CHUNKS - 2)
            take_vall(B - 1, CHUNKS - 1)
            second_k(B - 1, CHUNKS - 1)
            act.wait_ge(ld["log_gain"], 16)
            act.activation(sv[:, 0:1], vec[:, ALPHA:ALPHA + 1], ACT.Abs).then_inc(once("alpha_step"), 1)
            act.wait_ge(once("alpha_step"), 1)
            act.activation(sv[:, 1:2], sv[:, 0:1], ACT.Exp, scale=-1.0).then_inc(once("alpha_step"), 1)
            act.wait_ge(once("alpha_step"), 2)
            act.activation(sv[:, 2:3], sv[:, 1:2], ACT.Ln, bias=1.0).then_inc(once("alpha_step"), 1)
            act.activation(sv[:, 3:4], log_gain[:, :], ACT.Exp).then_inc(once("alpha_step"), 1)

            def exp_unit(b, u):
                c = u % CHUNKS
                for h in range(2):
                    hold(act, keyscores_ready, 2 * (UNITS * b + u) + h + 1)
                    if h == 0:
                        hold(act, pv_done, UNITS * b + u - 3)
                    act.activation(probs[:, c, h, :], ps[:, 4 + h, :], ACT.Exp).then_inc(probs_ready, 1)

            def copy_out(b, p):
                hold(act, pv_done, CHUNKS * (PAIRS * b + p) + CHUNKS)
                hold(act, o_turned, PAIRS * b + p - 1)
                copy(oT_sb[:, p % 2, :], ps[:, 6 + p % 2, 0:P], oT_ready)

            def batch(b):
                first = isinstance(b, int) and b == 0
                for u in range(UNITS):
                    exp_unit(b, u)
                    if u % CHUNKS == 0:
                        if u > 0:
                            copy_out(b, u // CHUNKS - 1)
                        elif not first:
                            copy_out(b - 1, PAIRS - 1)
            loop_batches(act, batch)
            copy_out(B - 1, PAIRS - 1)

            for h in range(2):
                act.wait_ge(once("oN_turned"), h + 1)
                act.activation(xnT[:, cols(h)], bank(h, TURN)[:, 0:HALF], ACT.Identity, bias=vec[:, BV:BV + 1]
                               ).then_inc(once("oNT_ready"), 1)
            for h in range(2):
                act.wait_ge(once("ln2_turned"), h + 1)
                copy(xnT[:, cols(h)], bank(h, TURN)[:, 0:HALF], once("ln2T_ready"))

            act.wait_ge(once("small_ready"), 2)
            for h in range(2):
                act.wait_ge(once("ssm_done"), h + 1)
                act.activation(SP_ABS[:, cols(h)], bank(h, RAW_DELTA)[:, 0:HALF], ACT.Abs, bias=sv[:, 5:6]
                               ).then_inc(once("abs_ready"), 1)
                act.wait_ge(once("abs_ready"), h + 1)
                act.activation(SP_EXP[:, cols(h)], SP_ABS[:, cols(h)], ACT.Exp, scale=-1.0
                               ).then_inc(once("exp_ready"), 1)
            for h in range(2):
                act.wait_ge(once("exp_ready"), h + 1)
                act.activation(SP_LN[:, cols(h)], SP_EXP[:, cols(h)], ACT.Ln, bias=1.0).then_inc(once("ln_ready"), 1)
            for h in range(2):
                act.wait_ge(once("ssm_done"), 2 + h + 1)
                for i, gate in enumerate((G_B, G_C)):
                    act.activation(gate[:, cols(h)], bank(h, RAW_BC)[:, HALF * i:HALF * i + HALF], ACT.Tanh,
                                   bias=vec[:, BP0 + 1 + i:BP0 + 2 + i]).then_inc(once("tanh_ready"), 1)
            for h in range(2):
                act.wait_ge(once("delta_ready"), h + 1)
                act.activation(G_A0[:, cols(h)], DELTA[:, cols(h)], ACT.Exp, scale=sv[:, 4:5]
                               ).then_inc(once("a0_ready"), 1)
            for h in range(2):
                act.wait_ge(once("tanh_ready"), 2 * h + 2)
                act.activation(G_CC[:, cols(h)], G_C[:, cols(h)], ACT.Square).then_inc(once("cc_ready"), 1)
                act.activation(G_R[:, cols(h)], G_B[:, cols(h)], ACT.Square).then_inc(once("r_ready"), 1)
            for h in range(2):
                act.wait_ge(once("ab_ready"), h + 1)
                act.activation(G_Q[:, cols(h)], G_Q[:, cols(h)], ACT.Square, scale=2.0).then_inc(once("q_ready"), 1)
            for h in range(2):
                act.wait_ge(once("disc_ready"), h + 1)
                act.activation(G_D[:, cols(h)], G_D[:, cols(h)], ACT.Sqrt).then_inc(once("disc_root"), 1)
            for h in range(2):
                act.wait_ge(once("lam_ready"), h + 1)
                act.activation(G_L[:, cols(h)], G_L[:, cols(h)], ACT.Sqrt).then_inc(once("scale_ready"), 1)
            for h in range(2):
                act.wait_ge(once("ln3_turned"), h + 1)
                copy(xnT[:, cols(h)], bank(h, TURN)[:, 0:HALF], once("ln3T_ready"))
            for h in range(2):
                for i in range(HB):
                    act.wait_ge(once("h_done"), 2 * h + i // 2 + 1)
                    act.activation(probs[:, i, 0, cols(h)], bank(h, HIDDEN + i // 2)[:, HALF * (i % 2):HALF * (i % 2) + HALF],
                                   ACT.Gelu, bias=vec[:, B1_0 + i:B1_0 + i + 1]).then_inc(once("gelu_ready"), 1)

        @block.gpsimd
        def _(gp):
            gp.memset(ones[:, :], 1.0).then_inc(once("ones_ready"), 1)
            gp.memset(neg_half[:, :], -0.5).then_inc(once("half_ready"), 1)

            def root_inv(name):
                gp.wait_ge(once(name + "_var"), 1)
                gp.tensor_tensor(rstd[:, :], var_eps[:, :], neg_half[:, :], ALU.pow).then_inc(once(name + "_rstd"), 1)

            def root_inv_halves(name):
                for h in range(2):
                    two = slice(2 * h, 2 * h + 2)
                    gp.wait_ge(once(name + "_var"), h + 1)
                    gp.tensor_tensor(rstd[:, two], var_eps[:, two], neg_half[:, two], ALU.pow
                                     ).then_inc(once(name + "_rstd"), 1)

            gp.dma_start(head_rows[:, :], head_rows_in).then_inc(ld["head_rows"], 16)
            spread = lambda v: v.rearrange("(a n) -> a n", a=1).broadcast_to((P, D))
            gp.dma_start(bo_rows[:, :], spread(bo)).then_inc(ld["rows"], 16)
            gp.dma_start(b2_rows[:, :], spread(b2)).then_inc(ld["rows"], 16)
            gp.dma_start(log_gain[:, :], log_gamma.broadcast_to((P, 1))).then_inc(ld["log_gain"], 16)
            gp.dma_start(gather[:, :], gather_in).then_inc(ld["gather"], 16)
            gp.memset(q_rows[:, :, :, :, :].rearrange("r p b h q -> r (p b h q)").bitcast(F32), 0.0
                      ).then_inc(once("q_pads_ready"), 1)
            gp.wait_ge(once("half_ready"), 1)
            root_inv("xn")
            gp.memset(v_all[:, :, :].rearrange("p t (h m) -> p (t h) m", m=HEAD_COLS)[:, :, HD:HD + 1], 1.0
                      ).then_inc(once("v_ones_ready"), 1)
            gp.memset(max_cols[:, :, :, :], 0.0).then_inc(once("q_pads_ready"), 1)

            def third(b, c):
                n = 4 * b + c
                keys = bass.ds(b * KEYS + 512 * c, 512)
                hold(gp, k2_ready, n + 1)
                gp.tensor_tensor(k_parts[:, 2, keys], k_r1[:, c % 2, :], k_parts[:, 1, keys], ALU.subtract
                                 ).then_inc(k3_ready, 1)

            w_halves = ((slice(0, HB), w1_nat[:, :, :].rearrange("p a d -> p (a d)")), (slice(HB, 2 * HB), w2_nat[:, :]))
            flat = lambda t, sl: t[:, sl, :].rearrange("p a d -> p (a d)")

            def binarise(c, half):
                sl, nat = w_halves[half]
                step = once("w_bin_step")
                if c == 0:
                    gp.wait_ge(once("w_neg_ready"), 2)
                    gp.tensor_tensor(flat(w_sgn, sl), flat(w_sgn, sl), flat(w_bin, sl), ALU.subtract).then_inc(step, 1)
                elif c == 1:
                    gp.wait_ge(step, half + 1)
                    gp.wait_ge(once("w_abs_ready"), 2)
                    if half == 0:
                        a = w_abs[:, 0:HB].unsqueeze(2).broadcast_to((P, HB, D))
                    else:
                        a = w_abs[:, HB:HB + 1].unsqueeze(2).broadcast_to((P, HB, D))
                    gp.tensor_tensor(w_bin[:, sl, :], w_sgn[:, sl, :], a, ALU.mult).then_inc(step, 1)
                elif c == 2:
                    gp.wait_ge(step, 2 + half + 1)
                    gp.tensor_tensor(flat(w_bin, sl), flat(w_bin, sl), nat, ALU.subtract).then_inc(step, 1)
                else:
                    gp.wait_ge(step, 4 + half + 1)
                    gp.tensor_tensor(flat(w_bin, sl), flat(w_bin, sl), nat, ALU.add).then_inc(once("w_bin_ready"), 1)

            for c in range(CHUNKS):
                third(0, c)
                if c < 2:
                    for b in range(2 * c, 2 * c + 2):
                        gp.wait_ge(ld["rows"], 32)
                        gp.tensor_tensor(x_bo[:, b, :], x_sb[:, b, :], bo_rows[:, :], ALU.add
                                         ).then_inc(once("x_bo_ready"), 1)
            for c in range(CHUNKS):
                binarise(c, 0)
                third(1, c)
                binarise(c, 1)
            with gp.Fori(2, B) as b:
                for c in range(CHUNKS):
                    third(b, c)

            def take_v(b, p):
                hold(gp, pv_done, CHUNKS * (PAIRS * b + p - 1))
                gp.tensor_copy(v_now[:, p % 2, :, :],
                               v_all[:, bass.ds(b * KT, KT), 2 * HEAD_COLS * p:2 * HEAD_COLS * (p + 1)]
                               ).then_inc(v_now_ready, 1)

            def split_max(b, p):
                i = PAIRS * b + p
                nm, r1, cols_ = negmax[:, p % 2, :], nm_r1[:, p % 2, :], max_cols[:, p % 2, :, :]
                hold(gp, negmax_ready, i + 1)
                hold(gp, max_turned, i - 1)
                gp.tensor_copy(cols_[:, :, MAX_ROW], nm).then_inc(split_step, 1)
                hold(gp, split_step, 4 * i + 1)
                gp.tensor_tensor(r1, nm, cols_[:, :, MAX_ROW], ALU.subtract).then_inc(split_step, 1)
                hold(gp, split_step, 4 * i + 2)
                gp.tensor_copy(cols_[:, :, MAX_ROW + 1], r1).then_inc(split_step, 1)
                hold(gp, split_step, 4 * i + 3)
                gp.tensor_tensor(cols_[:, :, MAX_ROW + 2], r1, cols_[:, :, MAX_ROW + 1], ALU.subtract
                                 ).then_inc(split_step, 1)

            gp.wait_ge(v_ready, B * CHUNKS)
            gp.wait_ge(once("v_ones_ready"), 1)
            def batch(b):
                for p in range(PAIRS):
                    split_max(b, p)
                    take_v(b, p)
            loop_batches(gp, batch)
            gp.wait_ge(once("norm_step"), 2)
            gp.tensor_tensor(norm_inv[:, :], norm_inv[:, :], neg_half[:, 0:2], ALU.pow).then_inc(once("norm_ready"), 1)
            root_inv_halves("ln2")
            for h in range(2):
                gp.wait_ge(once("p_ready"), h + 1)
                gp.wait_ge(once("r_ready"), h + 1)
                gp.tensor_tensor(G_S[:, cols(h)], G_P[:, cols(h)], G_R[:, cols(h)], ALU.add
                                 ).then_inc(once("s_ready"), 1)
            for h in range(2):
                gp.wait_ge(once("inv_ready"), h + 1)
                gp.tensor_tensor(G_CS[:, cols(h)], G_C[:, cols(h)], G_INV[:, cols(h)], ALU.mult
                                 ).then_inc(once("c_scaled"), 1)
            root_inv_halves("ln3")

        @block.vector
        def _(dve):
            def layernorm(src, name):
                s = once(name + "_step")
                for b in range(B):
                    dve.bn_stats(bn[:, b, :], src[:, b, :]).then_inc(s, 1)
                dve.wait_ge(s, B)
                for b in range(B):
                    dve.bn_aggr(mv[:, b, :], bn[:, b, :]).then_inc(s, 1)
                dve.wait_ge(s, 2 * B)
                dve.tensor_scalar(var_eps[:, :], mv[:, :, 1], LN_EPS, None, ALU.add).then_inc(once(name + "_var"), 1)
                dve.wait_ge(once(name + "_rstd"), 1)
                for b in range(B):
                    dve.tensor_scalar(xn[:, b, :], src[:, b, :], mv[:, b, 0:1], rstd[:, b:b + 1],
                                      ALU.subtract, ALU.mult).then_inc(once(name + "_ready"), 1)

            dve.memset(k_rows[:, 0:2, :], 1.0).then_inc(once("k_pads_ready"), 1)
            dve.wait_ge(sq_done, 1)
            dve.tensor_copy(gram[:, :, :], ps[:, 6, 0:2 * P].rearrange("p (w d) -> p w d", w=2)
                            ).then_inc(once("gram_ready"), 1)
            dve.wait_ge(once("gram_ready"), 1)
            dve.tensor_copy(power[:, 0, :, :], gram[:, :, :]).then_inc(pow_ready, 1)

            def split_q():
                dve.wait_ge(once("q_done"), 1)
                dve.tensor_scalar(q32[:, :], ps[:, 1, :], vec[:, BQ:BQ + 1], 1.0 / math.sqrt(HD), ALU.add, ALU.mult
                                  ).then_inc(once("q_step"), 1)
                dve.wait_ge(once("q_step"), 1)
                dve.tensor_copy(q_parts[:, 0, :], q32[:, :]).then_inc(once("q_step"), 1)
                dve.wait_ge(once("q_step"), 2)
                dve.tensor_tensor(q_r1[:, :], q32[:, :], q_parts[:, 0, :], ALU.subtract).then_inc(once("q_step"), 1)

            def split_q_rest():
                dve.wait_ge(once("q_step"), 3)
                dve.tensor_copy(q_parts[:, 1, :], q_r1[:, :]).then_inc(once("q_step"), 1)
                dve.wait_ge(once("q_step"), 4)
                dve.tensor_tensor(q_parts[:, 2, :], q_r1[:, :], q_parts[:, 1, :], ALU.subtract
                                  ).then_inc(once("q_parts_ready"), 1)

            def weight_means():
                dve.wait_ge(ld["mlp"], 32)
                dve.tensor_reduce(w_abs[:, 0:HB], w1_nat[:, :, :], AX.X, ALU.add, apply_absolute_value=True
                                  ).then_inc(once("w_abs_step"), 1)
                dve.tensor_reduce(w_abs[:, HB:HB + 1], w2_nat[:, :], AX.X, ALU.add, apply_absolute_value=True
                                  ).then_inc(once("w_abs_step"), 1)
                dve.wait_ge(once("w_abs_step"), 2)
                dve.tensor_scalar(w_abs[:, 0:HB], w_abs[:, 0:HB], 1.0 / D, None, ALU.mult
                                  ).then_inc(once("w_abs_ready"), 1)
                dve.tensor_scalar(w_abs[:, HB:HB + 1], w_abs[:, HB:HB + 1], 1.0 / HID, None, ALU.mult
                                  ).then_inc(once("w_abs_ready"), 1)

            def weight_signs():
                flat = lambda t, half: t[:, HB * half:HB * half + HB, :].rearrange("p a d -> p (a d)")
                for half, nat in enumerate((w1_nat[:, :, :].rearrange("p a d -> p (a d)"), w2_nat[:, :])):
                    dve.tensor_scalar(flat(w_sgn, half), nat, 0.0, None, ALU.is_gt)
                    dve.tensor_scalar(flat(w_bin, half), nat, 0.0, None, ALU.is_lt).then_inc(once("w_neg_ready"), 1)

            def mask_magnitude(half):
                dve.wait_ge(ld["mask"], 16)
                dve.tensor_reduce(mask_abs[:, 1 + half:2 + half], mask_sb[:, KEYS // 2 * half:KEYS // 2 * (half + 1)],
                                  AX.X, ALU.max, apply_absolute_value=True).then_inc(once("mask_half"), 1)
                if half == 1:
                    dve.wait_ge(once("mask_half"), 2)
                    dve.tensor_tensor(mask_abs[:, 0:1], mask_abs[:, 1:2], mask_abs[:, 2:3], ALU.max
                                      ).then_inc(once("mask_abs_ready"), 1)

            def flag_mask():
                dve.wait_ge(once("mask_turned"), 1)
                dve.tensor_reduce(mask_flag_f[:, :], ps[0:1, 1, 0:P], AX.X, ALU.max).then_inc(once("flag_step"), 1)
                dve.wait_ge(once("flag_step"), 1)
                dve.tensor_scalar(mask_flag[:, :], mask_flag_f[:, :], 0.0, None, ALU.is_gt
                                  ).then_inc(once("mask_flag_ready"), 1)

            def rest_k(b, c):
                n = 4 * b + c
                keys = bass.ds(b * KEYS + 512 * c, 512)
                dve.wait_ge(k1_ready, n + 1)
                wait(dve, k3_ready, n - 1)
                wait(dve, k2_ready, n - 1)
                dve.scalar_tensor_tensor(k_r1[:, c % 2, :], ps[:, 2 + c % 2, :], vec[:, BK:BK + 1],
                                         k_parts[:, 0, keys], ALU.add, ALU.subtract).then_inc(r1_ready, 1)

            def sum_squares(slot):
                for w in range(2):
                    dve.tensor_tensor_reduce(sq_junk[:, w, :], power[:, slot, w, :], power[:, slot, w, :],
                                             1.0, 0.0, ALU.mult, ALU.add, fro[:, w:w + 1]).then_inc(fro_ready, 1)

            def next_power(b, at):
                k, norms = 6 * b + at, 2 * b + at // SQ_PERIOD
                dve.wait_ge(pow_ready, k + 1)
                if at % SQ_PERIOD == 0:
                    dve.wait_ge(fro_summed, norms + 1)
                    dve.tensor_scalar(fro_inv[:, :], ps[:, 7, 0:2], TINY, None, ALU.max).then_inc(fro_inv_ready, 1)
                    dve.wait_ge(fro_inv_ready, 2 * norms + 1)
                    dve.reciprocal(fro_inv[:, :], fro_inv[:, :]).then_inc(fro_inv_ready, 1)
                    dve.wait_ge(fro_inv_ready, 2 * norms + 2)
                    dve.wait_ge(sq_done, k + 2)
                    for w in range(2):
                        t = dve.tensor_scalar(power[:, (at + 1) % 2, w, :], ps[:, 6, P * w:P * w + P],
                                              fro_inv[:, w:w + 1], None, ALU.mult)
                        if w == 0:
                            t.then_inc(once("pow_half"), 1)
                    t.then_inc(pow_ready, 1)
                else:
                    dve.wait_ge(sq_done, k + 2)
                    dve.tensor_copy(power[:, (at + 1) % 2, :, :],
                                    ps[:, 6, 0:2 * P].rearrange("p (w d) -> p w d", w=2)).then_inc(pow_ready, 1)
                if (at + 1) % SQ_PERIOD == 0:
                    dve.wait_ge(pow_ready, k + 2)
                    sum_squares((at + 1) % 2)

            def spread_q(c):
                pairs = slice(2 * c, 2 * c + 2)
                dve.wait_ge(once("q_loaded"), 16 * len(Q_BLOCKS))
                for h in range(2):
                    dve.tensor_scalar(q_rows[0:MAX_ROW, pairs, :, h, :].rearrange("r p b q -> r (p b) q"),
                                      q_both[0:MAX_ROW, pairs, :].rearrange("r p (b q) -> r (p b) q", b=B),
                                      head_rows[0:MAX_ROW, h:h + 1], None, ALU.mult).then_inc(once("q_rows_ready"), 1)

            def prep(b, extra, early=lambda c: None):
                at = 0
                for c in range(CHUNKS):
                    next_power(b, at)
                    at += 1
                    early(c)
                    if c % 2 == 1:
                        next_power(b, at)
                        at += 1
                    if chunk_before(b, c, 1):
                        rest_k(*chunk_before(b, c, 1))
                    extra(b, c)

            def extra_first(b, c):
                if c == 0:
                    dve.wait_ge(ld["x"], 16)
                    layernorm(x_sb, "xn")
                elif c == 1:
                    dve.wait_ge(ld["ident"], 16)
                    dve.tensor_copy(ident_bf[:, :], ident[:, :]).then_inc(once("ident_bf_ready"), 1)
                    weight_means()
                elif c == 2:
                    split_q()
                else:
                    split_q_rest()
                    weight_signs()

            def extra_last(b, c):
                spread_q(c)
                if c == 2:
                    flag_mask()

            def early_last(c):
                if c < 2:
                    mask_magnitude(c)

            dve.wait_ge(pow_ready, 1)
            sum_squares(0)
            dve.wait_ge(ld["head_rows"], 16)
            dve.wait_ge(once("q_pads_ready"), 1)
            prep(0, extra_first)
            with dve.Fori(1, B - 1) as b:
                prep(b, lambda b, c: None)
            prep(B - 1, extra_last, early_last)
            rest_k(B - 1, CHUNKS - 1)
            dve.wait_ge(fro_ready, 2 * (SQUARINGS // SQ_PERIOD + 1))
            dve.wait_ge(once("ray_done"), 1)
            for w in range(2):
                dve.tensor_tensor_reduce(sq_junk[:, w, :], ps[:, 6, P * w:P * w + P], power[:, 0, w, :],
                                         1.0, 0.0, ALU.mult, ALU.add, ray[:, w:w + 1]).then_inc(once("ray_ready"), 1)
            dve.wait_ge(once("ray_ready"), 2)
            for w in range(2):
                dve.tensor_tensor_reduce(sq_junk[:, w, :], power[:, 0, w, :], power[:, 0, w, :],
                                         1.0, 0.0, ALU.mult, ALU.add, ray[:, 2 + w:3 + w]
                                         ).then_inc(once("ray_ready"), 1)
            dve.memset(ps[:, 6, 0:P], 0.0).then_inc(once("out_banks_zeroed"), 1)

            def norms():
                dve.wait_ge(once("ray_summed"), 1)
                dve.tensor_scalar(ray_all[:, :], ps[:, 7, 0:4], TINY, None, ALU.max).then_inc(once("ray_all_ready"), 1)
                dve.wait_ge(once("ray_all_ready"), 1)
                dve.memset(ps[:, 7, 0:P], 0.0).then_inc(once("out_banks_zeroed"), 1)
                dve.reciprocal(fro_inv[:, :], ray_all[:, 2:4]).then_inc(once("ray_inv"), 1)
                dve.wait_ge(once("ray_inv"), 1)
                dve.tensor_tensor(norm_inv[:, :], ray_all[:, 0:2], fro_inv[:, :], ALU.mult
                                  ).then_inc(once("norm_step"), 1)
                dve.wait_ge(once("norm_step"), 1)
                dve.tensor_scalar(norm_inv[:, :], norm_inv[:, :], 1.0, None, ALU.max).then_inc(once("norm_step"), 1)

            def max_unit(b, u):
                p, c = divmod(u, CHUNKS)
                dve.wait_ge(scores_ready, UNITS * b + u + 1)
                if c == 0:
                    wait(dve, negmax_ready, PAIRS * b + p - 1)
                bank = 2 * (u % 2)
                dve.tensor_reduce(pmax[:, p % 2, :, c], ps[:, bank:bank + 2, :], AX.X, ALU.max
                                  ).then_inc(pmax_ready, 1)

            def neg_max(b, p):
                i = PAIRS * b + p
                dve.wait_ge(pmax_ready, CHUNKS * i + CHUNKS)
                wait(dve, split_step, 4 * (i - 1))
                dve.tensor_reduce(negmax[:, p % 2, :], pmax[:, p % 2, :, :], AX.X, ALU.max, negate=True
                                  ).then_inc(negmax_ready, 1)

            def add_max(b, p):
                dve.wait_ge(max_turned, PAIRS * b + p + 1)
                wait(dve, keyscores_ready, 2 * CHUNKS * (PAIRS * b + p - 1))
                dve.tensor_tensor(q_max[:, p % 2, :, :],
                                  ps[:, 6 + p % 2, 128:384].rearrange("r (h q) -> r h q", h=2),
                                  q_rows[:, p, bass.ds(b, 1), :, :].rearrange("r b h q -> r (b h) q"), ALU.add).then_inc(q_max_ready, 1)

            def out_of(p):
                return ps[:, 6 + p % 2, 384:384 + 2 * HEAD_COLS].rearrange("q (h m) -> q h m", h=2)

            def invert(b, p):
                dve.wait_ge(o_turned, PAIRS * b + p + 1)
                wait(dve, o_ready, PAIRS * b + p - 1)
                dve.reciprocal(rden[:, p % 2, :], out_of(p)[:, :, HD]).then_inc(rden_ready, 1)

            def normalise(b, p):
                i, o = PAIRS * b + p, out_of(p)
                dve.wait_ge(rden_ready, i + 1)
                dve.tensor_tensor(o_nat[:, bass.ds(b, 1), 16 * p:16 * p + 16].rearrange("q b (h m) -> q (b h) m", h=2),
                                  o[:, :, 0:HD], rden[:, p % 2, :].unsqueeze(2).broadcast_to((P, 2, HD)), ALU.mult
                                  ).then_inc(o_ready, 1)

            def before(b, p, lag):
                if p >= lag:
                    return b, p - lag
                if isinstance(b, int) and b == 0:
                    return None
                return b - 1, p - lag + PAIRS

            def batch(b):
                for u in range(UNITS):
                    p, c = divmod(u, CHUNKS)
                    max_unit(b, u)
                    if isinstance(b, int) and b == 0 and u == 6:
                        norms()
                    if c == CHUNKS - 1:
                        neg_max(b, p)
                    if c == 0 and before(b, p, 3):
                        invert(*before(b, p, 3))
                    if c == 0 and before(b, p, 3):
                        normalise(*before(b, p, 3))
                    if c == 1 and before(b, p, 1):
                        add_max(*before(b, p, 1))
            loop_batches(dve, batch)
            for p in range(PAIRS - 3, PAIRS):
                invert(B - 1, p)
                normalise(B - 1, p)
                if p == PAIRS - 3:
                    add_max(B - 1, PAIRS - 1)

            dve.memset(q_r1[:, :].rearrange("p (b t) -> p b t", b=B)[:, :, 0:1], 0.0
                       ).then_inc(once("first_step_ready"), 1)
            dve.tensor_scalar(sv[:, 6:7], vec[:, ALPHA:ALPHA + 1], 0.0, sv[:, 2:3], ALU.max, ALU.add
                              ).then_inc(once("small_step"), 1)
            dve.wait_ge(once("small_step"), 1)
            dve.tensor_scalar(sv[:, 4:5], sv[:, 6:7], -1.0, None, ALU.mult).then_inc(once("small_ready"), 1)
            dve.tensor_tensor(sv[:, 5:6], vec[:, BP0:BP0 + 1], vec[:, DBIAS:DBIAS + 1], ALU.add
                              ).then_inc(once("small_ready"), 1)
            dve.wait_ge(once("norm_ready"), 1)
            dve.tensor_tensor(sv[:, 7:8], sv[:, 3:4], norm_inv[:, 0:1], ALU.mult).then_inc(once("gain_ready"), 1)

            def by_half(a, h):
                return a[:, 2 * h:2 * h + 2, :].rearrange("p b d -> p (b d)")

            def layernorm_halves(name, add, producer):
                s = once(name + "_step")
                for h in range(2):
                    dve.wait_ge(once(producer), h + 1)
                    add(h).then_inc(once(name + "_in"), 1)
                    dve.wait_ge(once(name + "_in"), h + 1)
                    for b in halves[h]:
                        dve.bn_stats(bn[:, b, :], x_sb[:, b, :]).then_inc(s, 1)
                    dve.wait_ge(s, 2 * h + 2)
                    for b in halves[h]:
                        dve.bn_aggr(mv[:, b, :], bn[:, b, :]).then_inc(once(name + "_mean"), 1)
                    dve.wait_ge(once(name + "_mean"), 2 * h + 2)
                    dve.tensor_scalar(var_eps[:, 2 * h:2 * h + 2], mv[:, 2 * h:2 * h + 2, 1], LN_EPS, None, ALU.add
                                      ).then_inc(once(name + "_var"), 1)
                for h in range(2):
                    dve.wait_ge(once(name + "_rstd"), h + 1)
                    for b in halves[h]:
                        dve.tensor_scalar(xn[:, b, :], x_sb[:, b, :], mv[:, b, 0:1], rstd[:, b:b + 1],
                                          ALU.subtract, ALU.mult).then_inc(once(name + "_ready"), 1)

            own_steps = [0]

            def each(s, op, *waits):
                before_this = own_steps[0]
                for h in range(2):
                    for name in waits:
                        if name == "own":
                            dve.wait_ge(once("own_step"), before_this - 1 + h)
                        else:
                            dve.wait_ge(once(name), h + 1)
                    op(h, cols(h)).then_inc(once("own_step" if s == "own" else s), 1)
                    if s == "own":
                        own_steps[0] += 1

            dve.wait_ge(once("x_bo_ready"), B)
            layernorm_halves("ln2", lambda h: dve.tensor_tensor(
                by_half(x_sb, h), bank(h, PROJ)[:, 0:HALF], by_half(x_bo, h), ALU.add), "attn_done")
            dve.wait_ge(once("gain_ready"), 1)
            each("own", lambda h, t: dve.tensor_scalar(DELTA[:, t], bank(h, RAW_DELTA)[:, 0:HALF], sv[:, 5:6], 0.0,
                                                       ALU.add, ALU.max), "abs_ready")
            each("delta_ready", lambda h, t: dve.tensor_tensor(DELTA[:, t], DELTA[:, t], SP_LN[:, t], ALU.add),
                 "own", "ln_ready")
            for h in range(2):
                dve.wait_ge(once("ssm_done"), 4 + h + 1)
                dve.wait_ge(once("tanh_ready"), 2 * h + 2)
                dve.scalar_tensor_tensor(U_S[:, cols(h)], bank(h, RAW_U)[:, 0:HALF], sv[:, 7:8], G_B[:, cols(h)],
                                         ALU.mult, ALU.mult).then_inc(once("u_ready"), 1)
            each("a_ready", lambda h, t: dve.tensor_scalar(G_A[:, t], G_A0[:, t], 1.0 - EPS_A, None, ALU.min), "a0_ready")
            each("ab_ready", lambda h, t: dve.tensor_tensor(G_Q[:, t], G_A[:, t], G_B[:, t], ALU.mult), "a_ready")
            each("own", lambda h, t: dve.tensor_tensor(G_P[:, t], G_A[:, t], G_A[:, t], ALU.mult))
            each("p_ready", lambda h, t: dve.tensor_tensor(G_P[:, t], G_P[:, t], G_CC[:, t], ALU.add),
                 "own", "cc_ready")
            each("own", lambda h, t: dve.tensor_tensor(G_D[:, t], G_P[:, t], G_R[:, t], ALU.subtract),
                 "p_ready", "r_ready")
            each("own", lambda h, t: dve.tensor_tensor(G_D[:, t], G_D[:, t], G_D[:, t], ALU.mult), "own")
            each("disc_ready", lambda h, t: dve.scalar_tensor_tensor(G_D[:, t], G_D[:, t], EPS, G_Q[:, t],
                                                                     ALU.add, ALU.add), "own", "q_ready")
            each("own", lambda h, t: dve.tensor_tensor(G_L[:, t], G_S[:, t], G_D[:, t], ALU.add),
                 "s_ready", "disc_root")
            each("own", lambda h, t: dve.tensor_scalar(G_L[:, t], G_L[:, t], 0.5, EPS, ALU.mult, ALU.add),
                 "own")
            each("lam_ready", lambda h, t: dve.tensor_scalar(G_L[:, t], G_L[:, t], 1.0, None, ALU.max), "own")
            by_t = lambda a, h: a[:, cols(h)].rearrange("p (b t) -> p b t", t=T)

            def outputs(h):
                dve.wait_ge(once("state_ready"), 2 * h + 2)
                dve.wait_ge(once("c_scaled"), h + 1)
                dve.wait_ge(once("first_step_ready"), 1)
                dve.tensor_tensor(by_t(q_r1, h)[:, :, 1:T], by_t(G_CS, h)[:, :, 1:T], by_t(STATE, h)[:, :, 0:T - 1],
                                  ALU.mult).then_inc(once("yhat_ready"), 1)

            for h in range(2):
                t = cols(h)
                dve.wait_ge(once("scale_ready"), h + 1)
                dve.reciprocal(G_INV[:, t], G_L[:, t]).then_inc(once("inv_ready"), 1)
                if h == 1:
                    outputs(0)
                dve.wait_ge(once("inv_ready"), h + 1)
                dve.tensor_tensor(G_A[:, t], G_A[:, t], G_INV[:, t], ALU.mult).then_inc(once("a_scaled"), 1)
                dve.wait_ge(once("u_ready"), h + 1)
                dve.tensor_tensor(U_S[:, t], U_S[:, t], G_INV[:, t], ALU.mult).then_inc(once("u_scaled"), 1)
                dve.wait_ge(once("a_scaled"), h + 1)
                dve.wait_ge(once("u_scaled"), h + 1)
                for b in halves[h]:
                    t = slice(T * b, T * b + T)
                    dve.tensor_tensor_scan(STATE[:, t], G_A[:, t], U_S[:, t], 0.0, ALU.mult, ALU.add
                                           ).then_inc(once("state_ready"), 1)
            outputs(1)
            layernorm_halves("ln3", lambda h: dve.scalar_tensor_tensor(
                by_half(x_sb, h), bank(h, Y)[:, 0:HALF], norm_inv[:, 1:2], by_half(x_sb, h), ALU.mult, ALU.add), "y_done")
            for b in range(B):
                dve.tensor_tensor(x_bo[:, b, :], x_sb[:, b, :], b2_rows[:, :], ALU.add).then_inc(once("x_b2_ready"), 1)
            dve.wait_ge(once("x_b2_ready"), B)
            dve.wait_ge(once("ln3_turned"), 2)
            each("out_ready", lambda h, t: dve.tensor_tensor(by_half(xn, h), bank(h, OUT)[:, 0:HALF],
                                                             by_half(x_bo, h), ALU.add), "mlp_done")


_INS = ['x', 'ctx_1024', 'mask_1x1xSxS2_ff0', 'L0_xattn_Wq', 'L0_xattn_bq', 'L0_xattn_Wk', 'L0_xattn_bk',
        'L0_xattn_Wv', 'L0_xattn_bv', 'L0_xattn_Wo', 'L0_xattn_bo', 'L0_attn_W_in', 'L0_attn_W_out', 'L0_attn_Wp',
        'L0_attn_bp', 'L0_attn_alpha_log', 'L0_attn_delta_bias', 'L0_attn_log_gamma', 'L0_ffn_w1', 'L0_ffn_b1',
        'L0_ffn_w2', 'L0_ffn_b2']


def kernel(**inputs):
    import numpy as _np
    import concourse.bacc as _bacc
    from concourse import mybir as _mybir
    from concourse.bass_utils import run_bass_kernel_spmd as _run

    gather = _np.zeros((P, 2 * HEAD_COLS), _np.float32)
    for tile in range(4):
        for m in range(HEAD_COLS):
            gather[32 * tile + m, HEAD_COLS * (tile % 2) + m] = 1.0
    head_rows = (_np.arange(P)[:, None] // 8 % 2 == _np.arange(2)[None, :]).astype(_np.float32)
    consts = {"ident": _np.eye(P, dtype=_np.float32), "gather": gather, "head_rows": head_rows}

    nc = _bacc.Bacc("TRN2", target_bir_lowering=False, num_devices=1)
    arrays, args = {}, []
    for name in _INS + list(consts):
        a = _np.ascontiguousarray(consts[name] if name in consts else inputs[name])
        if a.ndim == 0:
            a = a.reshape(1)
        arrays[f"in_{name}_dram"] = a
        args.append(nc.dram_tensor(f"in_{name}_dram", a.shape, _mybir.dt.from_np(a.dtype),
                                   kind="ExternalInput").ap())
    args.append(nc.dram_tensor("out_0_dram", (4, 128, 128), _mybir.dt.float32, kind="ExternalOutput").ap())
    perceiver_block(nc, *args)
    r = _run(nc, [arrays], core_ids=[0])
    return r.results[0]["out_0_dram"]
```
